# Optimizing a Trainium2 kernel written in Bass

```python
import numpy as np
import jax
import jax.numpy as jnp

def _softmax(x, axis=-1):
    return jax.nn.softmax(x, axis=axis)

def _gelu(x):
    return jax.nn.gelu(x, approximate=True)

def _silu(x):
    return jax.nn.silu(x)

def _sigmoid(x):
    return jax.nn.sigmoid(x)

def _layernorm(x, axis=-1, eps=1e-05):
    m = jnp.mean(x, axis=axis, keepdims=True)
    v = jnp.var(x, axis=axis, keepdims=True)
    return (x - m) / jnp.sqrt(v + eps)

def _scatter_add(tgt, idx, src, axis=0):
    return tgt.at[idx].add(src)

def _segment_sum(src, seg, n):
    return jax.ops.segment_sum(src, seg, n)
kernel_name = 'mk_xattn_ffn_d2_seqx_r8_a6fca3'

def setup_inputs(seed: int=0):
    np.random.seed(seed)
    _w = jnp.asarray

    def _rec_inputs():
        import jax
        import jax.numpy as jnp
        _rk = jax.random.key(seed)
        x = 7.22e-05 + 1 * jax.random.normal(jax.random.fold_in(_rk, 1), (8, 256, 128), jnp.float32)
        _lenS = 256 - jax.random.randint(jax.random.fold_in(_rk, 7), (8,), 0, max(1, 256 // 4) + 1, jnp.int32)
        _lenS2 = 256 - jax.random.randint(jax.random.fold_in(_rk, 8), (8,), 0, max(1, 256 // 4) + 1, jnp.int32)
        _ctx_1024P = jax.random.normal(jax.random.fold_in(_rk, 11), (8, 16, 128), jnp.float32)
        _ctx_1024c = jax.random.dirichlet(jax.random.fold_in(_rk, 511), 0.3 * jnp.ones((16,), jnp.float32), (8, 256))
        _ctx_1024t = jnp.einsum('bsk,bkd->bsd', _ctx_1024c, _ctx_1024P)
        _ctx_1024t = _ctx_1024t * jax.lax.rsqrt(jnp.mean(jnp.square(_ctx_1024t)) + 1e-12) * 0.953939
        ctx_1024 = 4.13588e-05 + 0.999923 * (_ctx_1024t + 0.3 * jax.random.normal(jax.random.fold_in(_rk, 611), (8, 256, 128), jnp.float32))
        return (x, ctx_1024)
    x, ctx_1024 = _rec_inputs()

    def _L0_xattn_setup():
        import jax, jax.numpy as jnp
        import numpy as np
        import math
        D_MODEL = 128
        NHEAD = 16
        HEAD_DIM = D_MODEL // NHEAD
        ROPE_BASE = 10000.0

        def _rope_cos_sin(seq_len, dtype):
            inv_freq = 1.0 / ROPE_BASE ** (jnp.arange(0, HEAD_DIM, 2, dtype=jnp.float32) / HEAD_DIM)
            t = jnp.arange(seq_len, dtype=jnp.float32)
            freqs = jnp.einsum('i,j->ij', t, inv_freq)
            emb = jnp.concatenate([freqs, freqs], axis=-1)
            return (jnp.cos(emb).astype(dtype), jnp.sin(emb).astype(dtype))

        def _rotate_half(x):
            x1, x2 = jnp.split(x, 2, axis=-1)
            return jnp.concatenate([-x2, x1], axis=-1)
        key = jax.random.key(seed)
        ks = jax.random.split(key, 11)
        B, S = (4, 256)
        s = 1.0 / math.sqrt(D_MODEL)
        return {'query': jax.random.normal(ks[0], (B, S, D_MODEL), jnp.float32), 'key': jax.random.normal(ks[1], (B, S, D_MODEL), jnp.float32), 'value': jax.random.normal(ks[2], (B, S, D_MODEL), jnp.float32), 'Wq': jax.random.normal(ks[3], (D_MODEL, D_MODEL), jnp.float32) * s, 'bq': jnp.zeros((D_MODEL,), jnp.float32), 'Wk': jax.random.normal(ks[4], (D_MODEL, D_MODEL), jnp.float32) * s, 'bk': jnp.zeros((D_MODEL,), jnp.float32), 'Wv': jax.random.normal(ks[5], (D_MODEL, D_MODEL), jnp.float32) * s, 'bv': jnp.zeros((D_MODEL,), jnp.float32), 'Wo': jax.random.normal(ks[6], (D_MODEL, D_MODEL), jnp.float32) * s, 'bo': jnp.zeros((D_MODEL,), jnp.float32)}
    _L0_xattn_all = _L0_xattn_setup()
    _L0_xattn_in = {k: v for k, v in _L0_xattn_all.items() if k in ('Wq', 'bq', 'Wk', 'bk', 'Wv', 'bv', 'Wo', 'bo')}
    del _L0_xattn_all

    def _L0_ffn_setup():
        import jax, jax.numpy as jnp
        import numpy as np
        QP = 127.0
        MIN_RANGE = 1e-06

        def _ste_round(x):
            return x + jax.lax.stop_gradient(jnp.round(x) - x)

        def _quant_per_tensor(x):
            scale = jnp.maximum(jnp.max(jnp.abs(x)), MIN_RANGE) / QP
            return (_ste_round(x / scale), scale)

        def _qlinear(x2d, w, b):
            xq, sx = _quant_per_tensor(x2d)
            wq, sw = _quant_per_tensor(w)
            out = jnp.matmul(xq, wq.T) + b[None, :]
            return out * (sw * sx)
        key = jax.random.key(seed)
        k = jax.random.split(key, 5)
        B, N, D, H = (8, 128, 128, 512)
        return {'x': jax.random.normal(k[0], (B, N, D), dtype=jnp.float32), 'w1': jax.random.normal(k[1], (H, D), dtype=jnp.float32) * 0.02, 'b1': jax.random.normal(k[2], (H,), dtype=jnp.float32) * 0.02, 'w2': jax.random.normal(k[3], (D, H), dtype=jnp.float32) * 0.02, 'b2': jax.random.normal(k[4], (D,), dtype=jnp.float32) * 0.02}
    _L0_ffn_all = _L0_ffn_setup()
    _L0_ffn_in = {k: v for k, v in _L0_ffn_all.items() if k in ('w1', 'b1', 'w2', 'b2')}
    del _L0_ffn_all

    def _L1_xattn_setup():
        import jax, jax.numpy as jnp
        import numpy as np
        D_MODEL = 128
        NUM_HEADS = 16
        DEPTH = D_MODEL // NUM_HEADS

        def _split_heads(x, B):
            S = x.shape[1]
            return x.reshape(B, S, NUM_HEADS, DEPTH).transpose(0, 2, 1, 3)
        key = jax.random.key(seed)
        ks = jax.random.split(key, 11)
        B, S = (4, 256)
        scale = 1.0 / np.sqrt(D_MODEL)
        inp = {'v': jax.random.normal(ks[0], (B, S, D_MODEL), jnp.float32), 'k': jax.random.normal(ks[1], (B, S, D_MODEL), jnp.float32), 'q': jax.random.normal(ks[2], (B, S, D_MODEL), jnp.float32), 'wq': jax.random.normal(ks[3], (D_MODEL, D_MODEL), jnp.float32) * scale, 'bq': jnp.zeros((D_MODEL,), jnp.float32), 'wk': jax.random.normal(ks[4], (D_MODEL, D_MODEL), jnp.float32) * scale, 'bk': jnp.zeros((D_MODEL,), jnp.float32), 'wv': jax.random.normal(ks[5], (D_MODEL, D_MODEL), jnp.float32) * scale, 'bv': jnp.zeros((D_MODEL,), jnp.float32), 'wo': jax.random.normal(ks[6], (D_MODEL, D_MODEL), jnp.float32) * scale, 'bo': jnp.zeros((D_MODEL,), jnp.float32)}
        return inp
    _L1_xattn_all = _L1_xattn_setup()
    _L1_xattn_in = {k: v for k, v in _L1_xattn_all.items() if k in ('wq', 'bq', 'wk', 'bk', 'wv', 'bv', 'wo', 'bo')}
    del _L1_xattn_all

    def _L1_ffn_setup():
        import jax, jax.numpy as jnp
        import numpy as np
        TOP_K = 2

        def _ffn(x, gw, uw, dw):
            return jax.nn.silu(x @ gw.T) * (x @ uw.T) @ dw.T
        key = jax.random.key(seed)
        ks = jax.random.split(key, 8)
        w = lambda k, shape: jax.random.normal(k, shape, jnp.float32) * 0.02
        return dict(x=jax.random.normal(ks[0], (4, 256, 128), jnp.float32), gate_w=w(ks[1], (8, 128)), expert_gate=w(ks[2], (8, 352, 128)), expert_up=w(ks[3], (8, 352, 128)), expert_down=w(ks[4], (8, 128, 352)), shared_gate=w(ks[5], (352, 128)), shared_up=w(ks[6], (352, 128)), shared_down=w(ks[7], (128, 352)))
    _L1_ffn_all = _L1_ffn_setup()
    _L1_ffn_in = {k: v for k, v in _L1_ffn_all.items() if k in ('gate_w', 'expert_gate', 'expert_up', 'expert_down', 'shared_gate', 'shared_up', 'shared_down')}
    del _L1_ffn_all
    return {'x': x, 'ctx_1024': ctx_1024, 'L0_xattn_Wq': _L0_xattn_in['Wq'], 'L0_xattn_bq': _L0_xattn_in['bq'], 'L0_xattn_Wk': _L0_xattn_in['Wk'], 'L0_xattn_bk': _L0_xattn_in['bk'], 'L0_xattn_Wv': _L0_xattn_in['Wv'], 'L0_xattn_bv': _L0_xattn_in['bv'], 'L0_xattn_Wo': _L0_xattn_in['Wo'], 'L0_xattn_bo': _L0_xattn_in['bo'], 'L0_ffn_w1': _L0_ffn_in['w1'], 'L0_ffn_b1': _L0_ffn_in['b1'], 'L0_ffn_w2': _L0_ffn_in['w2'], 'L0_ffn_b2': _L0_ffn_in['b2'], 'L1_xattn_wq': _L1_xattn_in['wq'], 'L1_xattn_bq': _L1_xattn_in['bq'], 'L1_xattn_wk': _L1_xattn_in['wk'], 'L1_xattn_bk': _L1_xattn_in['bk'], 'L1_xattn_wv': _L1_xattn_in['wv'], 'L1_xattn_bv': _L1_xattn_in['bv'], 'L1_xattn_wo': _L1_xattn_in['wo'], 'L1_xattn_bo': _L1_xattn_in['bo'], 'L1_ffn_gate_w': _L1_ffn_in['gate_w'], 'L1_ffn_expert_gate': _L1_ffn_in['expert_gate'], 'L1_ffn_expert_up': _L1_ffn_in['expert_up'], 'L1_ffn_expert_down': _L1_ffn_in['expert_down'], 'L1_ffn_shared_gate': _L1_ffn_in['shared_gate'], 'L1_ffn_shared_up': _L1_ffn_in['shared_up'], 'L1_ffn_shared_down': _L1_ffn_in['shared_down']}

def reference(x, ctx_1024, L0_xattn_Wq, L0_xattn_bq, L0_xattn_Wk, L0_xattn_bk, L0_xattn_Wv, L0_xattn_bv, L0_xattn_Wo, L0_xattn_bo, L0_ffn_w1, L0_ffn_b1, L0_ffn_w2, L0_ffn_b2, L1_xattn_wq, L1_xattn_bq, L1_xattn_wk, L1_xattn_bk, L1_xattn_wv, L1_xattn_bv, L1_xattn_wo, L1_xattn_bo, L1_ffn_gate_w, L1_ffn_expert_gate, L1_ffn_expert_up, L1_ffn_expert_down, L1_ffn_shared_gate, L1_ffn_shared_up, L1_ffn_shared_down):
    import jax
    import jax.numpy as jnp

    def _L0_xattn_ref(query, key, value, Wq, bq, Wk, bk, Wv, bv, Wo, bo):
        import jax, jax.numpy as jnp
        import numpy as np
        import math
        D_MODEL = 128
        NHEAD = 16
        HEAD_DIM = D_MODEL // NHEAD
        ROPE_BASE = 10000.0

        def _rope_cos_sin(seq_len, dtype):
            inv_freq = 1.0 / ROPE_BASE ** (jnp.arange(0, HEAD_DIM, 2, dtype=jnp.float32) / HEAD_DIM)
            t = jnp.arange(seq_len, dtype=jnp.float32)
            freqs = jnp.einsum('i,j->ij', t, inv_freq)
            emb = jnp.concatenate([freqs, freqs], axis=-1)
            return (jnp.cos(emb).astype(dtype), jnp.sin(emb).astype(dtype))

        def _rotate_half(x):
            x1, x2 = jnp.split(x, 2, axis=-1)
            return jnp.concatenate([-x2, x1], axis=-1)
        B, Sq, _ = query.shape
        Sk = key.shape[1]
        q = (query @ Wq.T + bq).reshape(B, Sq, NHEAD, HEAD_DIM)
        k = (key @ Wk.T + bk).reshape(B, Sk, NHEAD, HEAD_DIM)
        v = (value @ Wv.T + bv).reshape(B, Sk, NHEAD, HEAD_DIM)
        cos, sin = _rope_cos_sin(Sq, q.dtype)
        cos = cos[None, :, None, :]
        sin = sin[None, :, None, :]
        q = q * cos + _rotate_half(q) * sin
        k = k * cos + _rotate_half(k) * sin
        scale = 1.0 / math.sqrt(HEAD_DIM)
        scores = jnp.einsum('bqhd,bkhd->bhqk', q * scale, k)
        attn = jax.nn.softmax(scores, axis=-1)
        out = jnp.einsum('bhqk,bkhd->bqhd', attn, v).reshape(B, Sq, D_MODEL)
        return out @ Wo.T + bo

    def _L0_ffn_ref(x, w1, b1, w2, b2):
        import jax, jax.numpy as jnp
        import numpy as np
        QP = 127.0
        MIN_RANGE = 1e-06

        def _ste_round(x):
            return x + jax.lax.stop_gradient(jnp.round(x) - x)

        def _quant_per_tensor(x):
            scale = jnp.maximum(jnp.max(jnp.abs(x)), MIN_RANGE) / QP
            return (_ste_round(x / scale), scale)

        def _qlinear(x2d, w, b):
            xq, sx = _quant_per_tensor(x2d)
            wq, sw = _quant_per_tensor(w)
            out = jnp.matmul(xq, wq.T) + b[None, :]
            return out * (sw * sx)
        B, N, D = x.shape
        h = _qlinear(x.reshape(-1, D), w1, b1)
        h = jax.nn.gelu(h, approximate=False)
        o = _qlinear(h, w2, b2)
        return o.reshape(B, N, -1)

    def _L1_xattn_ref(v, k, q, wq, bq, wk, bk, wv, bv, wo, bo):
        import jax, jax.numpy as jnp
        import numpy as np
        D_MODEL = 128
        NUM_HEADS = 16
        DEPTH = D_MODEL // NUM_HEADS

        def _split_heads(x, B):
            S = x.shape[1]
            return x.reshape(B, S, NUM_HEADS, DEPTH).transpose(0, 2, 1, 3)
        B, S, _ = q.shape
        qh = _split_heads(q @ wq + bq, B)
        kh = _split_heads(k @ wk + bk, B)
        vh = _split_heads(v @ wv + bv, B)
        logits = jnp.einsum('bhqd,bhkd->bhqk', qh, kh) / jnp.sqrt(jnp.float32(DEPTH))
        weights = jax.nn.softmax(logits, axis=-1)
        attn = jnp.einsum('bhqk,bhkd->bhqd', weights, vh)
        concat = attn.transpose(0, 2, 1, 3).reshape(B, S, D_MODEL)
        return concat @ wo + bo

    def _L1_ffn_ref(x, gate_w, expert_gate, expert_up, expert_down, shared_gate, shared_up, shared_down):
        import jax, jax.numpy as jnp
        import numpy as np
        TOP_K = 2

        def _ffn(x, gw, uw, dw):
            return jax.nn.silu(x @ gw.T) * (x @ uw.T) @ dw.T
        B, S, H = x.shape
        xf = x.reshape(-1, H)
        T = xf.shape[0]
        E = expert_gate.shape[0]
        shared = _ffn(xf, shared_gate, shared_up, shared_down)
        logits = xf @ gate_w.T
        probs = jax.nn.softmax(logits, axis=-1)
        topw, topi = jax.lax.top_k(probs, TOP_K)
        topw = topw / (topw.sum(-1, keepdims=True) + 1e-20)
        comb = jnp.zeros((T, E), xf.dtype).at[jnp.arange(T)[:, None], topi].add(topw)

        def body(acc, ws):
            gw, uw, dw, wcol = ws
            return (acc + _ffn(xf, gw, uw, dw) * wcol[:, None], None)
        routed, _ = jax.lax.scan(body, jnp.zeros_like(xf), (expert_gate, expert_up, expert_down, comb.T))
        return (shared + routed).reshape(B, S, H)
    x = x + _L0_xattn_ref(_layernorm(x, axis=-1), ctx_1024, ctx_1024, L0_xattn_Wq, L0_xattn_bq, L0_xattn_Wk, L0_xattn_bk, L0_xattn_Wv, L0_xattn_bv, L0_xattn_Wo, L0_xattn_bo)
    x = x + _L0_ffn_ref(_layernorm(x, axis=-1), L0_ffn_w1, L0_ffn_b1, L0_ffn_w2, L0_ffn_b2)
    x = x + _L1_xattn_ref(ctx_1024, ctx_1024, _layernorm(x, axis=-1), L1_xattn_wq, L1_xattn_bq, L1_xattn_wk, L1_xattn_bk, L1_xattn_wv, L1_xattn_bv, L1_xattn_wo, L1_xattn_bo)
    x = x + _L1_ffn_ref(_layernorm(x, axis=-1), L1_ffn_gate_w, L1_ffn_expert_gate, L1_ffn_expert_up, L1_ffn_expert_down, L1_ffn_shared_gate, L1_ffn_shared_up, L1_ffn_shared_down)
    return x

_drawn_inputs = setup_inputs


def setup_inputs(seed=0):
    import zlib

    import numpy as np

    out = dict(_drawn_inputs(seed))
    spreads = {'L0_xattn_bq': (0.0, 0.474),
     'L0_xattn_bk': (0.0, 0.8),
     'L0_xattn_bv': (0.0, 0.1),
     'L0_xattn_bo': (0.0, 0.1),
     'L1_xattn_bq': (0.0, 0.461),
     'L1_xattn_bk': (0.0, 0.8),
     'L1_xattn_bv': (0.0, 0.1),
     'L1_xattn_bo': (0.0, 0.1)}
    factors = {'L0_ffn_b1': 8.0,
     'L0_ffn_b2': 8.0,
     'L1_ffn_gate_w': 8.0,
     'L1_ffn_expert_gate': 8.0,
     'L1_ffn_expert_up': 8.0,
     'L1_ffn_expert_down': 8.0,
     'L1_ffn_shared_gate': 7.174,
     'L1_ffn_shared_up': 7.156,
     'L1_ffn_shared_down': 7.117}
    for name, (base, spread) in spreads.items():
        noise = np.random.default_rng([zlib.crc32(name.encode()), seed]).standard_normal(out[name].shape)
        drawn = base * np.exp(spread * noise) if base else spread * noise
        out[name] = jnp.asarray(drawn.astype(out[name].dtype))
    for name, factor in factors.items():
        out[name] = (out[name] * factor).astype(out[name].dtype)
    return out
```

```python
from contextlib import ExitStack

import numpy as np

import concourse.bass as bass
from concourse import mybir

F32 = mybir.dt.float32
F16 = mybir.dt.float16
BF16 = mybir.dt.bfloat16
U32 = mybir.dt.uint32
ALU = mybir.AluOpType
ACT = mybir.ActivationFunctionType
AX = mybir.AxisListType

P = 128
NB = 8
S = 256
D = 128
H = 16
HD = D // H
G = H // 2
NT = NB * S
TILES = NT // P
FF = 512
FT = FF // P
E = 8
NE = E + 1
FE = 352
FTE = [(0, 128), (128, 128), (256, 96)]
QP = 127.0
MIN_RANGE = 1e-6
LN_EPS = 1e-5
SM_SCALE = float(HD) ** -0.5
MAXROW = 64.0
ROUND = 12582912.0

T_K = -50
T_V = -45
T_X = -42
T_Q = -40
T_S = -24
T_MX = -6
T_AV = 5
T_O1 = 20
T_O2 = 24
T_OUT = 28
T_XT = 33
T_FIRST, T_LAST = T_K, 16 * (NB - 1) + T_XT + 1


def issued(offset, t, per=1):
    return per * min(NB, max(0, -((offset - t) // 16)))


def due(offset, t):
    m, r = divmod(t - offset, 16)
    return m if r == 0 and 0 <= m < NB else None


def head_of(k):
    half, j, c = k // 8, (k // 4) % 2, k % 4
    g = 4 * half + c
    return half, j, c, g, 2 * g + j


def layers(nc, io, out):
    ctx = ExitStack()
    with ctx:
        def sb(name, shape, dt=F32):
            return ctx.enter_context(nc.sbuf_tensor(name, shape, dt))

        def sem(name):
            return ctx.enter_context(nc.semaphore(name))

        ps = ctx.enter_context(nc.psum_tensor("ps", [P, 8, 512], F32))
        ps_st = [0, 1, 2]
        ps_s = [3, 4]
        AVB, BA, BB = 5, 6, 7

        x = sb("x", [P, TILES, D])
        xb = sb("xb", [P, 2, 2, D])
        xn = sb("xn", [P, 2, 2, D])
        xp = sb("xp", [P, 2, 2, D])
        xT = sb("xT", [P, NT])
        pre_T = sb("pre_T", [P, 2, S])
        ctxT = sb("ctxT", [P, 2, S])
        ident = sb("ident", [P, P])
        cos = sb("cos", [P, S])
        sin = sb("sin", [P, S])
        w_at = sb("w_at", [P, 2, 4, D])
        w_sw = sb("w_sw", [P, 2, D])
        b_at = sb("b_at", [P, 2, 2])
        b_sw = sb("b_sw", [P, 2])
        bv = sb("bv", [P, 2, D])
        bo = sb("bo", [P, 2, D])
        kf = sb("kf", [P, 2, S])
        rot = sb("rot", [P, 2, S])
        khi = sb("khi", [P, 2, S], F16)
        klo = sb("klo", [P, 2, S], F16)
        qf = sb("qf", [P, 2, S])
        rotq = sb("rotq", [P, 2, S])
        qhi = sb("qhi", [P, 2, S], F16)
        qlo = sb("qlo", [P, 2, S], F16)
        QS = sb("QS", [P, 4, G, S], F16)
        KP = sb("KP", [P, 4, G, 2, S], F16)
        VA = sb("VA", [P, 4, 2, G * 80])
        mx = sb("mx", [P, 2, 2, H])
        negm = sb("negm", [H, 2, S], F16)
        Pt = sb("Pt", [P, 2, 4, 512])
        raw = sb("raw", [P, 512])
        rsum = sb("rsum", [P, 4 * 4 * 2])
        on = sb("on", [P, 2, D])
        onT = sb("onT", [P, S])
        st6 = sb("st6", [P, 2, 2, 6])
        mv = sb("mv", [P, 2, 2, 2])
        sd = sb("sd", [P, 2, 2])
        rs = sb("rs", [P, 2, 2])
        st6p = sb("st6p", [P, 2, 2, 6])
        mvp = sb("mvp", [P, 2, 2, 2])
        sdp = sb("sdp", [P, 2, 2])
        rsp = sb("rsp", [P, 2, 2])
        neghalf = sb("neghalf", [P, 2])
        ones = sb("ones", [P, P])
        amax = sb("amax", [P, 16])
        g1 = sb("g1", [P, 8])
        w1q = sb("w1q", [P, FF], BF16)
        w2q = sb("w2q", [P, FT, D], BF16)
        b1 = sb("b1", [P, FT])
        b1s = sb("b1s", [P, FT])
        b2 = sb("b2", [P, D])
        sc = sb("sc", [P, 16])
        xq = sb("xq", [P, NT], BF16)
        hb = sb("hb", [P, FT, NT])
        hq = Pt[:, 0, :, :].rearrange("p a b -> p (a b)").bitcast(BF16).rearrange("p (f c t) -> p f c t", f=FT, c=2)
        w12 = hb[:, 0, 0:2 * FF]
        wst = sb("wst", [P, 2, 2 * FE])
        whi = sb("whi", [P, NE, 2 * FE], F16)
        wlo = sb("wlo", [P, NE, 2 * FE], F16)
        wd = hb[:, 1:3, :].rearrange("p a b -> p (a b)")[:, 0:NE * 3 * D].rearrange("p (e f d) -> p e f d", e=NE, f=3)
        gw = sb("gw", [P, E])
        xhi = hb[:, 0, 0:NT // 2].bitcast(F16)
        xlo = hb[:, 0, NT // 2:NT].bitcast(F16)
        rt_sb = hb[:, 3, :]
        lg, pr, t8, i8, oh0, oh1, comb = (rt_sb[:, P * i:P * i + P].rearrange("p (t e) -> p t e", e=E) for i in range(7))
        i8 = i8.bitcast(U32)
        oh = rt_sb[:, 4 * P:6 * P].rearrange("p (a t e) -> p a t e", a=2, e=E)
        i8f = rt_sb[:, 7 * P:7 * P + 2 * TILES].rearrange("p (t a) -> p t a", a=2)
        r1 = rt_sb[:, 8 * P:8 * P + TILES]
        r2 = rt_sb[:, 8 * P + TILES:8 * P + 2 * TILES]
        iota = sb("iota", [P, TILES, E])
        sg = Pt[:, :, :, :].rearrange("p a b c -> p (a b c)")[:, 3072:4096].rearrange("p (q t) -> p q t", q=2)
        hh = Pt[:, :, :, :].rearrange("p a b c -> p (a b c)")[:, 0:3072].rearrange("p (q f t) -> p q f t", q=2, f=3)

        in_w = sem("in_w")
        in_x = sem("in_x")
        in_wd = sem("in_wd")
        in_kp = sem("in_kp")
        in_e = [sem("in_e0"), sem("in_e1")]
        in_ctx = [sem("in_ctx0"), sem("in_ctx1")]
        memset_done = sem("memset_done")
        zero_done = sem("zero_done")
        xb_done = sem("xb_done")
        pre_st = sem("pre_st"); pre_mv = sem("pre_mv"); pre_sd = sem("pre_sd"); pre_rs = sem("pre_rs"); pre_n = sem("pre_n")
        post_st = sem("post_st"); post_mv = sem("post_mv"); post_sd = sem("post_sd"); post_rs = sem("post_rs"); post_n = sem("post_n")
        k_mm = sem("k_mm"); v_mm = sem("v_mm"); xt_mm = sem("xt_mm"); q_mm = sem("q_mm")
        k_ev = sem("k_ev"); v_ev = sem("v_ev"); xt_ev = sem("xt_ev"); q_ev = sem("q_ev")
        k_rot = sem("k_rot"); q_rot = sem("q_rot")
        k_hi = sem("k_hi"); q_hi = sem("q_hi"); k_lo = sem("k_lo"); q_lo = sem("q_lo")
        kp_in = [sem(f"kp_in{i}") for i in range(4)]
        qs_in = [sem(f"qs_in{i}") for i in range(4)]
        m_in = [sem(f"m_in{i}") for i in range(4)]
        s_mm = sem("s_mm"); s_max = sem("s_max"); mx_t = sem("mx_t"); negm_ev = sem("negm_ev")
        st_mm = sem("st_mm"); exp_done = sem("exp_done"); av_mm = sem("av_mm"); raw_ev = sem("raw_ev")
        o1_t = sem("o1_t"); rsum_done = sem("rsum_done"); on_done = sem("on_done")
        o2_t = sem("o2_t"); onT_ev = sem("onT_ev"); out_mm = sem("out_mm"); x_new = sem("x_new")
        post_t = sem("post_t"); post_ev = sem("post_ev"); amax_done = sem("amax_done")
        gm_a = sem("gm_a"); gm_t = sem("gm_t"); gm_b = sem("gm_b"); gm_bc = sem("gm_bc"); gm_s = sem("gm_s")
        w_abs = sem("w_abs"); w_q1 = sem("w_q1"); w_q2 = sem("w_q2")
        f_sc = sem("f_sc"); xq_a = sem("xq_a"); xq_b = sem("xq_b"); f1_mm = sem("f1_mm"); gelu = sem("gelu"); habs = sem("habs")
        hq_a = sem("hq_a"); hq_b = sem("hq_b"); f2_mm = sem("f2_mm"); f2_ev = sem("f2_ev"); ffn_out = sem("ffn_out")
        e_hi = sem("e_hi"); e_lo = sem("e_lo")
        x2hi = sem("x2hi"); x2lo = sem("x2lo"); r_mm = sem("r_mm")
        rt = sem("rt")
        g_mm = sem("g_mm"); u_mm = sem("u_mm"); silu = sem("silu"); h_done = sem("h_done"); d_mm = sem("d_mm"); acc = sem("acc")
        stored = sem("stored")

        NW = 0
        block = ctx.enter_context(nc.Block())

        x_dram = io["x"].rearrange("b (a p) d -> p (b a) d", p=P)
        out_dram = out.rearrange("b (a p) d -> p (b a) d", p=P)

        weights = [
            (ident[:, :], io["c_ident"]), (cos[:, :], io["c_cos"]), (sin[:, :], io["c_sin"]),
            (w_at[:, :, :, :], io["w_at"]), (w_sw[:, :, :], io["w_sw"]),
            (b_at[:, :, :], io["b_at"]), (b_sw[:, :], io["b_sw"]),
            (bv[:, :, :], io["bv"].partition_broadcast(P)), (bo[:, :, :], io["bo"].partition_broadcast(P)),
            (w12, io["w12"]), (b1[:, :], io["b1"]), (b2[:, :], io["b2"].partition_broadcast(P)),
            (gw[:, :], io["gw"]),
            (iota[:, :, :], io["c_iota"].partition_broadcast(P)),
        ]
        ALL_W = 16 * len(weights)

        @block.sync
        def _(sp):
            for b in range(NB):
                if b < 2:
                    sp.dma_start(ctxT[:, b, :], io["ctxT"][b]).then_inc(in_ctx[b], 16)
            for dst, src in weights:
                sp.dma_start(dst, src).then_inc(in_w, 16)
            sp.dma_start(x[:, :, :], x_dram).then_inc(in_x, 16)
            for e in range(2):
                sp.dma_start(wst[:, e, :], io["wgu"][e]).then_inc(in_e[e], 16)
            sp.wait_ge(zero_done, 2)
            for i in range(4):
                sp.dma_start(KP[96:98, i], io["c_kp"]).then_inc(in_kp, 16)
            for L in range(2):
                if L == 1:
                    sp.wait_ge(hq_b, 16)
                    sp.dma_start(wd, io["wd"]).then_inc(in_wd, 16)
                for t in range(T_FIRST, T_LAST + 1):
                    m = due(T_K + 8, t)
                    if m is not None:
                        n = NB * L + m
                        if n + 2 < 2 * NB:
                            sp.wait_ge(k_mm, n + 1)
                            sp.wait_ge(v_mm, n + 1)
                            sp.dma_start(ctxT[:, n % 2, :], io["ctxT"][(n + 2) % NB]).then_inc(in_ctx[n % 2], 16)
                        if n >= 4:
                            sp.wait_ge(st_mm, H * (n - 3))
                        sp.wait_ge(k_hi, n + 1)
                        for r in range(2):
                            for j in range(2):
                                sp.dma_start(KP[16 * r + 8 * j:16 * r + 8 * j + 8, n % 4, :, j, :],
                                             khi[64 * j:64 * j + 64, n % 2, :]).then_inc(kp_in[n % 4], 16)
                    m = due(T_K + 14, t)
                    if m is not None:
                        n = NB * L + m
                        sp.wait_ge(k_lo, n + 1)
                        for r in range(2, 4):
                            for j in range(2):
                                sp.dma_start(KP[16 * r + 8 * j:16 * r + 8 * j + 8, n % 4, :, j, :],
                                             klo[64 * j:64 * j + 64, n % 2, :]).then_inc(kp_in[n % 4], 16)
                    m = due(T_Q + 8, t)
                    if m is not None:
                        n = NB * L + m
                        if n >= 4:
                            sp.wait_ge(st_mm, H * (n - 3))
                        sp.wait_ge(q_hi, n + 1)
                        for r in (0, 2):
                            sp.dma_start(QS[16 * r:16 * r + 16, n % 4, :, :], qhi[:, n % 2, :]).then_inc(qs_in[n % 4], 16)
                        sp.wait_ge(q_lo, n + 1)
                        for r in (1, 3):
                            sp.dma_start(QS[16 * r:16 * r + 16, n % 4, :, :], qlo[:, n % 2, :]).then_inc(qs_in[n % 4], 16)
                    m = due(T_MX + 1, t)
                    if m is not None:
                        n = NB * L + m
                        sp.wait_ge(negm_ev, n + 1)
                        sp.dma_start(QS[96:98, n % 4, :, :], negm[:, n % 2, :]).then_inc(m_in[n % 4], 16)
                    m = due(T_O1 + 4, t)
                    if m is not None and NB * L + m + 2 < NE:
                        n = NB * L + m
                        sp.wait_ge(e_lo, n + 1)
                        sp.dma_start(wst[:, n % 2, :], io["wgu"][n + 2]).then_inc(in_e[n % 2], 16)
            for c in range(4):
                sp.wait_ge(acc, NE * 16 - 12 + 4 * c)
                sp.dma_start(out_dram[:, 4 * c:4 * c + 4, :], x[:, 4 * c:4 * c + 4, :]).then_inc(stored, 16)
            sp.wait_ge(stored, 64)

        @block.gpsimd
        def _(pool):
            nc.gpsimd.memset(neghalf[:, :], -0.5).then_inc(memset_done, 1)
            nc.gpsimd.memset(ones[:, :], 1.0).then_inc(memset_done, 1)
            nc.gpsimd.memset(VA[:, :, :, :], 0.0).then_inc(memset_done, 1)
            va5 = VA[:, :, :, :].rearrange("p b k (g w) -> p (b k) g w", g=G)
            pool.wait_ge(memset_done, 3)
            nc.gpsimd.memset(va5[:, :, :, 16:17], 1.0).then_inc(memset_done, 1)
            nc.gpsimd.memset(va5[:, :, :, 49:50], 1.0).then_inc(memset_done, 1)

            def split_expert(e):
                pool.wait_ge(e_hi, e + 1)
                nc.gpsimd.tensor_tensor(wlo[:, e, :], wst[:, e % 2, :], whi[:, e, :], ALU.subtract).then_inc(e_lo, 1)

            def pre_norm(n):
                pool.wait_ge(pre_mv, 2 * (n + 1))
                if n >= 2:
                    pool.wait_ge(pre_n, 2 * (n - 1))
                nc.gpsimd.tensor_scalar(sd[:, n % 2, :], mv[:, n % 2, :, 1], LN_EPS, None, ALU.add).then_inc(pre_sd, 1)
                pool.wait_ge(pre_sd, n + 1)
                nc.gpsimd.tensor_tensor(rs[:, n % 2, :], sd[:, n % 2, :], neghalf[:, :], ALU.pow).then_inc(pre_rs, 1)

            def post_norm(n):
                pool.wait_ge(post_mv, 2 * (n + 1))
                if n >= 2:
                    pool.wait_ge(post_n, 2 * (n - 1))
                nc.gpsimd.tensor_scalar(sdp[:, n % 2, :], mvp[:, n % 2, :, 1], LN_EPS, None, ALU.add).then_inc(post_sd, 1)
                pool.wait_ge(post_sd, n + 1)
                nc.gpsimd.tensor_tensor(rsp[:, n % 2, :], sdp[:, n % 2, :], neghalf[:, :], ALU.pow).then_inc(post_rs, 1)

            pool.wait_ge(in_w, ALL_W)
            pool.wait_ge(in_x, 16)
            for L in range(2):
                if L == 1:
                    pool.wait_ge(ffn_out, 4)
                for t in range(T_FIRST, T_LAST + 1):
                    m = due(T_K + 1, t)
                    if m is not None:
                        n = NB * L + m
                        pre_norm(n)
                    m = due(T_K + 2, t)
                    if m is not None and L == 0:
                        n = NB * L + m
                        pool.wait_ge(k_ev, n + 1)
                        nc.gpsimd.tensor_tensor(kf[:, n % 2, :], kf[:, n % 2, :], cos[:, :], ALU.mult).then_inc(k_rot, 1)
                        nc.gpsimd.tensor_tensor(rot[:, n % 2, :], rot[:, n % 2, :], sin[:, :], ALU.mult).then_inc(k_rot, 1)
                        pool.wait_ge(k_rot, 3 * n + 2)
                        nc.gpsimd.tensor_tensor(kf[:, n % 2, :], kf[:, n % 2, :], rot[:, n % 2, :], ALU.add).then_inc(k_rot, 1)
                    m = due(T_K + 7, t)
                    if m is not None:
                        n = NB * L + m
                        pool.wait_ge(k_hi, n + 1)
                        nc.gpsimd.tensor_tensor(klo[:, n % 2, :], kf[:, n % 2, :], khi[:, n % 2, :], ALU.subtract).then_inc(k_lo, 1)
                    m = due(T_Q + 2, t)
                    if m is not None and L == 0:
                        n = NB * L + m
                        pool.wait_ge(q_ev, n + 1)
                        nc.gpsimd.tensor_tensor(qf[:, n % 2, :], qf[:, n % 2, :], cos[:, :], ALU.mult).then_inc(q_rot, 1)
                        nc.gpsimd.tensor_tensor(rotq[:, n % 2, :], rotq[:, n % 2, :], sin[:, :], ALU.mult).then_inc(q_rot, 1)
                        pool.wait_ge(q_rot, 3 * n + 2)
                        nc.gpsimd.tensor_tensor(qf[:, n % 2, :], qf[:, n % 2, :], rotq[:, n % 2, :], ALU.add).then_inc(q_rot, 1)
                    m = due(T_Q + 7, t)
                    if m is not None:
                        n = NB * L + m
                        pool.wait_ge(q_hi, n + 1)
                        nc.gpsimd.tensor_tensor(qlo[:, n % 2, :], qf[:, n % 2, :], qhi[:, n % 2, :], ALU.subtract).then_inc(q_lo, 1)
                    m = due(T_O1, t)
                    if m is not None:
                        n = NB * L + m
                        if n >= 2:
                            pool.wait_ge(x_new, n - 1)
                        for a in range(2):
                            ins = nc.gpsimd.tensor_tensor(xb[:, n % 2, a, :], x[:, 2 * m + a, :], bo[:, L, :], ALU.add)
                        ins.then_inc(xb_done, 1)
                        if n < NE:
                            split_expert(n)
                    m = due(T_OUT + 2, t)
                    if m is not None:
                        post_norm(NB * L + m)
            pool.wait_ge(stored, 64)

        @block.tensor
        def _(pe):
            mm = nc.tensor.matmul

            def spread_max(i):
                pe.wait_ge(gm_a, i + 1)
                if i:
                    pe.wait_ge(gm_s, i)
                pe.transpose(ps[0:1, BA, 0:P], g1[:, i:i + 1], ident[:, :]).then_inc(gm_t, 1)
                pe.wait_ge(gm_b, i + 1)
                mm(ps[:, BA, P:P + 1], ones[0:1, :], g1[0:1, 4 + i:5 + i], start=True, stop=True).then_inc(gm_bc, 1)

            pe.wait_ge(in_w, ALL_W)
            pe.wait_ge(memset_done, 5)
            spread_max(0)
            spread_max(1)
            pe.wait_ge(gm_s, 2)

            for L in range(2):
                for t in range(T_FIRST, T_LAST + 1):
                    m = due(T_K, t)
                    if m is not None:
                        n = NB * L + m
                        pe.wait_ge(in_ctx[n % 2], 16 * (n // 2 + 1))
                        if n:
                            pe.wait_ge(q_ev, n)
                        if (c := NB * L + issued(T_O1, t)):
                            pe.wait_ge(on_done, c)
                        ins = mm(ps[:, BA, 0:S], w_at[:, L, 1, :], ctxT[:, n % 2, :], start=True, stop=True)
                        if L == 0:
                            ins = mm(ps[:, BA, S:2 * S], w_sw[:, 1, :], ctxT[:, n % 2, :], start=True, stop=True)
                        ins.then_inc(k_mm, 1)
                    m = due(T_V, t)
                    if m is not None:
                        n = NB * L + m
                        if n:
                            pe.wait_ge(xt_ev, n)
                        if (c := NB * L + issued(T_MX, t)):
                            pe.wait_ge(negm_ev, c)
                        if (c := NB * L + issued(T_OUT, t)):
                            pe.wait_ge(x_new, c)
                        if (c := NB * L + issued(T_XT, t)):
                            pe.wait_ge(post_ev, c)
                        if L and m == 0:
                            pe.wait_ge(ffn_out, 4)
                        for a in range(2):
                            ins = mm(ps[:, BB, P * a:P * a + P], ctxT[:, n % 2, P * a:P * a + P], w_at[:, L, 2, :],
                                     start=True, stop=True)
                        ins.then_inc(v_mm, 1)
                    m = due(T_X, t)
                    if m is not None:
                        n = NB * L + m
                        pe.wait_ge(pre_n, 2 * (n + 1))
                        pe.wait_ge(v_ev, n + 1)
                        if (c := NB * L + issued(T_O2, t)):
                            pe.wait_ge(onT_ev, c)
                        if (c := NB * L + issued(T_OUT, t)):
                            pe.wait_ge(x_new, c)
                        if (c := NB * L + issued(T_XT, t)):
                            pe.wait_ge(post_ev, c)
                        for a in range(2):
                            ins = pe.transpose(ps[:, BB, P * a:P * a + P], xn[:, n % 2, a, :], ident[:, :])
                        ins.then_inc(xt_mm, 1)
                    m = due(T_Q, t)
                    if m is not None:
                        n = NB * L + m
                        pe.wait_ge(xt_ev, n + 1)
                        pe.wait_ge(k_ev, n + 1)
                        if (c := NB * L + issued(T_O1, t)):
                            pe.wait_ge(on_done, c)
                        ins = mm(ps[:, BA, 0:S], w_at[:, L, 0, :], pre_T[:, n % 2, :], start=True, stop=True)
                        if L == 0:
                            ins = mm(ps[:, BA, S:2 * S], w_sw[:, 0, :], pre_T[:, n % 2, :], start=True, stop=True)
                        ins.then_inc(q_mm, 1)
                    m, k = divmod(t - T_S, 16)
                    if 0 <= m < NB:
                        n = NB * L + m
                        i = H * n + k
                        g, a = k // 2, k % 2
                        if k == 0:
                            if n == 0:
                                pe.wait_ge(in_kp, 64)
                            pe.wait_ge(kp_in[n % 4], 128 * (n // 4 + 1))
                            pe.wait_ge(qs_in[n % 4], 64 * (n // 4 + 1))
                        if i >= 2:
                            pe.wait_ge(s_max, i - 1)
                        mm(ps[:, ps_s[i % 2], :], QS[0:96, n % 4, g, P * a:P * a + P],
                           KP[0:96, n % 4, g, :, :].rearrange("p j k -> p (j k)"), start=True, stop=True).then_inc(s_mm, 1)
                    m = due(T_MX, t)
                    if m is not None:
                        n = NB * L + m
                        pe.wait_ge(s_max, H * (n + 1))
                        pe.wait_ge(xt_ev, NB * L + issued(T_X, t))
                        pe.wait_ge(v_ev, NB * L + issued(T_V, t))
                        if (c := NB * L + issued(T_OUT, t)):
                            pe.wait_ge(x_new, c)
                        if (c := NB * L + issued(T_O2, t)):
                            pe.wait_ge(onT_ev, c)
                        if (c := NB * L + issued(T_XT, t)):
                            pe.wait_ge(post_ev, c)
                        for a in range(2):
                            ins = pe.transpose(ps[0:H, BB, P * a:P * a + P], mx[:, n % 2, a, :], ident[:, :])
                        ins.then_inc(mx_t, 1)
                    m, k = divmod(t, 16)
                    if 0 <= m < NB:
                        n = NB * L + m
                        i = H * n + k
                        half, j, c4, g, h = head_of(k)
                        if k == 0:
                            pe.wait_ge(m_in[n % 4], 16 * (n // 4 + 1))
                        if i >= 3:
                            pe.wait_ge(exp_done, i - 2)
                        for a in range(2):
                            ins = mm(ps[:, ps_st[i % 3], S * a:S * a + S], KP[:, n % 4, g, j, P * a:P * a + P],
                                     QS[:, n % 4, g, :], start=True, stop=True)
                        ins.then_inc(st_mm, 1)
                    m, u = divmod(t - T_AV, 16)
                    if u % 4 == 0 and 0 <= m < NB:
                        n, u = NB * L + m, u // 4
                        pe.wait_ge(exp_done, H * n + 4 * u + 4)
                        if u == 0:
                            pe.wait_ge(v_ev, n + 1)
                            if n:
                                pe.wait_ge(raw_ev, n)
                        for a in range(2):
                            for c4 in range(4):
                                half, j, _, g, h = head_of(4 * u + c4)
                                ins = mm(ps[32 * c4:32 * c4 + 32, AVB, S * half:S * half + S],
                                         VA[:, n % 4, a, 80 * g + 32 * j:80 * g + 32 * j + 32],
                                         Pt[:, u % 2, c4, S * a:S * a + S],
                                         start=(j == 0 and a == 0), stop=(j == 1 and a == 1), skip_group_check=True)
                        ins.then_inc(av_mm, 1)
                    m = due(T_O1, t)
                    if m is not None:
                        n = NB * L + m
                        pe.wait_ge(raw_ev, n + 1)
                        pe.wait_ge(k_ev, NB * L + issued(T_K, t))
                        pe.wait_ge(q_ev, NB * L + issued(T_Q, t))
                        for i in range(4):
                            ins = pe.transpose(ps[:, BA, P * i:P * i + P], raw[:, P * i:P * i + P], ident[:, :])
                        ins.then_inc(o1_t, 1)
                    m = due(T_O2, t)
                    if m is not None:
                        n = NB * L + m
                        pe.wait_ge(on_done, n + 1)
                        pe.wait_ge(xt_ev, NB * L + issued(T_X, t))
                        pe.wait_ge(v_ev, NB * L + issued(T_V, t))
                        pe.wait_ge(negm_ev, NB * L + issued(T_MX, t))
                        if (c := NB * L + issued(T_XT, t)):
                            pe.wait_ge(post_ev, c)
                        for a in range(2):
                            ins = pe.transpose(ps[:, BB, P * a:P * a + P], on[:, a, :], ident[:, :])
                        ins.then_inc(o2_t, 1)
                    m = due(T_OUT, t)
                    if m is not None:
                        n = NB * L + m
                        pe.wait_ge(onT_ev, n + 1)
                        pe.wait_ge(v_ev, NB * L + issued(T_V, t))
                        pe.wait_ge(xt_ev, NB * L + issued(T_X, t))
                        pe.wait_ge(negm_ev, NB * L + issued(T_MX, t))
                        for a in range(2):
                            ins = mm(ps[:, BB, P * a:P * a + P], onT[:, P * a:P * a + P], w_at[:, L, 3, :],
                                     start=True, stop=True)
                        ins.then_inc(out_mm, 1)
                    m = due(T_XT, t)
                    if m is not None:
                        n = NB * L + m
                        pe.wait_ge(post_n, 2 * (n + 1))
                        pe.wait_ge(v_ev, NB * L + issued(T_V, t))
                        pe.wait_ge(xt_ev, NB * L + issued(T_X, t))
                        pe.wait_ge(x_new, NB * L + issued(T_OUT, t))
                        pe.wait_ge(negm_ev, NB * L + issued(T_MX, t))
                        pe.wait_ge(onT_ev, NB * L + issued(T_O2, t))
                        for a in range(2):
                            ins = pe.transpose(ps[:, BB, P * a:P * a + P], xp[:, n % 2, a, :], ident[:, :])
                        ins.then_inc(post_t, 1)
                if L == 0:
                    spread_max(2)
                    for c in range(4):
                        for f in range(FT):
                            i = 4 * c + f
                            if f == 0:
                                pe.wait_ge(xq_b, c + 1)
                            if i >= 2:
                                pe.wait_ge(gelu, i - 1)
                            mm(ps[:, ps_st[i % 2], :], w1q[:, P * f:P * f + P], xq[:, 512 * c:512 * c + 512],
                               start=True, stop=True).then_inc(f1_mm, 1)
                    spread_max(3)
                    for c in range(4):
                        pe.wait_ge(hq_b, FT * (c + 1))
                        if c >= 2:
                            pe.wait_ge(ffn_out, c - 1)
                        for a in range(4):
                            for f in range(FT):
                                ins = mm(ps[:, ps_s[c % 2], P * a:P * a + P], hq[:, f, c % 2, P * a:P * a + P],
                                         w2q[:, f, :], start=(f == 0), stop=(f == FT - 1))
                        ins.then_inc(f2_mm, 1)

            pe.wait_ge(post_ev, 2 * NB)
            for i in range(TILES):
                ins = mm(ps[:, BA, E * i:E * i + E], xT[:, P * i:P * i + P], gw[:, :], start=True, stop=True)
            ins.then_inc(r_mm, 1)
            pe.wait_ge(e_lo, NE)
            pe.wait_ge(x2lo, 4)
            pe.wait_ge(in_wd, 16)
            i = 0
            for q in range(4 * NE + 1):
                if q < 4 * NE:
                    e, c = divmod(q, 4)
                    for f, (f0, fn) in enumerate(FTE):
                        for gu, s_in, s_free in ((0, g_mm, silu), (1, u_mm, h_done)):
                            if i >= 2:
                                pe.wait_ge(s_free, i - 1)
                            bank = 2 * gu + i % 2
                            w0 = FE * gu + f0
                            cols = slice(512 * c, 512 * c + 512)
                            mm(ps[0:fn, bank, :], whi[:, e, w0:w0 + fn], xhi[:, cols], start=True, stop=False)
                            mm(ps[0:fn, bank, :], whi[:, e, w0:w0 + fn], xlo[:, cols], start=False, stop=False)
                            mm(ps[0:fn, bank, :], wlo[:, e, w0:w0 + fn], xhi[:, cols],
                               start=False, stop=True).then_inc(s_in, 1)
                        i += 1
                if q >= 1:
                    p = q - 1
                    e = p // 4
                    pe.wait_ge(h_done, 3 * (p + 1))
                    if p >= 2:
                        pe.wait_ge(acc, 4 * (p - 1))
                    for a in range(4):
                        for f, (f0, fn) in enumerate(FTE):
                            ins = mm(ps[:, 4 + p % 2, P * a:P * a + P], hh[0:fn, p % 2, f, P * a:P * a + P],
                                     wd[0:fn, e, f, :], start=(f == 0), stop=(f == 2))
                    ins.then_inc(d_mm, 1)

        @block.scalar
        def _(act):
            A = nc.scalar.activation

            def split_expert(e):
                act.wait_ge(in_e[e % 2], 16 * (e // 2 + 1))
                A(whi[:, e, :], wst[:, e % 2, :], ACT.Identity).then_inc(e_hi, 1)

            act.wait_ge(in_w, ALL_W)
            for L in range(2):
                for t in range(T_FIRST, T_LAST + 1):
                    m = due(T_K + 1, t)
                    if m is not None:
                        n = NB * L + m
                        act.wait_ge(k_mm, n + 1)
                        if n >= 2:
                            act.wait_ge(k_lo, n - 1)
                        if L == 0:
                            A(kf[:, n % 2, :], ps[:, BA, 0:S], ACT.Identity, bias=b_at[:, L, 1:2])
                            A(rot[:, n % 2, :], ps[:, BA, S:2 * S], ACT.Identity, bias=b_sw[:, 1:2]).then_inc(k_ev, 1)
                        else:
                            A(kf[:, n % 2, :], ps[:, BA, 0:S], ACT.Identity, bias=b_at[:, L, 1:2]).then_inc(k_ev, 1)
                    m = due(T_X + 1, t)
                    if m is not None:
                        n = NB * L + m
                        act.wait_ge(xt_mm, n + 1)
                        if n >= 2:
                            act.wait_ge(q_mm, n - 1)
                        A(pre_T[:, n % 2, :], ps[:, BB, 0:S], ACT.Copy).then_inc(xt_ev, 1)
                    m = due(T_Q + 1, t)
                    if m is not None:
                        n = NB * L + m
                        act.wait_ge(q_mm, n + 1)
                        if n >= 2:
                            act.wait_ge(q_lo, n - 1)
                        if L == 0:
                            A(qf[:, n % 2, :], ps[:, BA, 0:S], ACT.Identity, bias=b_at[:, L, 0:1])
                            A(rotq[:, n % 2, :], ps[:, BA, S:2 * S], ACT.Identity, bias=b_sw[:, 0:1]).then_inc(q_ev, 1)
                        else:
                            A(qf[:, n % 2, :], ps[:, BA, 0:S], ACT.Identity, bias=b_at[:, L, 0:1]).then_inc(q_ev, 1)
                    m = due(T_K + 6, t)
                    if m is not None:
                        n = NB * L + m
                        if L == 0:
                            act.wait_ge(k_rot, 3 * n + 3)
                        else:
                            act.wait_ge(k_ev, n + 1)
                        if n >= 2:
                            act.wait_ge(kp_in[(n - 2) % 4], 128 * ((n - 2) // 4 + 1))
                        A(khi[:, n % 2, :], kf[:, n % 2, :], ACT.Copy).then_inc(k_hi, 1)
                    m = due(T_Q + 6, t)
                    if m is not None:
                        n = NB * L + m
                        if L == 0:
                            act.wait_ge(q_rot, 3 * n + 3)
                        else:
                            act.wait_ge(q_ev, n + 1)
                        if n >= 2:
                            act.wait_ge(qs_in[(n - 2) % 4], 64 * ((n - 2) // 4 + 1))
                        A(qhi[:, n % 2, :], qf[:, n % 2, :], ACT.Copy).then_inc(q_hi, 1)
                    m = due(T_MX + 1, t)
                    if m is not None:
                        n = NB * L + m
                        act.wait_ge(mx_t, n + 1)
                        if n >= 2:
                            act.wait_ge(m_in[(n - 2) % 4], 16 * ((n - 2) // 4 + 1))
                        A(negm[:, n % 2, :], ps[0:H, BB, 0:S], ACT.Copy, scale=-1.0 / MAXROW).then_inc(negm_ev, 1)
                    m, k = divmod(t, 16)
                    if 0 <= m < NB:
                        n = NB * L + m
                        i = H * n + k
                        act.wait_ge(st_mm, i + 1)
                        if k % 4 == 0 and i >= 8:
                            act.wait_ge(av_mm, i // 4 - 1)
                        A(Pt[:, (i // 4) % 2, i % 4, :], ps[:, ps_st[i % 3], :], ACT.Exp, scale=SM_SCALE)\
                            .then_inc(exp_done, 1)
                    m = due(T_AV + 13, t)
                    if m is not None:
                        n = NB * L + m
                        act.wait_ge(av_mm, 4 * (n + 1))
                        if n:
                            act.wait_ge(o1_t, n)
                        A(raw[:, :], ps[:, AVB, :], ACT.Copy).then_inc(raw_ev, 1)
                    m = due(T_O2 + 1, t)
                    if m is not None:
                        n = NB * L + m
                        act.wait_ge(o2_t, n + 1)
                        if n:
                            act.wait_ge(out_mm, n)
                        A(onT[:, :], ps[:, BB, 0:S], ACT.Copy).then_inc(onT_ev, 1)
                        if n < NE:
                            split_expert(n)
                    m = due(T_XT + 1, t)
                    if m is not None:
                        n = NB * L + m
                        act.wait_ge(post_t, n + 1)
                        if n == NB:
                            act.wait_ge(xq_a, 4)
                        A(xT[:, S * m:S * m + S], ps[:, BB, 0:S], ACT.Copy).then_inc(post_ev, 1)
                if L == 0:
                    act.wait_ge(f_sc, 1)
                    for i in range(16):
                        c, f = divmod(i, 4)
                        act.wait_ge(f1_mm, i + 1)
                        A(hb[:, f, 512 * c:512 * c + 512], ps[:, ps_st[i % 2], :], ACT.Gelu,
                          bias=b1s[:, f:f + 1], scale=sc[:, 3:4]).then_inc(gelu, 1)
                    act.wait_ge(gm_s, 4)
                    for c in range(4):
                        for f in range(FT):
                            A(hb[:, f, 512 * c:512 * c + 512], hb[:, f, 512 * c:512 * c + 512], ACT.Copy,
                              scale=sc[:, 6:7], bias=ROUND).then_inc(hq_a, 1)

            act.wait_ge(post_ev, 2 * NB)
            for c in range(4):
                A(xhi[:, 512 * c:512 * c + 512], xT[:, 512 * c:512 * c + 512], ACT.Copy).then_inc(x2hi, 1)
            act.wait_ge(rt, 3)
            A(pr[:, :, :], lg[:, :, :], ACT.Exp).then_inc(rt, 1)
            i = 0
            for q in range(4 * NE):
                for f, (f0, fn) in enumerate(FTE):
                    act.wait_ge(g_mm, i + 1)
                    if i >= 2:
                        act.wait_ge(h_done, i - 1)
                    A(sg[0:fn, i % 2, :], ps[0:fn, i % 2, :], ACT.Silu).then_inc(silu, 1)
                    i += 1

        @block.vector
        def _(dve):
            V = nc.vector

            def norm_stats(n, src, st, mv_, s_st, s_mv, s_n):
                if n >= 2:
                    dve.wait_ge(s_n, 2 * (n - 1))
                for a in range(2):
                    V.bn_stats(st[:, n % 2, a, :], src(a)).then_inc(s_st, 1)
                for a in range(2):
                    dve.wait_ge(s_st, 2 * n + a + 1)
                    V.bn_aggr(mv_[:, n % 2, a, :], st[:, n % 2, a, :]).then_inc(s_mv, 1)

            def norm_rows(n, src, dst, mv_, r, s_rs, s_n):
                dve.wait_ge(s_rs, n + 1)
                for a in range(2):
                    V.tensor_scalar(dst[:, n % 2, a, :], src(a), mv_[:, n % 2, a, 0:1], r[:, n % 2, a:a + 1],
                                    ALU.subtract, ALU.mult).then_inc(s_n, 1)

            def global_max(i):
                dve.wait_ge(gm_t, i + 1)
                V.tensor_reduce(g1[0:1, 4 + i:5 + i], ps[0:1, BA, 0:P], AX.X, ALU.max).then_inc(gm_b, 1)
                dve.wait_ge(gm_bc, i + 1)
                V.tensor_scalar(sc[:, 8 + i:9 + i], ps[:, BA, P:P + 1], MIN_RANGE, None, ALU.max).then_inc(gm_s, 1)
                dve.wait_ge(gm_s, i + 1)

            chain = [0]

            def step(ins):
                chain[0] += 1
                ins.then_inc(w_abs, 1)
                dve.wait_ge(w_abs, chain[0])

            V.memset(QS[:, :, :, :].rearrange("p b g t -> p (b g t)").bitcast(U32), 0).then_inc(zero_done, 1)
            V.memset(KP[:, :, :, :, :].rearrange("p b g j t -> p (b g j t)").bitcast(U32), 0).then_inc(zero_done, 1)
            dve.wait_ge(in_w, ALL_W)
            for i in range(2):
                V.tensor_reduce(g1[:, i:i + 1], w12[:, FF * i:FF * i + FF], AX.X, ALU.max,
                                apply_absolute_value=True).then_inc(gm_a, 1)
            for i in range(2):
                global_max(i)
                step(V.reciprocal(sc[:, 12 + i:13 + i], sc[:, 8 + i:9 + i]))
                step(V.tensor_scalar(sc[:, 12 + i:13 + i], sc[:, 12 + i:13 + i], QP, None, ALU.mult))
                step(V.tensor_scalar(w12[:, FF * i:FF * i + FF], w12[:, FF * i:FF * i + FF],
                                     sc[:, 12 + i:13 + i], ROUND, ALU.mult, ALU.add))
                dst = w1q[:, :] if i == 0 else w2q[:, :, :].rearrange("p f d -> p (f d)")
                step(V.tensor_scalar(dst, w12[:, FF * i:FF * i + FF], ROUND, None, ALU.subtract))
            dve.wait_ge(in_x, 16)

            for L in range(2):
                for t in range(T_FIRST, T_LAST + 1):
                    m = due(T_K, t)
                    if m is not None:
                        n = NB * L + m
                        def src(a, m=m):
                            return x[:, 2 * m + a, :]
                        norm_stats(n, src, st6, mv, pre_st, pre_mv, pre_n)
                    m = due(T_V + 1, t)
                    if m is not None:
                        n = NB * L + m
                        dve.wait_ge(v_mm, n + 1)
                        if n == 0:
                            dve.wait_ge(memset_done, 5)
                        if n >= 4:
                            dve.wait_ge(av_mm, 4 * (n - 3))
                        for a in range(2):
                            ins = V.tensor_tensor(
                                VA[:, n % 4, a, :].rearrange("p (g j w) -> p g j w", g=G, j=2)[:, :, :, 0:HD],
                                ps[:, BB, P * a:P * a + P].rearrange("p (g j d) -> p g j d", g=G, j=2),
                                bv[:, L, :].rearrange("p (g j d) -> p g j d", g=G, j=2), ALU.add)
                        ins.then_inc(v_ev, 1)
                    m = due(T_K + 3, t)
                    if m is not None:
                        n = NB * L + m
                        if n >= 2:
                            dve.wait_ge(xt_mm, n - 1)
                        def src(a, m=m):
                            return x[:, 2 * m + a, :]
                        norm_rows(n, src, xn, mv, rs, pre_rs, pre_n)
                    m, k = divmod(t - T_S, 16)
                    if 0 <= m < NB:
                        n = NB * L + m
                        i = H * n + k
                        g, a = k // 2, k % 2
                        dve.wait_ge(s_mm, i + 1)
                        if k == 0 and n >= 2:
                            dve.wait_ge(mx_t, n - 1)
                        V.tensor_reduce(mx[:, n % 2, a, g:H:G], ps[:, ps_s[i % 2], :].rearrange("p (j k) -> p j k", j=2),
                                        AX.X, ALU.max).then_inc(s_max, 1)
                    m = due(T_O1 + 1, t)
                    if m is not None:
                        n = NB * L + m
                        dve.wait_ge(o1_t, n + 1)
                        o = ps[:, BA, :].rearrange("p (u w) -> p u w", w=32)
                        V.reciprocal(rsum[:, :].rearrange("p (u j) -> p u j", j=2), o[:, :, 16:18]).then_inc(rsum_done, 1)
                        dve.wait_ge(rsum_done, n + 1)
                        if n:
                            dve.wait_ge(o2_t, n)
                        for half in range(2):
                            for a in range(2):
                                q0 = 2 * half + a
                                ins = V.tensor_tensor(
                                    on[:, a, 64 * half:64 * half + 64].rearrange("p (c j d) -> p c j d", c=4, j=2),
                                    ps[:, BA, P * q0:P * q0 + P].rearrange("p (c w) -> p c w", c=4)[:, :, 0:16]
                                        .rearrange("p c (j d) -> p c j d", j=2),
                                    rsum[:, 8 * q0:8 * q0 + 8].rearrange("p (c j) -> p c j", j=2).unsqueeze(3)
                                        .to_broadcast([P, 4, 2, HD]), ALU.mult)
                        ins.then_inc(on_done, 1)
                    m = due(T_OUT + 1, t)
                    if m is not None:
                        n = NB * L + m
                        dve.wait_ge(out_mm, n + 1)
                        dve.wait_ge(xb_done, n + 1)
                        V.tensor_tensor(x[:, 2 * m:2 * m + 2, :], ps[:, BB, 0:S].rearrange("p (a d) -> p a d", a=2),
                                        xb[:, n % 2, :, :], ALU.add).then_inc(x_new, 1)
                        dve.wait_ge(x_new, n + 1)
                        def src(a, m=m):
                            return x[:, 2 * m + a, :]
                        norm_stats(n, src, st6p, mvp, post_st, post_mv, post_n)
                    m = due(T_OUT + 4, t)
                    if m is not None:
                        n = NB * L + m
                        if n >= 2:
                            dve.wait_ge(post_t, n - 1)
                            if n <= NB + 1:
                                dve.wait_ge(amax_done, min(n - 1, NB))
                        def src(a, m=m):
                            return x[:, 2 * m + a, :]
                        norm_rows(n, src, xp, mvp, rsp, post_rs, post_n)
                        if L == 0:
                            dve.wait_ge(post_n, 2 * (n + 1))
                            V.tensor_reduce(amax[:, m:m + 1], xp[:, n % 2, :, :].rearrange("p a d -> p (a d)"), AX.X, ALU.max,
                                            apply_absolute_value=True).then_inc(amax_done, 1)
                if L == 0:
                    dve.wait_ge(amax_done, NB)
                    V.tensor_reduce(g1[:, 2:3], amax[:, 0:NB], AX.X, ALU.max).then_inc(gm_a, 1)
                    global_max(2)
                    step(V.reciprocal(sc[:, 2:3], sc[:, 10:11]))
                    step(V.tensor_scalar(sc[:, 2:3], sc[:, 2:3], QP, None, ALU.mult))
                    for c in range(4):
                        if c == 0:
                            dve.wait_ge(post_ev, NB)
                        V.tensor_scalar(xT[:, 512 * c:512 * c + 512], xT[:, 512 * c:512 * c + 512], sc[:, 2:3], ROUND,
                                        ALU.mult, ALU.add).then_inc(xq_a, 1)
                        dve.wait_ge(xq_a, c + 1)
                        V.tensor_scalar(xq[:, 512 * c:512 * c + 512], xT[:, 512 * c:512 * c + 512], ROUND, None,
                                        ALU.subtract).then_inc(xq_b, 1)
                        if c == 0:
                            step(V.tensor_scalar(sc[:, 0:1], sc[:, 8:9], 1.0 / QP, None, ALU.mult))
                            step(V.tensor_scalar(sc[:, 1:2], sc[:, 10:11], 1.0 / QP, sc[:, 0:1], ALU.mult, ALU.mult))
                            step(V.tensor_copy(sc[:, 3:4], sc[:, 1:2]))
                            V.tensor_scalar(b1s[:, :], b1[:, :], sc[:, 3:4], None, ALU.mult).then_inc(f_sc, 1)
                    for i in range(16):
                        c, f = divmod(i, 4)
                        dve.wait_ge(gelu, i + 1)
                        if i == 0:
                            pass
                        V.tensor_reduce(amax[:, i:i + 1], hb[:, f, 512 * c:512 * c + 512], AX.X, ALU.max,
                                        apply_absolute_value=True).then_inc(habs, 1)
                    dve.wait_ge(habs, 16)
                    V.tensor_reduce(g1[:, 3:4], amax[:, 0:16], AX.X, ALU.max).then_inc(gm_a, 1)
                    dve.wait_ge(gm_t, 4)
                    V.tensor_reduce(g1[0:1, 7:8], ps[0:1, BA, 0:P], AX.X, ALU.max).then_inc(gm_b, 1)
                    dve.wait_ge(gm_bc, 4)
                    step(V.tensor_scalar(sc[:, 11:12], ps[:, BA, P:P + 1], MIN_RANGE, None, ALU.max))
                    step(V.reciprocal(sc[:, 5:6], sc[:, 11:12]))
                    V.tensor_scalar(sc[:, 6:7], sc[:, 5:6], QP, None, ALU.mult).then_inc(gm_s, 1)
                    step(V.tensor_scalar(sc[:, 4:5], sc[:, 9:10], 1.0 / QP, None, ALU.mult))
                    step(V.tensor_scalar(sc[:, 7:8], sc[:, 11:12], 1.0 / QP, sc[:, 4:5], ALU.mult, ALU.mult))
                    for c in range(5):
                        if c < 4:
                            for f in range(FT):
                                dve.wait_ge(hq_a, FT * c + f + 1)
                                if f == 0 and c >= 2:
                                    dve.wait_ge(f2_mm, c - 1)
                                V.tensor_scalar(hq[:, f, c % 2, :], hb[:, f, 512 * c:512 * c + 512], ROUND, None,
                                                ALU.subtract).then_inc(hq_b, 1)
                        if c >= 1:
                            p = c - 1
                            xs = x[:, 4 * p:4 * p + 4, :]
                            dve.wait_ge(f2_mm, p + 1)
                            if p >= 1:
                                dve.wait_ge(ffn_out, p)
                            V.tensor_tensor(sg[:, 0, :].rearrange("p (a d) -> p a d", a=4),
                                            ps[:, ps_s[p % 2], :].rearrange("p (a d) -> p a d", a=4),
                                            b2[:, :].unsqueeze(1).to_broadcast([P, 4, D]), ALU.add).then_inc(f2_ev, 1)
                            dve.wait_ge(f2_ev, p + 1)
                            V.scalar_tensor_tensor(out=xs, in0=sg[:, 0, :].rearrange("p (a d) -> p a d", a=4),
                                                   scalar=sc[:, 7:8], in1=xs, op0=ALU.mult, op1=ALU.add).then_inc(ffn_out, 1)
                            if p == 3:
                                dve.wait_ge(ffn_out, 4)

            for c in range(4):
                dve.wait_ge(x2hi, c + 1)
                V.tensor_tensor(xlo[:, 512 * c:512 * c + 512], xT[:, 512 * c:512 * c + 512],
                                xhi[:, 512 * c:512 * c + 512], ALU.subtract).then_inc(x2lo, 1)
            bc = [P, TILES, E]
            dve.wait_ge(r_mm, 1)
            V.tensor_copy(lg[:, :, :], ps[:, BA, 0:TILES * E].rearrange("p (t e) -> p t e", e=E)).then_inc(rt, 1)
            dve.wait_ge(rt, 1)
            V.tensor_reduce(r1[:, :], lg[:, :, :], AX.X, ALU.max).then_inc(rt, 1)
            dve.wait_ge(rt, 2)
            V.tensor_tensor(lg[:, :, :], lg[:, :, :], r1[:, :].unsqueeze(2).to_broadcast(bc), ALU.subtract).then_inc(rt, 1)
            dve.wait_ge(rt, 4)
            step(V.tensor_reduce(r1[:, :], pr[:, :, :], AX.X, ALU.add))
            step(V.reciprocal(r2[:, :], r1[:, :]))
            step(V.tensor_tensor(pr[:, :, :], pr[:, :, :], r2[:, :].unsqueeze(2).to_broadcast(bc), ALU.mult))
            for i in range(TILES):
                step(V.max(t8[:, i, :], pr[:, i, :])) if i == TILES - 1 else V.max(t8[:, i, :], pr[:, i, :])
            for i in range(TILES):
                ins = V.max_index(i8[:, i, :], t8[:, i, :], pr[:, i, :])
            step(ins)
            step(V.tensor_copy(i8f[:, :, :], i8[:, :, 0:2]))
            for a in range(2):
                ins = V.tensor_tensor(oh[:, a, :, :], iota[:, :, :], i8f[:, :, a].unsqueeze(2).to_broadcast(bc), ALU.is_equal)
            step(ins)
            step(V.tensor_tensor(oh[:, 0, :, :], oh[:, 0, :, :], oh[:, 1, :, :], ALU.add))
            step(V.tensor_tensor(pr[:, :, :], pr[:, :, :], oh[:, 0, :, :], ALU.mult))
            step(V.tensor_reduce(r1[:, :], pr[:, :, :], AX.X, ALU.add))
            step(V.tensor_scalar(r1[:, :], r1[:, :], 1e-20, None, ALU.add))
            step(V.reciprocal(r2[:, :], r1[:, :]))
            step(V.tensor_tensor(comb[:, :, :], pr[:, :, :], r2[:, :].unsqueeze(2).to_broadcast(bc), ALU.mult))
            i = 0
            for q in range(4 * NE + 1):
                if q < 4 * NE:
                    e, c = divmod(q, 4)
                    for f, (f0, fn) in enumerate(FTE):
                        dve.wait_ge(silu, i + 1)
                        dve.wait_ge(u_mm, i + 1)
                        if f == 0 and q >= 2:
                            dve.wait_ge(d_mm, q - 1)
                        V.tensor_tensor(hh[0:fn, q % 2, f, :], sg[0:fn, i % 2, :], ps[0:fn, 2 + i % 2, :],
                                        ALU.mult).then_inc(h_done, 1)
                        i += 1
                if q >= 1:
                    p = q - 1
                    e, c = divmod(p, 4)
                    dve.wait_ge(d_mm, p + 1)
                    if p >= 4:
                        dve.wait_ge(acc, 4 * (p - 3))
                    for a in range(4):
                        xs = x[:, 4 * c + a, :]
                        w = comb[:, 4 * c + a, e:e + 1] if e < E else 1.0
                        V.scalar_tensor_tensor(out=xs, in0=ps[:, 4 + p % 2, P * a:P * a + P], scalar=w, in1=xs,
                                               op0=ALU.mult, op1=ALU.add).then_inc(acc, 1)


def kernel(**inputs):
    import concourse.bacc as _bacc
    from concourse import mybir as _mybir
    from concourse.bass_utils import run_bass_kernel_spmd as _run

    a = {k: np.asarray(v) for k, v in inputs.items()}
    f32 = np.float32

    order = np.array([(2 * g + j) * HD + d for j in range(2) for d in range(HD) for g in range(G)])
    swapped = np.array([(2 * g + j) * HD + (d + HD // 2) % HD for j in range(2) for d in range(HD) for g in range(G)])
    w0 = {k: a[f"L0_xattn_W{k}"].T for k in "qkvo"}
    w1 = {k: a[f"L1_xattn_w{k}"] for k in "qkvo"}
    w_at = np.stack([np.stack([w["q"][:, order], w["k"][:, order], w["v"], w["o"]], 1) for w in (w0, w1)], 1)
    w_sw = np.stack([w0["q"][:, swapped], w0["k"][:, swapped]], 1)
    b = [{k: a[f"L{n}_xattn_b{k}"] for k in "qkvo"} for n in range(2)]
    b_at = np.stack([np.stack([c["q"][order], c["k"][order]], 1) for c in b], 1)
    b_sw = np.stack([b[0]["q"][swapped], b[0]["k"][swapped]], 1)

    inv = (1.0 / 10000.0 ** (np.arange(0, HD, 2, dtype=f32) / f32(HD))).astype(f32)
    ang = np.outer(np.arange(S, dtype=f32), inv).astype(f32)
    dd = np.array([d for _ in range(2) for d in range(HD) for _ in range(G)])
    cos = np.cos(ang)[:, dd % (HD // 2)].T.astype(f32)
    sin = (np.sin(ang)[:, dd % (HD // 2)].T * np.where(dd < HD // 2, -1, 1)[:, None]).astype(f32)
    kp = np.zeros((2, G, 2, S), np.float16)
    kp[0, :, 0] = MAXROW
    kp[1, :, 1] = MAXROW

    gate = np.concatenate([a["L1_ffn_expert_gate"], a["L1_ffn_shared_gate"][None]])
    up = np.concatenate([a["L1_ffn_expert_up"], a["L1_ffn_shared_up"][None]])
    down = np.concatenate([a["L1_ffn_expert_down"], a["L1_ffn_shared_down"][None]])
    wgu = np.concatenate([gate, up], 1).transpose(0, 2, 1)
    wd = np.zeros((P, NE, 3, D), f32)
    for f, (f0, fn) in enumerate(FTE):
        wd[:fn, :, f] = down[:, :, f0:f0 + fn].transpose(2, 0, 1)
    arrays = {
        "x": a["x"],
        "ctxT": a["ctx_1024"].transpose(0, 2, 1),
        "w_at": w_at, "w_sw": w_sw, "b_at": b_at, "b_sw": b_sw,
        "bv": np.stack([c["v"] for c in b]), "bo": np.stack([c["o"] for c in b]),
        "w12": np.concatenate([a["L0_ffn_w1"].T, a["L0_ffn_w2"].T.reshape(FT, P, D).transpose(1, 0, 2).reshape(P, FF)], 1),
        "b1": a["L0_ffn_b1"].reshape(FT, P).T, "b2": a["L0_ffn_b2"],
        "wgu": wgu, "wd": wd, "gw": a["L1_ffn_gate_w"].T,
        "c_ident": np.eye(P, dtype=f32), "c_cos": cos, "c_sin": sin, "c_kp": kp,
        "c_iota": np.tile(np.arange(E, dtype=f32), (TILES, 1)),
    }
    nc = _bacc.Bacc("TRN2", target_bir_lowering=False, num_devices=1)
    feeds, io = {}, {}
    for name, v in arrays.items():
        v = np.ascontiguousarray(v)
        feeds[f"in_{name}"] = v
        io[name] = nc.dram_tensor(f"in_{name}", v.shape, _mybir.dt.from_np(v.dtype), kind="ExternalInput").ap()
    out = nc.dram_tensor("out_0", (NB, S, D), F32, kind="ExternalOutput").ap()
    layers(nc, io, out)
    r = _run(nc, [feeds], core_ids=[0])
    return r.results[0]["out_0"]
```

```python
from contextlib import ExitStack

import numpy as np

import concourse.bass as bass
from concourse import mybir

F32 = mybir.dt.float32
F16 = mybir.dt.float16
BF16 = mybir.dt.bfloat16
U32 = mybir.dt.uint32
ALU = mybir.AluOpType
ACT = mybir.ActivationFunctionType
AX = mybir.AxisListType

P = 128
NB = 8
S = 256
D = 128
H = 16
HD = D // H
G = H // 2
NT = NB * S
TILES = NT // P
FF = 512
FT = FF // P
E = 8
NE = E + 1
FE = 352
FTE = [(0, 128), (128, 128), (256, 96)]
ROW = D + 2
SLOTS = 2 * NT // P + E - 1
RING = 8
QP = 127.0
MIN_RANGE = 1e-6
LN_EPS = 1e-5
SM_SCALE = float(HD) ** -0.5
MAXROW = 64.0
ROUND = 12582912.0

T_K = -51
T_V = -43
T_X = -41
T_Q = -39
T_S = -21
T_MX = -4
T_AV = 6
T_O1 = 20
T_O2 = 24
T_OUT = 29
T_XT = 35
SP_K = -40
SP_KLO = -32
SP_Q = -29
SP_M = -1
G_PRE = -47
G_KROT = -41
G_KLO = -40
G_QROT = -40
G_QLO = -26
G_XB = 23
G_POST = 28
A_K = -47
A_X = -42
A_Q = -38
A_KHI = -44
A_QHI = -32
A_MX = -5
A_RAW = 17
A_O2 = 24
A_XT = 33
D_STAT = -53
D_V = -43
D_NORM = -45
D_O1 = 22
D_OUT = 29
D_POST = 34
T_FIRST, T_LAST = min(T_K, SP_K, G_PRE, A_K, D_STAT), 16 * (NB - 1) + max(T_XT, A_XT, D_POST) + 1


def issued(offset, t, per=1):
    return per * min(NB, max(0, -((offset - t) // 16)))


def due(offset, t):
    m, r = divmod(t - offset, 16)
    return m if r == 0 and 0 <= m < NB else None


def head_of(k):
    half, j, c = k // 8, (k // 4) % 2, k % 4
    g = 4 * half + c
    return half, j, c, g, 2 * g + j


def layers(nc, io, out):
    ctx = ExitStack()
    with ctx:
        def sb(name, shape, dt=F32):
            return ctx.enter_context(nc.sbuf_tensor(name, shape, dt))

        def sem(name):
            return ctx.enter_context(nc.semaphore(name))

        ps = ctx.enter_context(nc.psum_tensor("ps", [P, 8, 512], F32))
        ps_st = [0, 1, 2]
        ps_s = [3, 4]
        AVB, BA, BB = 5, 6, 7

        x = sb("x", [P, TILES, D])
        xb = sb("xb", [P, 2, 2, D])
        xn = sb("xn", [P, 2, 2, D])
        xp = sb("xp", [P, 2, 2, D])
        xT = sb("xT", [P, NT])
        pre_T = sb("pre_T", [P, 2, S])
        ctxT = sb("ctxT", [P, 2, S])
        ident = sb("ident", [P, P])
        cos = sb("cos", [P, S])
        sin = sb("sin", [P, S])
        w_at = sb("w_at", [P, 2, 4, D])
        w_sw = sb("w_sw", [P, 2, D])
        b_at = sb("b_at", [P, 2, 2])
        b_sw = sb("b_sw", [P, 2])
        bv = sb("bv", [P, 2, D])
        bo = sb("bo", [P, 2, D])
        kf = sb("kf", [P, 2, S])
        rot = sb("rot", [P, 2, S])
        khi = sb("khi", [P, 2, S], F16)
        klo = sb("klo", [P, 2, S], F16)
        qf = sb("qf", [P, 2, S])
        rotq = sb("rotq", [P, 2, S])
        qhi = sb("qhi", [P, 2, S], F16)
        qlo = sb("qlo", [P, 2, S], F16)
        QS = sb("QS", [P, 4, G, S], F16)
        KP = sb("KP", [P, 4, G, 2, S], F16)
        VA = sb("VA", [P, 4, 2, G * 80])
        mx = sb("mx", [P, 2, 2, H])
        negm = sb("negm", [H, 2, S], F16)
        Pt = sb("Pt", [P, 2, 4, 512])
        raw = sb("raw", [P, 512])
        rsum = sb("rsum", [P, 4 * 4 * 2])
        on = sb("on", [P, 2, D])
        onT = sb("onT", [P, S])
        st6 = sb("st6", [P, 2, 2, 6])
        mv = sb("mv", [P, 2, 2, 2])
        sd = sb("sd", [P, 2, 2])
        rs = sb("rs", [P, 2, 2])
        st6p = sb("st6p", [P, 2, 2, 6])
        mvp = sb("mvp", [P, 2, 2, 2])
        sdp = sb("sdp", [P, 2, 2])
        rsp = sb("rsp", [P, 2, 2])
        neghalf = sb("neghalf", [P, 2])
        ones = sb("ones", [P, P])
        amax = sb("amax", [P, 16])
        g1 = sb("g1", [P, 8])
        w1q = sb("w1q", [P, FF], BF16)
        w2q = sb("w2q", [P, FT, D], BF16)
        b1 = sb("b1", [P, FT])
        b1s = sb("b1s", [P, FT])
        b2 = sb("b2", [P, D])
        sc = sb("sc", [P, 16])
        xq = sb("xq", [P, NT], BF16)
        hb = sb("hb", [P, FT, NT])
        hq = Pt[:, 0, :, :].rearrange("p a b -> p (a b)").bitcast(BF16).rearrange("p (f c t) -> p f c t", f=FT, c=2)
        w12 = hb[:, 0, 0:2 * FF]
        wst = sb("wst", [P, 2, 2 * FE])
        whi = sb("whi", [P, NE, 2 * FE], F16)
        wlo = sb("wlo", [P, NE, 2 * FE], F16)
        kp32 = KP[:, :, :, :, :].rearrange("p b g j t -> p (b g j t)").bitcast(F32)
        qs32 = QS[:, :, :, :].rearrange("p b g t -> p (b g t)").bitcast(F32)
        hb32 = hb[:, :, :].rearrange("p f t -> p (f t)")
        wd = kp32[:, 0:NE * 3 * D].rearrange("p (e f d) -> p e f d", e=NE, f=3)
        ytok = kp32[:, 3456:3456 + TILES * 2 * D].rearrange("p (t k d) -> p t k d", t=TILES, k=2)
        xh = kp32[:, 7936:8064].bitcast(F16).rearrange("p (b t) -> p b t", b=2)
        xl = kp32[:, 8064:8192].bitcast(F16).rearrange("p (b t) -> p b t", b=2)
        xhi = qs32[:, 0:NT // 2].bitcast(F16)
        xlo = qs32[:, NT // 2:NT].bitcast(F16)
        ht = qs32[:, 2440:2440 + 2 * FE].rearrange("p (b f) -> p b f", b=2)
        hT = qs32[:, 3144:3144 + 6 * P].rearrange("p (b f t) -> p b f t", b=2, f=3)
        rows = hb32[:, 0:RING * ROW].rearrange("p (b c) -> p b c", b=RING)
        yb = hb32[:, RING * ROW:RING * (ROW + D)].rearrange("p (b d) -> p b d", b=RING)
        XR = hb32[:, 0:2 * TILES * ROW].rearrange("p (k t c) -> p k t c", k=2, t=TILES)
        gw = sb("gw", [P, E])
        rt_sb = hb32[:, 4224:8192]
        lg, pr, t8, i8, oh0, oh1, cum, slot, tmp, cnt, big = (
            rt_sb[:, P * i:P * i + P].rearrange("p (t e) -> p t e", e=E) for i in range(11))
        i8 = i8.bitcast(U32)
        oh = rt_sb[:, 4 * P:6 * P].rearrange("p (a t e) -> p a t e", a=2, e=E)
        r0 = 11 * P
        i8f = rt_sb[:, r0:r0 + 32].rearrange("p (t a) -> p t a", a=2)
        r1 = rt_sb[:, r0 + 32:r0 + 48]
        r2 = rt_sb[:, r0 + 48:r0 + 64]
        tot = rt_sb[:, r0 + 64:r0 + 72]
        b_a = rt_sb[:, r0 + 72:r0 + 80]
        b_b = rt_sb[:, r0 + 80:r0 + 88]
        b_c = rt_sb[:, r0 + 88:r0 + 96]
        slot_u = rt_sb[:, r0 + 96:r0 + 128].rearrange("p (k t) -> p k t", k=2).bitcast(U32)
        selh = rt_sb[:, 12 * P:12 * P + P // 2].bitcast(F16)
        cmp_ = rt_sb[:, 13 * P:13 * P + SLOTS * E].rearrange("p (i e) -> p i e", e=E)
        exf = rt_sb[:, 17 * P:17 * P + SLOTS]
        exu = rt_sb[:, 18 * P:18 * P + SLOTS].bitcast(U32)
        dst_u = sb("dst_u", [P, RING], U32)
        iota = hb32[:, 7168:7296].rearrange("p (t e) -> p t e", e=E)
        tokd = hb32[:, 7296:7328].rearrange("p (k t) -> p k t", k=2)
        tri = hb32[:, 7328:7456].bitcast(F16).rearrange("p (a c) -> p a c", a=2)
        tile0 = hb32[:, 7456:7456 + SLOTS * E].rearrange("p (i e) -> p i e", e=E)
        sg = Pt[:, :, :, :].rearrange("p a b c -> p (a b c)")[:, 3072:4096].rearrange("p (q t) -> p q t", q=2)
        hh = Pt[:, :, :, :].rearrange("p a b c -> p (a b c)")[:, 0:3072].rearrange("p (q f t) -> p q f t", q=2, f=3)

        in_w = sem("in_w")
        in_x = sem("in_x")
        in_wd = sem("in_wd")
        in_tab = sem("in_tab")
        in_kp = sem("in_kp")
        in_e = [sem("in_e0"), sem("in_e1")]
        in_ctx = [sem("in_ctx0"), sem("in_ctx1")]
        memset_done = sem("memset_done")
        zero_done = sem("zero_done")
        xb_done = sem("xb_done")
        pre_st = sem("pre_st"); pre_mv = sem("pre_mv"); pre_sd = sem("pre_sd"); pre_rs = sem("pre_rs"); pre_n = sem("pre_n")
        post_st = sem("post_st"); post_mv = sem("post_mv"); post_sd = sem("post_sd"); post_rs = sem("post_rs"); post_n = sem("post_n")
        k_mm = sem("k_mm"); v_mm = sem("v_mm"); xt_mm = sem("xt_mm"); q_mm = sem("q_mm")
        k_ev = sem("k_ev"); v_ev = sem("v_ev"); xt_ev = sem("xt_ev"); q_ev = sem("q_ev")
        k_rot = sem("k_rot"); q_rot = sem("q_rot")
        k_hi = sem("k_hi"); q_hi = sem("q_hi"); k_lo = sem("k_lo"); q_lo = sem("q_lo")
        kp_in = [sem(f"kp_in{i}") for i in range(4)]
        qs_in = [sem(f"qs_in{i}") for i in range(4)]
        m_in = [sem(f"m_in{i}") for i in range(4)]
        s_mm = sem("s_mm"); s_max = sem("s_max"); mx_t = sem("mx_t"); negm_ev = sem("negm_ev")
        st_mm = sem("st_mm"); exp_done = sem("exp_done"); av_mm = sem("av_mm"); raw_ev = sem("raw_ev")
        o1_t = sem("o1_t"); rsum_done = sem("rsum_done"); on_done = sem("on_done")
        o2_t = sem("o2_t"); onT_ev = sem("onT_ev"); out_mm = sem("out_mm"); x_new = sem("x_new")
        post_t = sem("post_t"); post_ev = sem("post_ev"); amax_done = sem("amax_done")
        gm_a = sem("gm_a"); gm_t = sem("gm_t"); gm_b = sem("gm_b"); gm_bc = sem("gm_bc"); gm_s = sem("gm_s")
        w_abs = sem("w_abs"); w_q1 = sem("w_q1"); w_q2 = sem("w_q2")
        f_sc = sem("f_sc"); xq_a = sem("xq_a"); xq_b = sem("xq_b"); f1_mm = sem("f1_mm"); gelu = sem("gelu"); habs = sem("habs")
        hq_a = sem("hq_a"); hq_b = sem("hq_b"); f2_mm = sem("f2_mm"); f2_ev = sem("f2_ev"); ffn_out = sem("ffn_out")
        e_hi = sem("e_hi"); e_lo = sem("e_lo")
        x2hi = sem("x2hi"); x2lo = sem("x2lo"); r_mm = sem("r_mm")
        rt = sem("rt"); r_sel = sem("r_sel"); r_pre = sem("r_pre"); r_slot = sem("r_slot"); r_exp = sem("r_exp")
        xr_copy = sem("xr_copy"); filled = sem("filled"); sent = sem("sent")
        row_in = [sem(f"row_in{i}") for i in range(RING)]
        a_t = sem("a_t"); a_hi = sem("a_hi"); a_lo = sem("a_lo"); b_mm = sem("b_mm"); b_silu = sem("b_silu"); b_h = sem("b_h")
        c_t = sem("c_t"); c_ev = sem("c_ev"); d2_mm = sem("d2_mm"); d2_ev = sem("d2_ev"); d2_idx = sem("d2_idx")
        back = [sem(f"back{i}") for i in range(RING)]
        y_in = [sem(f"y_in{c}") for c in range(4)]; y_sum = sem("y_sum")
        g_mm = sem("g_mm"); u_mm = sem("u_mm"); silu = sem("silu"); h_done = sem("h_done"); d_mm = sem("d_mm"); acc = sem("acc")
        stored = sem("stored")

        NW = 0
        def post_rows(n, a):
            return xp[:, n % 2, a, :] if n < NB else XR[:, 0, 2 * (n - NB) + a, 2:ROW]

        block = ctx.enter_context(nc.Block())

        x_dram = io["x"].rearrange("b (a p) d -> p (b a) d", p=P)
        out_dram = out.rearrange("b (a p) d -> p (b a) d", p=P)

        rows_dram = nc.dram_tensor("rows", [SLOTS * P, ROW], F32).ap()
        y_dram = nc.dram_tensor("y_rows", [2 * NT + SLOTS * P, D], F32).ap()
        weights = [
            (ident[:, :], io["c_ident"]), (cos[:, :], io["c_cos"]), (sin[:, :], io["c_sin"]),
            (w_at[:, :, :, :], io["w_at"]), (w_sw[:, :, :], io["w_sw"]),
            (b_at[:, :, :], io["b_at"]), (b_sw[:, :], io["b_sw"]),
            (bv[:, :, :], io["bv"].partition_broadcast(P)), (bo[:, :, :], io["bo"].partition_broadcast(P)),
            (w12, io["w12"]), (b1[:, :], io["b1"]), (b2[:, :], io["b2"].partition_broadcast(P)),
            (gw[:, :], io["gw"]),
        ]
        tables = [(iota, io["c_iota"].partition_broadcast(P)), (tokd, io["c_tokd"]), (tri, io["c_tri"]),
                  (tile0, io["c_tile0"].partition_broadcast(P))]
        ALL_W = 16 * len(weights)

        @block.sync
        def _(sp):
            for b in range(NB):
                if b < 2:
                    sp.dma_start(ctxT[:, b, :], io["ctxT"][b]).then_inc(in_ctx[b], 16)
            for dst, src in weights:
                sp.dma_start(dst, src).then_inc(in_w, 16)
            sp.dma_start(x[:, :, :], x_dram).then_inc(in_x, 16)
            for e in range(2):
                sp.dma_start(wst[:, e, :], io["wgu"][e]).then_inc(in_e[e], 16)
            sp.dma_start(rows_dram, io["c_fill"]).then_inc(filled, 16)
            sp.wait_ge(zero_done, 2)
            for i in range(4):
                sp.dma_start(KP[96:98, i], io["c_kp"]).then_inc(in_kp, 16)
            for L in range(2):
                if L == 1:
                    sp.wait_ge(hq_b, 16)
                    for dst, src in tables:
                        sp.dma_start(dst, src).then_inc(in_tab, 16)
                for t in range(T_FIRST, T_LAST + 1):
                    m = due(SP_K, t)
                    if m is not None:
                        n = NB * L + m
                        if n + 2 < 2 * NB:
                            sp.wait_ge(k_mm, n + 1)
                            sp.wait_ge(v_mm, n + 1)
                            sp.dma_start(ctxT[:, n % 2, :], io["ctxT"][(n + 2) % NB]).then_inc(in_ctx[n % 2], 16)
                        if n >= 4:
                            sp.wait_ge(st_mm, H * (n - 3))
                        sp.wait_ge(k_hi, n + 1)
                        for r in range(2):
                            for j in range(2):
                                sp.dma_start(KP[16 * r + 8 * j:16 * r + 8 * j + 8, n % 4, :, j, :],
                                             khi[64 * j:64 * j + 64, n % 2, :]).then_inc(kp_in[n % 4], 16)
                    m = due(SP_KLO, t)
                    if m is not None:
                        n = NB * L + m
                        sp.wait_ge(k_lo, n + 1)
                        for r in range(2, 4):
                            for j in range(2):
                                sp.dma_start(KP[16 * r + 8 * j:16 * r + 8 * j + 8, n % 4, :, j, :],
                                             klo[64 * j:64 * j + 64, n % 2, :]).then_inc(kp_in[n % 4], 16)
                    m = due(SP_Q, t)
                    if m is not None:
                        n = NB * L + m
                        if n >= 4:
                            sp.wait_ge(st_mm, H * (n - 3))
                        sp.wait_ge(q_hi, n + 1)
                        for r in (0, 2):
                            sp.dma_start(QS[16 * r:16 * r + 16, n % 4, :, :], qhi[:, n % 2, :]).then_inc(qs_in[n % 4], 16)
                        sp.wait_ge(q_lo, n + 1)
                        for r in (1, 3):
                            sp.dma_start(QS[16 * r:16 * r + 16, n % 4, :, :], qlo[:, n % 2, :]).then_inc(qs_in[n % 4], 16)
                    m = due(SP_M, t)
                    if m is not None:
                        n = NB * L + m
                        sp.wait_ge(negm_ev, n + 1)
                        sp.dma_start(QS[96:98, n % 4, :, :], negm[:, n % 2, :]).then_inc(m_in[n % 4], 16)
                    m = due(T_O1 + 4, t)
                    if m is not None and NB * L + m + 2 < NE:
                        n = NB * L + m
                        sp.wait_ge(e_lo, n + 1)
                        sp.dma_start(wst[:, n % 2, :], io["wgu"][n + 2]).then_inc(in_e[n % 2], 16)
            sp.wait_ge(st_mm, 2 * NB * H)
            sp.wait_ge(s_mm, 2 * NB * H)
            sp.dma_start(wd, io["wd"]).then_inc(in_wd, 16)
            sp.wait_ge(sent, 16 * 2 * TILES)
            for i in range(SLOTS):
                if i >= RING:
                    sp.wait_ge(a_t, i - RING + 1)
                    sp.wait_ge(d2_ev, i - RING + 1)
                    sp.wait_ge(d2_idx, i - RING + 1)
                sp.dma_start(rows[:, i % RING, :], rows_dram[P * i:P * i + P, :]).then_inc(row_in[i % RING], 16)
            for b in range(RING):
                sp.wait_ge(back[b], 16 * len(range(b, SLOTS, RING)))
            for c in range(4):
                sp.dma_start(ytok[:, 4 * c:4 * c + 4, :, :], y_dram[0:2 * NT, :].rearrange(
                    "(t p k) d -> p t k d", p=P, k=2)[:, 4 * c:4 * c + 4]).then_inc(y_in[c], 16)
            for c in range(4):
                sp.wait_ge(y_sum, 2 * c + 2)
                sp.dma_start(out_dram[:, 4 * c:4 * c + 4, :], x[:, 4 * c:4 * c + 4, :]).then_inc(stored, 16)
            sp.wait_ge(stored, 64)

        @block.gpsimd
        def _(pool):
            nc.gpsimd.memset(neghalf[:, :], -0.5).then_inc(memset_done, 1)
            nc.gpsimd.memset(ones[:, :], 1.0).then_inc(memset_done, 1)
            nc.gpsimd.memset(VA[:, :, :, :], 0.0).then_inc(memset_done, 1)
            va5 = VA[:, :, :, :].rearrange("p b k (g w) -> p (b k) g w", g=G)
            pool.wait_ge(memset_done, 3)
            nc.gpsimd.memset(va5[:, :, :, 16:17], 1.0).then_inc(memset_done, 1)
            nc.gpsimd.memset(va5[:, :, :, 49:50], 1.0).then_inc(memset_done, 1)

            def split_expert(e):
                pool.wait_ge(e_hi, e + 1)
                nc.gpsimd.tensor_tensor(wlo[:, e, :], wst[:, e % 2, :], whi[:, e, :], ALU.subtract).then_inc(e_lo, 1)

            def pre_norm(n):
                pool.wait_ge(pre_mv, 2 * (n + 1))
                if n >= 2:
                    pool.wait_ge(pre_n, 2 * (n - 1))
                nc.gpsimd.tensor_scalar(sd[:, n % 2, :], mv[:, n % 2, :, 1], LN_EPS, None, ALU.add).then_inc(pre_sd, 1)
                pool.wait_ge(pre_sd, n + 1)
                nc.gpsimd.tensor_tensor(rs[:, n % 2, :], sd[:, n % 2, :], neghalf[:, :], ALU.pow).then_inc(pre_rs, 1)

            def post_norm(n):
                pool.wait_ge(post_mv, 2 * (n + 1))
                if n >= 2:
                    pool.wait_ge(post_n, 2 * (n - 1))
                nc.gpsimd.tensor_scalar(sdp[:, n % 2, :], mvp[:, n % 2, :, 1], LN_EPS, None, ALU.add).then_inc(post_sd, 1)
                pool.wait_ge(post_sd, n + 1)
                nc.gpsimd.tensor_tensor(rsp[:, n % 2, :], sdp[:, n % 2, :], neghalf[:, :], ALU.pow).then_inc(post_rs, 1)

            pool.wait_ge(in_w, ALL_W)
            pool.wait_ge(in_x, 16)
            for L in range(2):
                if L == 1:
                    pool.wait_ge(ffn_out, 4)
                for t in range(T_FIRST, T_LAST + 1):
                    m = due(G_PRE, t)
                    if m is not None:
                        n = NB * L + m
                        pre_norm(n)
                    m = due(G_KROT, t)
                    if m is not None and L == 0:
                        n = NB * L + m
                        pool.wait_ge(k_ev, n + 1)
                        nc.gpsimd.tensor_tensor(kf[:, n % 2, :], kf[:, n % 2, :], cos[:, :], ALU.mult).then_inc(k_rot, 1)
                        nc.gpsimd.tensor_tensor(rot[:, n % 2, :], rot[:, n % 2, :], sin[:, :], ALU.mult).then_inc(k_rot, 1)
                        pool.wait_ge(k_rot, 3 * n + 2)
                        nc.gpsimd.tensor_tensor(kf[:, n % 2, :], kf[:, n % 2, :], rot[:, n % 2, :], ALU.add).then_inc(k_rot, 1)
                    m = due(G_KLO, t)
                    if m is not None:
                        n = NB * L + m
                        pool.wait_ge(k_hi, n + 1)
                        nc.gpsimd.tensor_tensor(klo[:, n % 2, :], kf[:, n % 2, :], khi[:, n % 2, :], ALU.subtract).then_inc(k_lo, 1)
                    m = due(G_QROT, t)
                    if m is not None and L == 0:
                        n = NB * L + m
                        pool.wait_ge(q_ev, n + 1)
                        nc.gpsimd.tensor_tensor(qf[:, n % 2, :], qf[:, n % 2, :], cos[:, :], ALU.mult).then_inc(q_rot, 1)
                        nc.gpsimd.tensor_tensor(rotq[:, n % 2, :], rotq[:, n % 2, :], sin[:, :], ALU.mult).then_inc(q_rot, 1)
                        pool.wait_ge(q_rot, 3 * n + 2)
                        nc.gpsimd.tensor_tensor(qf[:, n % 2, :], qf[:, n % 2, :], rotq[:, n % 2, :], ALU.add).then_inc(q_rot, 1)
                    m = due(G_QLO, t)
                    if m is not None:
                        n = NB * L + m
                        pool.wait_ge(q_hi, n + 1)
                        nc.gpsimd.tensor_tensor(qlo[:, n % 2, :], qf[:, n % 2, :], qhi[:, n % 2, :], ALU.subtract).then_inc(q_lo, 1)
                    m = due(G_XB, t)
                    if m is not None:
                        n = NB * L + m
                        if n >= 2:
                            pool.wait_ge(x_new, n - 1)
                        for a in range(2):
                            ins = nc.gpsimd.tensor_tensor(xb[:, n % 2, a, :], x[:, 2 * m + a, :], bo[:, L, :], ALU.add)
                        ins.then_inc(xb_done, 1)
                        if n < NE:
                            split_expert(n)
                    m = due(G_POST, t)
                    if m is not None:
                        post_norm(NB * L + m)
                    m = due(T_XT, t)
                    if m is not None and L == 1:
                        pool.wait_ge(post_n, 2 * (NB + m + 1))
                        nc.gpsimd.tensor_scalar(XR[:, 1, 2 * m:2 * m + 2, 2:ROW], XR[:, 0, 2 * m:2 * m + 2, 2:ROW],
                                                1.0, 0.0, ALU.mult, ALU.add).then_inc(xr_copy, 1)
            pool.wait_ge(filled, 16)
            pool.wait_ge(xr_copy, NB)
            pool.wait_ge(r_slot, 1)
            for t in range(TILES):
                for k in range(2):
                    pool.indirect_dma_start(rows_dram, bass.IndirectOffsetOnAxis(ap=slot_u[:, k, t:t + 1], axis=0),
                                            XR[:, k, t, :], None).then_inc(sent, 16)
            for i in range(SLOTS):
                pool.wait_ge(d2_ev, i + 1)
                pool.wait_ge(d2_idx, i + 1)
                pool.indirect_dma_start(y_dram, bass.IndirectOffsetOnAxis(ap=dst_u[:, i % RING:i % RING + 1], axis=0),
                                        yb[:, i % RING, :], None).then_inc(back[i % RING], 16)
            pool.wait_ge(stored, 64)

        @block.tensor
        def _(pe):
            mm = nc.tensor.matmul

            def spread_max(i):
                pe.wait_ge(gm_a, i + 1)
                if i:
                    pe.wait_ge(gm_s, i)
                pe.transpose(ps[0:1, BA, 0:P], g1[:, i:i + 1], ident[:, :]).then_inc(gm_t, 1)
                pe.wait_ge(gm_b, i + 1)
                mm(ps[:, BA, P:P + 1], ones[0:1, :], g1[0:1, 4 + i:5 + i], start=True, stop=True).then_inc(gm_bc, 1)

            pe.wait_ge(in_w, ALL_W)
            pe.wait_ge(memset_done, 5)
            spread_max(0)
            spread_max(1)
            pe.wait_ge(gm_s, 2)

            for L in range(2):
                for t in range(T_FIRST, T_LAST + 1):
                    m = due(T_K, t)
                    if m is not None:
                        n = NB * L + m
                        pe.wait_ge(in_ctx[n % 2], 16 * (n // 2 + 1))
                        if n:
                            pe.wait_ge(q_ev, n)
                        if (c := NB * L + issued(T_O1, t)):
                            pe.wait_ge(on_done, c)
                        ins = mm(ps[:, BA, 0:S], w_at[:, L, 1, :], ctxT[:, n % 2, :], start=True, stop=True)
                        if L == 0:
                            ins = mm(ps[:, BA, S:2 * S], w_sw[:, 1, :], ctxT[:, n % 2, :], start=True, stop=True)
                        ins.then_inc(k_mm, 1)
                    m = due(T_V, t)
                    if m is not None:
                        n = NB * L + m
                        if n:
                            pe.wait_ge(xt_ev, n)
                        if (c := NB * L + issued(T_MX, t)):
                            pe.wait_ge(negm_ev, c)
                        if (c := NB * L + issued(T_OUT, t)):
                            pe.wait_ge(x_new, c)
                        if (c := NB * L + issued(T_XT, t)):
                            pe.wait_ge(post_ev, c)
                        if L and m == 0:
                            pe.wait_ge(ffn_out, 4)
                        for a in range(2):
                            ins = mm(ps[:, BB, P * a:P * a + P], ctxT[:, n % 2, P * a:P * a + P], w_at[:, L, 2, :],
                                     start=True, stop=True)
                        ins.then_inc(v_mm, 1)
                    m = due(T_X, t)
                    if m is not None:
                        n = NB * L + m
                        pe.wait_ge(pre_n, 2 * (n + 1))
                        pe.wait_ge(v_ev, n + 1)
                        if (c := NB * L + issued(T_O2, t)):
                            pe.wait_ge(onT_ev, c)
                        if (c := NB * L + issued(T_OUT, t)):
                            pe.wait_ge(x_new, c)
                        if (c := NB * L + issued(T_XT, t)):
                            pe.wait_ge(post_ev, c)
                        for a in range(2):
                            ins = pe.transpose(ps[:, BB, P * a:P * a + P], xn[:, n % 2, a, :], ident[:, :])
                        ins.then_inc(xt_mm, 1)
                    m = due(T_Q, t)
                    if m is not None:
                        n = NB * L + m
                        pe.wait_ge(xt_ev, n + 1)
                        pe.wait_ge(k_ev, n + 1)
                        if (c := NB * L + issued(T_O1, t)):
                            pe.wait_ge(on_done, c)
                        ins = mm(ps[:, BA, 0:S], w_at[:, L, 0, :], pre_T[:, n % 2, :], start=True, stop=True)
                        if L == 0:
                            ins = mm(ps[:, BA, S:2 * S], w_sw[:, 0, :], pre_T[:, n % 2, :], start=True, stop=True)
                        ins.then_inc(q_mm, 1)
                    m, k = divmod(t - T_S, 16)
                    if 0 <= m < NB:
                        n = NB * L + m
                        i = H * n + k
                        g, a = k // 2, k % 2
                        if k == 0:
                            if n == 0:
                                pe.wait_ge(in_kp, 64)
                            pe.wait_ge(kp_in[n % 4], 128 * (n // 4 + 1))
                            pe.wait_ge(qs_in[n % 4], 64 * (n // 4 + 1))
                        if i >= 2:
                            pe.wait_ge(s_max, i - 1)
                        mm(ps[:, ps_s[i % 2], :], QS[0:96, n % 4, g, P * a:P * a + P],
                           KP[0:96, n % 4, g, :, :].rearrange("p j k -> p (j k)"), start=True, stop=True).then_inc(s_mm, 1)
                    m = due(T_MX, t)
                    if m is not None:
                        n = NB * L + m
                        pe.wait_ge(s_max, H * (n + 1))
                        pe.wait_ge(xt_ev, NB * L + issued(T_X, t))
                        pe.wait_ge(v_ev, NB * L + issued(T_V, t))
                        if (c := NB * L + issued(T_OUT, t)):
                            pe.wait_ge(x_new, c)
                        if (c := NB * L + issued(T_O2, t)):
                            pe.wait_ge(onT_ev, c)
                        if (c := NB * L + issued(T_XT, t)):
                            pe.wait_ge(post_ev, c)
                        for a in range(2):
                            ins = pe.transpose(ps[0:H, BB, P * a:P * a + P], mx[:, n % 2, a, :], ident[:, :])
                        ins.then_inc(mx_t, 1)
                    m, k = divmod(t, 16)
                    if 0 <= m < NB:
                        n = NB * L + m
                        i = H * n + k
                        half, j, c4, g, h = head_of(k)
                        if k == 0:
                            pe.wait_ge(m_in[n % 4], 16 * (n // 4 + 1))
                        if i >= 3:
                            pe.wait_ge(exp_done, i - 2)
                        for a in range(2):
                            ins = mm(ps[:, ps_st[i % 3], S * a:S * a + S], KP[:, n % 4, g, j, P * a:P * a + P],
                                     QS[:, n % 4, g, :], start=True, stop=True)
                        ins.then_inc(st_mm, 1)
                    m, u = divmod(t - T_AV, 16)
                    if u % 4 == 0 and 0 <= m < NB:
                        n, u = NB * L + m, u // 4
                        pe.wait_ge(exp_done, H * n + 4 * u + 4)
                        if u == 0:
                            pe.wait_ge(v_ev, n + 1)
                            if n:
                                pe.wait_ge(raw_ev, n)
                        for a in range(2):
                            for c4 in range(4):
                                half, j, _, g, h = head_of(4 * u + c4)
                                ins = mm(ps[32 * c4:32 * c4 + 32, AVB, S * half:S * half + S],
                                         VA[:, n % 4, a, 80 * g + 32 * j:80 * g + 32 * j + 32],
                                         Pt[:, u % 2, c4, S * a:S * a + S],
                                         start=(j == 0 and a == 0), stop=(j == 1 and a == 1), skip_group_check=True)
                        ins.then_inc(av_mm, 1)
                    m = due(T_O1, t)
                    if m is not None:
                        n = NB * L + m
                        pe.wait_ge(raw_ev, n + 1)
                        pe.wait_ge(k_ev, NB * L + issued(T_K, t))
                        pe.wait_ge(q_ev, NB * L + issued(T_Q, t))
                        for i in range(4):
                            ins = pe.transpose(ps[:, BA, P * i:P * i + P], raw[:, P * i:P * i + P], ident[:, :])
                        ins.then_inc(o1_t, 1)
                    m = due(T_O2, t)
                    if m is not None:
                        n = NB * L + m
                        pe.wait_ge(on_done, n + 1)
                        pe.wait_ge(xt_ev, NB * L + issued(T_X, t))
                        pe.wait_ge(v_ev, NB * L + issued(T_V, t))
                        pe.wait_ge(negm_ev, NB * L + issued(T_MX, t))
                        if (c := NB * L + issued(T_XT, t)):
                            pe.wait_ge(post_ev, c)
                        for a in range(2):
                            ins = pe.transpose(ps[:, BB, P * a:P * a + P], on[:, a, :], ident[:, :])
                        ins.then_inc(o2_t, 1)
                    m = due(T_OUT, t)
                    if m is not None:
                        n = NB * L + m
                        pe.wait_ge(onT_ev, n + 1)
                        pe.wait_ge(v_ev, NB * L + issued(T_V, t))
                        pe.wait_ge(xt_ev, NB * L + issued(T_X, t))
                        pe.wait_ge(negm_ev, NB * L + issued(T_MX, t))
                        for a in range(2):
                            ins = mm(ps[:, BB, P * a:P * a + P], onT[:, P * a:P * a + P], w_at[:, L, 3, :],
                                     start=True, stop=True)
                        ins.then_inc(out_mm, 1)
                    m = due(T_XT, t)
                    if m is not None:
                        n = NB * L + m
                        pe.wait_ge(post_n, 2 * (n + 1))
                        pe.wait_ge(v_ev, NB * L + issued(T_V, t))
                        pe.wait_ge(xt_ev, NB * L + issued(T_X, t))
                        pe.wait_ge(x_new, NB * L + issued(T_OUT, t))
                        pe.wait_ge(negm_ev, NB * L + issued(T_MX, t))
                        pe.wait_ge(onT_ev, NB * L + issued(T_O2, t))
                        for a in range(2):
                            ins = pe.transpose(ps[:, BB, P * a:P * a + P], post_rows(n, a), ident[:, :])
                        ins.then_inc(post_t, 1)
                if L == 0:
                    spread_max(2)
                    for c in range(4):
                        for f in range(FT):
                            i = 4 * c + f
                            if f == 0:
                                pe.wait_ge(xq_b, c + 1)
                            if i >= 2:
                                pe.wait_ge(gelu, i - 1)
                            mm(ps[:, ps_st[i % 2], :], w1q[:, P * f:P * f + P], xq[:, 512 * c:512 * c + 512],
                               start=True, stop=True).then_inc(f1_mm, 1)
                    spread_max(3)
                    for c in range(4):
                        pe.wait_ge(hq_b, FT * (c + 1))
                        if c >= 2:
                            pe.wait_ge(ffn_out, c - 1)
                        for a in range(4):
                            for f in range(FT):
                                ins = mm(ps[:, ps_s[c % 2], P * a:P * a + P], hq[:, f, c % 2, P * a:P * a + P],
                                         w2q[:, f, :], start=(f == 0), stop=(f == FT - 1))
                        ins.then_inc(f2_mm, 1)

            pe.wait_ge(post_ev, 2 * NB)
            for i in range(TILES):
                ins = mm(ps[:, BA, E * i:E * i + E], xT[:, P * i:P * i + P], gw[:, :], start=True, stop=True)
            ins.then_inc(r_mm, 1)
            pe.wait_ge(in_tab, 64)
            pe.wait_ge(r_sel, 1)
            mm(ps[:, BB, 0:P], tri[:, 0, :], selh, start=True, stop=True)
            mm(ps[:, BB, P:2 * P], tri[:, 1, :], selh, start=True, stop=True).then_inc(r_pre, 1)
            pe.wait_ge(e_lo, NE)
            pe.wait_ge(x2lo, 4)
            pe.wait_ge(in_wd, 16)
            e = E
            i = 0
            for q in range(5):
                if q < 4:
                    c = q
                    for f, (f0, fn) in enumerate(FTE):
                        for gu, s_in, s_free in ((0, g_mm, silu), (1, u_mm, h_done)):
                            if i >= 2:
                                pe.wait_ge(s_free, i - 1)
                            bank = 2 * gu + i % 2
                            w0 = FE * gu + f0
                            cols = slice(512 * c, 512 * c + 512)
                            mm(ps[0:fn, bank, :], whi[:, e, w0:w0 + fn], xhi[:, cols], start=True, stop=False)
                            mm(ps[0:fn, bank, :], whi[:, e, w0:w0 + fn], xlo[:, cols], start=False, stop=False)
                            mm(ps[0:fn, bank, :], wlo[:, e, w0:w0 + fn], xhi[:, cols],
                               start=False, stop=True).then_inc(s_in, 1)
                        i += 1
                if q >= 1:
                    p = q - 1
                    pe.wait_ge(h_done, 3 * (p + 1))
                    if p >= 2:
                        pe.wait_ge(acc, p - 1)
                    for a in range(4):
                        for f, (f0, fn) in enumerate(FTE):
                            ins = mm(ps[:, 4 + p % 2, P * a:P * a + P], hh[0:fn, p % 2, f, P * a:P * a + P],
                                     wd[0:fn, e, f, :], start=(f == 0), stop=(f == 2))
                    ins.then_inc(d_mm, 1)
            pe.wait_ge(acc, 4)
            pe.wait_ge(r_exp, 1)
            expert = {}
            wd_flat = wd.rearrange("p e f d -> p (e f d)")
            whi_flat = whi[:, :, :].rearrange("p e f -> p (e f)")
            wlo_flat = wlo[:, :, :].rearrange("p e f -> p (e f)")

            def a_step(i):
                pe.wait_ge(row_in[i % RING], 16 * (i // RING + 1))
                if i >= 2:
                    pe.wait_ge(a_lo, i - 1)
                pe.transpose(ps[:, 6 + i % 2, 0:P], rows[:, i % RING, 2:ROW], ident[:, :]).then_inc(a_t, 1)

            def b_step(i):
                expert[i] = e = pe.value_load(exu[0:1, i:i + 1], min_val=0, max_val=E - 1)
                pe.wait_ge(a_hi, i + 1)
                if i >= 2:
                    pe.wait_ge(b_h, i - 1)
                g, u = ps[:, 2 * (i % 2), 0:FE], ps[:, 2 * (i % 2) + 1, 0:FE]
                off = e * (2 * FE)
                mm(g, xh[:, i % 2, :], whi_flat[:, bass.ds(off, FE)], start=True, stop=False)
                mm(g, xh[:, i % 2, :], wlo_flat[:, bass.ds(off, FE)], start=False, stop=False)
                mm(u, xh[:, i % 2, :], whi_flat[:, bass.ds(off + FE, FE)], start=True, stop=False)
                mm(u, xh[:, i % 2, :], wlo_flat[:, bass.ds(off + FE, FE)], start=False, stop=False)
                pe.wait_ge(a_lo, i + 1)
                mm(g, xl[:, i % 2, :], whi_flat[:, bass.ds(off, FE)], start=False, stop=True)
                mm(u, xl[:, i % 2, :], whi_flat[:, bass.ds(off + FE, FE)], start=False, stop=True).then_inc(b_mm, 1)

            def c_step(i):
                pe.wait_ge(b_h, i + 1)
                if i >= 1:
                    pe.wait_ge(c_ev, i)
                for f, (f0, fn) in enumerate(FTE):
                    ins = pe.transpose(ps[0:fn, 4, P * f:P * f + P], ht[:, i % 2, f0:f0 + fn], ident[:, :])
                ins.then_inc(c_t, 1)

            def d_step(i):
                pe.wait_ge(c_ev, i + 1)
                if i >= 1:
                    pe.wait_ge(d2_ev, i)
                off = expert[i] * (3 * D)
                for f, (f0, fn) in enumerate(FTE):
                    ins = mm(ps[:, 5, 0:D], hT[0:fn, i % 2, f, :], wd_flat[0:fn, bass.ds(off + f * D, D)],
                             start=(f == 0), stop=(f == 2))
                ins.then_inc(d2_mm, 1)

            a_step(0)
            for i in range(SLOTS + 2):
                if i + 1 < SLOTS:
                    a_step(i + 1)
                if i < SLOTS:
                    b_step(i)
                if 1 <= i <= SLOTS:
                    c_step(i - 1)
                if i >= 2:
                    d_step(i - 2)

        @block.scalar
        def _(act):
            A = nc.scalar.activation

            def split_expert(e):
                act.wait_ge(in_e[e % 2], 16 * (e // 2 + 1))
                A(whi[:, e, :], wst[:, e % 2, :], ACT.Identity).then_inc(e_hi, 1)

            act.wait_ge(in_w, ALL_W)
            for L in range(2):
                for t in range(T_FIRST, T_LAST + 1):
                    m = due(A_K, t)
                    if m is not None:
                        n = NB * L + m
                        act.wait_ge(k_mm, n + 1)
                        if n >= 2:
                            act.wait_ge(k_lo, n - 1)
                        if L == 0:
                            A(kf[:, n % 2, :], ps[:, BA, 0:S], ACT.Identity, bias=b_at[:, L, 1:2])
                            A(rot[:, n % 2, :], ps[:, BA, S:2 * S], ACT.Identity, bias=b_sw[:, 1:2]).then_inc(k_ev, 1)
                        else:
                            A(kf[:, n % 2, :], ps[:, BA, 0:S], ACT.Identity, bias=b_at[:, L, 1:2]).then_inc(k_ev, 1)
                    m = due(A_X, t)
                    if m is not None:
                        n = NB * L + m
                        act.wait_ge(xt_mm, n + 1)
                        if n >= 2:
                            act.wait_ge(q_mm, n - 1)
                        A(pre_T[:, n % 2, :], ps[:, BB, 0:S], ACT.Copy).then_inc(xt_ev, 1)
                    m = due(A_Q, t)
                    if m is not None:
                        n = NB * L + m
                        act.wait_ge(q_mm, n + 1)
                        if n >= 2:
                            act.wait_ge(q_lo, n - 1)
                        if L == 0:
                            A(qf[:, n % 2, :], ps[:, BA, 0:S], ACT.Identity, bias=b_at[:, L, 0:1])
                            A(rotq[:, n % 2, :], ps[:, BA, S:2 * S], ACT.Identity, bias=b_sw[:, 0:1]).then_inc(q_ev, 1)
                        else:
                            A(qf[:, n % 2, :], ps[:, BA, 0:S], ACT.Identity, bias=b_at[:, L, 0:1]).then_inc(q_ev, 1)
                    m = due(A_KHI, t)
                    if m is not None:
                        n = NB * L + m
                        if L == 0:
                            act.wait_ge(k_rot, 3 * n + 3)
                        else:
                            act.wait_ge(k_ev, n + 1)
                        if n >= 2:
                            act.wait_ge(kp_in[(n - 2) % 4], 128 * ((n - 2) // 4 + 1))
                        A(khi[:, n % 2, :], kf[:, n % 2, :], ACT.Copy).then_inc(k_hi, 1)
                    m = due(A_QHI, t)
                    if m is not None:
                        n = NB * L + m
                        if L == 0:
                            act.wait_ge(q_rot, 3 * n + 3)
                        else:
                            act.wait_ge(q_ev, n + 1)
                        if n >= 2:
                            act.wait_ge(qs_in[(n - 2) % 4], 64 * ((n - 2) // 4 + 1))
                        A(qhi[:, n % 2, :], qf[:, n % 2, :], ACT.Copy).then_inc(q_hi, 1)
                    m = due(A_MX, t)
                    if m is not None:
                        n = NB * L + m
                        act.wait_ge(mx_t, n + 1)
                        if n >= 2:
                            act.wait_ge(m_in[(n - 2) % 4], 16 * ((n - 2) // 4 + 1))
                        A(negm[:, n % 2, :], ps[0:H, BB, 0:S], ACT.Copy, scale=-1.0 / MAXROW).then_inc(negm_ev, 1)
                    m, k = divmod(t, 16)
                    if 0 <= m < NB:
                        n = NB * L + m
                        i = H * n + k
                        act.wait_ge(st_mm, i + 1)
                        if k % 4 == 0 and i >= 8:
                            act.wait_ge(av_mm, i // 4 - 1)
                        A(Pt[:, (i // 4) % 2, i % 4, :], ps[:, ps_st[i % 3], :], ACT.Exp, scale=SM_SCALE)\
                            .then_inc(exp_done, 1)
                    m = due(A_RAW, t)
                    if m is not None:
                        n = NB * L + m
                        act.wait_ge(av_mm, 4 * (n + 1))
                        if n:
                            act.wait_ge(o1_t, n)
                        A(raw[:, :], ps[:, AVB, :], ACT.Copy).then_inc(raw_ev, 1)
                    m = due(A_O2, t)
                    if m is not None:
                        n = NB * L + m
                        act.wait_ge(o2_t, n + 1)
                        if n:
                            act.wait_ge(out_mm, n)
                        A(onT[:, :], ps[:, BB, 0:S], ACT.Copy).then_inc(onT_ev, 1)
                        if n < NE:
                            split_expert(n)
                    m = due(A_XT, t)
                    if m is not None:
                        n = NB * L + m
                        act.wait_ge(post_t, n + 1)
                        if n == NB:
                            act.wait_ge(xq_a, 4)
                        A(xT[:, S * m:S * m + S], ps[:, BB, 0:S], ACT.Copy).then_inc(post_ev, 1)
                if L == 0:
                    act.wait_ge(f_sc, 1)
                    for i in range(16):
                        c, f = divmod(i, 4)
                        act.wait_ge(f1_mm, i + 1)
                        A(hb[:, f, 512 * c:512 * c + 512], ps[:, ps_st[i % 2], :], ACT.Gelu,
                          bias=b1s[:, f:f + 1], scale=sc[:, 3:4]).then_inc(gelu, 1)
                    act.wait_ge(gm_s, 4)
                    for c in range(4):
                        for f in range(FT):
                            A(hb[:, f, 512 * c:512 * c + 512], hb[:, f, 512 * c:512 * c + 512], ACT.Copy,
                              scale=sc[:, 6:7], bias=ROUND).then_inc(hq_a, 1)

            act.wait_ge(post_ev, 2 * NB)
            act.wait_ge(st_mm, 2 * NB * H)
            for c in range(4):
                A(xhi[:, 512 * c:512 * c + 512], xT[:, 512 * c:512 * c + 512], ACT.Copy).then_inc(x2hi, 1)
            act.wait_ge(rt, 3)
            A(pr[:, :, :], lg[:, :, :], ACT.Exp).then_inc(rt, 1)
            i = 0
            for q in range(4):
                for f, (f0, fn) in enumerate(FTE):
                    act.wait_ge(g_mm, i + 1)
                    if i >= 2:
                        act.wait_ge(h_done, i - 1)
                    A(sg[0:fn, i % 2, :], ps[0:fn, i % 2, :], ACT.Silu).then_inc(silu, 1)
                    i += 1
            act.wait_ge(h_done, 12)

            def hi(i):
                act.wait_ge(a_t, i + 1)
                if i >= 2:
                    act.wait_ge(b_mm, i - 1)
                A(xh[:, i % 2, :], ps[:, 6 + i % 2, 0:P], ACT.Copy).then_inc(a_hi, 1)

            hi(0)
            for i in range(SLOTS + 2):
                if i + 1 < SLOTS:
                    hi(i + 1)
                if i < SLOTS:
                    act.wait_ge(b_mm, i + 1)
                    A(sg[:, i % 2, 0:FE], ps[:, 2 * (i % 2), 0:FE], ACT.Silu).then_inc(b_silu, 1)
                if 1 <= i <= SLOTS:
                    act.wait_ge(c_t, i)
                    if i >= 3:
                        act.wait_ge(d2_mm, i - 2)
                    A(hT[:, (i - 1) % 2, 0:2, :], ps[:, 4, 0:2 * P].rearrange("p (f t) -> p f t", f=2), ACT.Copy)
                    A(hT[0:96, (i - 1) % 2, 2, :], ps[0:96, 4, 2 * P:3 * P], ACT.Copy).then_inc(c_ev, 1)

        @block.vector
        def _(dve):
            V = nc.vector

            def norm_stats(n, src, st, mv_, s_st, s_mv, s_n):
                if n >= 2:
                    dve.wait_ge(s_n, 2 * (n - 1))
                for a in range(2):
                    V.bn_stats(st[:, n % 2, a, :], src(a)).then_inc(s_st, 1)
                for a in range(2):
                    dve.wait_ge(s_st, 2 * n + a + 1)
                    V.bn_aggr(mv_[:, n % 2, a, :], st[:, n % 2, a, :]).then_inc(s_mv, 1)

            def norm_rows(n, src, dst, mv_, r, s_rs, s_n):
                dve.wait_ge(s_rs, n + 1)
                for a in range(2):
                    V.tensor_scalar(dst(n, a), src(a), mv_[:, n % 2, a, 0:1], r[:, n % 2, a:a + 1],
                                    ALU.subtract, ALU.mult).then_inc(s_n, 1)

            def global_max(i):
                dve.wait_ge(gm_t, i + 1)
                V.tensor_reduce(g1[0:1, 4 + i:5 + i], ps[0:1, BA, 0:P], AX.X, ALU.max).then_inc(gm_b, 1)
                dve.wait_ge(gm_bc, i + 1)
                V.tensor_scalar(sc[:, 8 + i:9 + i], ps[:, BA, P:P + 1], MIN_RANGE, None, ALU.max).then_inc(gm_s, 1)
                dve.wait_ge(gm_s, i + 1)

            chain = [0]

            def step(ins):
                chain[0] += 1
                ins.then_inc(w_abs, 1)
                dve.wait_ge(w_abs, chain[0])

            V.memset(QS[:, :, :, :].rearrange("p b g t -> p (b g t)").bitcast(U32), 0).then_inc(zero_done, 1)
            V.memset(KP[:, :, :, :, :].rearrange("p b g j t -> p (b g j t)").bitcast(U32), 0).then_inc(zero_done, 1)
            dve.wait_ge(in_w, ALL_W)
            for i in range(2):
                V.tensor_reduce(g1[:, i:i + 1], w12[:, FF * i:FF * i + FF], AX.X, ALU.max,
                                apply_absolute_value=True).then_inc(gm_a, 1)
            for i in range(2):
                global_max(i)
                step(V.reciprocal(sc[:, 12 + i:13 + i], sc[:, 8 + i:9 + i]))
                step(V.tensor_scalar(sc[:, 12 + i:13 + i], sc[:, 12 + i:13 + i], QP, None, ALU.mult))
                step(V.tensor_scalar(w12[:, FF * i:FF * i + FF], w12[:, FF * i:FF * i + FF],
                                     sc[:, 12 + i:13 + i], ROUND, ALU.mult, ALU.add))
                dst = w1q[:, :] if i == 0 else w2q[:, :, :].rearrange("p f d -> p (f d)")
                step(V.tensor_scalar(dst, w12[:, FF * i:FF * i + FF], ROUND, None, ALU.subtract))
            dve.wait_ge(in_x, 16)

            for L in range(2):
                for t in range(T_FIRST, T_LAST + 1):
                    m = due(D_STAT, t)
                    if m is not None:
                        n = NB * L + m
                        def src(a, m=m):
                            return x[:, 2 * m + a, :]
                        norm_stats(n, src, st6, mv, pre_st, pre_mv, pre_n)
                    m = due(D_V, t)
                    if m is not None:
                        n = NB * L + m
                        dve.wait_ge(v_mm, n + 1)
                        if n == 0:
                            dve.wait_ge(memset_done, 5)
                        if n >= 4:
                            dve.wait_ge(av_mm, 4 * (n - 3))
                        for a in range(2):
                            ins = V.tensor_tensor(
                                VA[:, n % 4, a, :].rearrange("p (g j w) -> p g j w", g=G, j=2)[:, :, :, 0:HD],
                                ps[:, BB, P * a:P * a + P].rearrange("p (g j d) -> p g j d", g=G, j=2),
                                bv[:, L, :].rearrange("p (g j d) -> p g j d", g=G, j=2), ALU.add)
                        ins.then_inc(v_ev, 1)
                    m = due(D_NORM, t)
                    if m is not None:
                        n = NB * L + m
                        if n >= 2:
                            dve.wait_ge(xt_mm, n - 1)
                        def src(a, m=m):
                            return x[:, 2 * m + a, :]
                        norm_rows(n, src, lambda n, a: xn[:, n % 2, a, :], mv, rs, pre_rs, pre_n)
                    m, k = divmod(t - T_S, 16)
                    if 0 <= m < NB:
                        n = NB * L + m
                        i = H * n + k
                        g, a = k // 2, k % 2
                        dve.wait_ge(s_mm, i + 1)
                        if k == 0 and n >= 2:
                            dve.wait_ge(mx_t, n - 1)
                        V.tensor_reduce(mx[:, n % 2, a, g:H:G], ps[:, ps_s[i % 2], :].rearrange("p (j k) -> p j k", j=2),
                                        AX.X, ALU.max).then_inc(s_max, 1)
                    m = due(D_O1, t)
                    if m is not None:
                        n = NB * L + m
                        dve.wait_ge(o1_t, n + 1)
                        o = ps[:, BA, :].rearrange("p (u w) -> p u w", w=32)
                        V.reciprocal(rsum[:, :].rearrange("p (u j) -> p u j", j=2), o[:, :, 16:18]).then_inc(rsum_done, 1)
                        dve.wait_ge(rsum_done, n + 1)
                        if n:
                            dve.wait_ge(o2_t, n)
                        for half in range(2):
                            for a in range(2):
                                q0 = 2 * half + a
                                ins = V.tensor_tensor(
                                    on[:, a, 64 * half:64 * half + 64].rearrange("p (c j d) -> p c j d", c=4, j=2),
                                    ps[:, BA, P * q0:P * q0 + P].rearrange("p (c w) -> p c w", c=4)[:, :, 0:16]
                                        .rearrange("p c (j d) -> p c j d", j=2),
                                    rsum[:, 8 * q0:8 * q0 + 8].rearrange("p (c j) -> p c j", j=2).unsqueeze(3)
                                        .to_broadcast([P, 4, 2, HD]), ALU.mult)
                        ins.then_inc(on_done, 1)
                    m = due(D_OUT, t)
                    if m is not None:
                        n = NB * L + m
                        dve.wait_ge(out_mm, n + 1)
                        dve.wait_ge(xb_done, n + 1)
                        V.tensor_tensor(x[:, 2 * m:2 * m + 2, :], ps[:, BB, 0:S].rearrange("p (a d) -> p a d", a=2),
                                        xb[:, n % 2, :, :], ALU.add).then_inc(x_new, 1)
                        dve.wait_ge(x_new, n + 1)
                        def src(a, m=m):
                            return x[:, 2 * m + a, :]
                        norm_stats(n, src, st6p, mvp, post_st, post_mv, post_n)
                    m = due(D_POST, t)
                    if m is not None:
                        n = NB * L + m
                        if n >= 2:
                            dve.wait_ge(post_t, n - 1)
                            if n <= NB + 1:
                                dve.wait_ge(amax_done, min(n - 1, NB))
                        if n == NB:
                            dve.wait_ge(f2_mm, 4)
                        def src(a, m=m):
                            return x[:, 2 * m + a, :]
                        norm_rows(n, src, post_rows, mvp, rsp, post_rs, post_n)
                        if L == 0:
                            dve.wait_ge(post_n, 2 * (n + 1))
                            V.tensor_reduce(amax[:, m:m + 1], xp[:, n % 2, :, :].rearrange("p a d -> p (a d)"), AX.X, ALU.max,
                                            apply_absolute_value=True).then_inc(amax_done, 1)
                if L == 0:
                    dve.wait_ge(amax_done, NB)
                    V.tensor_reduce(g1[:, 2:3], amax[:, 0:NB], AX.X, ALU.max).then_inc(gm_a, 1)
                    global_max(2)
                    step(V.reciprocal(sc[:, 2:3], sc[:, 10:11]))
                    step(V.tensor_scalar(sc[:, 2:3], sc[:, 2:3], QP, None, ALU.mult))
                    for c in range(4):
                        if c == 0:
                            dve.wait_ge(post_ev, NB)
                        V.tensor_scalar(xT[:, 512 * c:512 * c + 512], xT[:, 512 * c:512 * c + 512], sc[:, 2:3], ROUND,
                                        ALU.mult, ALU.add).then_inc(xq_a, 1)
                        dve.wait_ge(xq_a, c + 1)
                        V.tensor_scalar(xq[:, 512 * c:512 * c + 512], xT[:, 512 * c:512 * c + 512], ROUND, None,
                                        ALU.subtract).then_inc(xq_b, 1)
                        if c == 0:
                            step(V.tensor_scalar(sc[:, 0:1], sc[:, 8:9], 1.0 / QP, None, ALU.mult))
                            step(V.tensor_scalar(sc[:, 1:2], sc[:, 10:11], 1.0 / QP, sc[:, 0:1], ALU.mult, ALU.mult))
                            step(V.tensor_copy(sc[:, 3:4], sc[:, 1:2]))
                            V.tensor_scalar(b1s[:, :], b1[:, :], sc[:, 3:4], None, ALU.mult).then_inc(f_sc, 1)
                    for i in range(16):
                        c, f = divmod(i, 4)
                        dve.wait_ge(gelu, i + 1)
                        if i == 0:
                            pass
                        V.tensor_reduce(amax[:, i:i + 1], hb[:, f, 512 * c:512 * c + 512], AX.X, ALU.max,
                                        apply_absolute_value=True).then_inc(habs, 1)
                    dve.wait_ge(habs, 16)
                    V.tensor_reduce(g1[:, 3:4], amax[:, 0:16], AX.X, ALU.max).then_inc(gm_a, 1)
                    dve.wait_ge(gm_t, 4)
                    V.tensor_reduce(g1[0:1, 7:8], ps[0:1, BA, 0:P], AX.X, ALU.max).then_inc(gm_b, 1)
                    dve.wait_ge(gm_bc, 4)
                    step(V.tensor_scalar(sc[:, 11:12], ps[:, BA, P:P + 1], MIN_RANGE, None, ALU.max))
                    step(V.reciprocal(sc[:, 5:6], sc[:, 11:12]))
                    V.tensor_scalar(sc[:, 6:7], sc[:, 5:6], QP, None, ALU.mult).then_inc(gm_s, 1)
                    step(V.tensor_scalar(sc[:, 4:5], sc[:, 9:10], 1.0 / QP, None, ALU.mult))
                    step(V.tensor_scalar(sc[:, 7:8], sc[:, 11:12], 1.0 / QP, sc[:, 4:5], ALU.mult, ALU.mult))
                    for c in range(5):
                        if c < 4:
                            for f in range(FT):
                                dve.wait_ge(hq_a, FT * c + f + 1)
                                if f == 0 and c >= 2:
                                    dve.wait_ge(f2_mm, c - 1)
                                V.tensor_scalar(hq[:, f, c % 2, :], hb[:, f, 512 * c:512 * c + 512], ROUND, None,
                                                ALU.subtract).then_inc(hq_b, 1)
                        if c >= 1:
                            p = c - 1
                            xs = x[:, 4 * p:4 * p + 4, :]
                            dve.wait_ge(f2_mm, p + 1)
                            if p >= 1:
                                dve.wait_ge(ffn_out, p)
                            V.tensor_tensor(sg[:, 0, :].rearrange("p (a d) -> p a d", a=4),
                                            ps[:, ps_s[p % 2], :].rearrange("p (a d) -> p a d", a=4),
                                            b2[:, :].unsqueeze(1).to_broadcast([P, 4, D]), ALU.add).then_inc(f2_ev, 1)
                            dve.wait_ge(f2_ev, p + 1)
                            V.scalar_tensor_tensor(out=xs, in0=sg[:, 0, :].rearrange("p (a d) -> p a d", a=4),
                                                   scalar=sc[:, 7:8], in1=xs, op0=ALU.mult, op1=ALU.add).then_inc(ffn_out, 1)
                            if p == 3:
                                dve.wait_ge(ffn_out, 4)

            for c in range(4):
                dve.wait_ge(x2hi, c + 1)
                V.tensor_tensor(xlo[:, 512 * c:512 * c + 512], xT[:, 512 * c:512 * c + 512],
                                xhi[:, 512 * c:512 * c + 512], ALU.subtract).then_inc(x2lo, 1)
            bc = [P, TILES, E]
            dve.wait_ge(r_mm, 1)
            V.tensor_copy(lg[:, :, :], ps[:, BA, 0:TILES * E].rearrange("p (t e) -> p t e", e=E)).then_inc(rt, 1)
            dve.wait_ge(rt, 1)
            V.tensor_reduce(r1[:, :], lg[:, :, :], AX.X, ALU.max).then_inc(rt, 1)
            dve.wait_ge(rt, 2)
            V.tensor_tensor(lg[:, :, :], lg[:, :, :], r1[:, :].unsqueeze(2).to_broadcast(bc), ALU.subtract).then_inc(rt, 1)
            dve.wait_ge(rt, 4)
            step(V.tensor_reduce(r1[:, :], pr[:, :, :], AX.X, ALU.add))
            step(V.reciprocal(r2[:, :], r1[:, :]))
            step(V.tensor_tensor(pr[:, :, :], pr[:, :, :], r2[:, :].unsqueeze(2).to_broadcast(bc), ALU.mult))
            for i in range(TILES):
                step(V.max(t8[:, i, :], pr[:, i, :])) if i == TILES - 1 else V.max(t8[:, i, :], pr[:, i, :])
            for i in range(TILES):
                ins = V.max_index(i8[:, i, :], t8[:, i, :], pr[:, i, :])
            step(ins)
            step(V.tensor_copy(i8f, i8[:, :, 0:2]))
            dve.wait_ge(in_tab, 64)
            for k in range(2):
                ins = V.tensor_tensor(oh[:, k, :, :], iota[:, :, :], i8f[:, :, k].unsqueeze(2).to_broadcast(bc), ALU.is_equal)
            step(ins)
            V.tensor_tensor(selh.rearrange("p (t e) -> p t e", e=E), oh[:, 0, :, :], oh[:, 1, :, :], ALU.add).then_inc(r_sel, 1)
            step(V.tensor_tensor(r1, t8[:, :, 0], t8[:, :, 1], ALU.add))
            step(V.tensor_scalar(r1, r1, 1e-20, None, ALU.add))
            step(V.reciprocal(r2, r1))
            for k in range(2):
                V.tensor_tensor(XR[:, k, :, 1], t8[:, :, k], r2, ALU.mult)
                ins = V.tensor_copy(XR[:, k, :, 0], tokd[:, k, :])
            step(ins)
            dve.wait_ge(r_pre, 1)
            step(V.tensor_copy(cnt, ps[:, BB, P:2 * P].rearrange("p (t e) -> p t e", e=E)))
            bufs = (cnt, big)
            for n_, sh in enumerate((1, 2, 4, 8)):
                a_, b_ = bufs[n_ % 2], bufs[1 - n_ % 2]
                V.tensor_copy(b_[:, 0:sh, :], a_[:, 0:sh, :])
                step(V.tensor_tensor(b_[:, sh:TILES, :], a_[:, sh:TILES, :], a_[:, 0:TILES - sh, :], ALU.add))
            step(V.tensor_scalar(b_a, cnt[:, TILES - 1, :], 1.0 / P, (P - 1.0) / P - 0.5 + 0.5 / P, ALU.mult, ALU.add))
            step(V.tensor_scalar(b_a, b_a, ROUND, None, ALU.add))
            step(V.tensor_scalar(b_a, b_a, ROUND, float(P), ALU.subtract, ALU.mult))
            src_, dst_ = b_a, b_b
            for sh in (1, 2, 4):
                V.tensor_copy(dst_[:, 0:sh], src_[:, 0:sh])
                step(V.tensor_tensor(dst_[:, sh:E], src_[:, sh:E], src_[:, 0:E - sh], ALU.add))
                src_, dst_ = dst_, (b_c if src_ is b_a else src_)
            ends = src_
            step(V.tensor_tensor(cmp_, tile0[:, :, :], ends.unsqueeze(1).to_broadcast([P, SLOTS, E]), ALU.is_ge))
            step(V.tensor_reduce(exf, cmp_, AX.X, ALU.add))
            V.tensor_scalar(exu, exf, E - 1.0, None, ALU.min).then_inc(r_exp, 1)
            step(V.memset(tot[:, 0:1], 0.0))
            step(V.tensor_copy(tot[:, 1:E], ends[:, 0:E - 1]))
            step(V.tensor_tensor(slot, ps[:, BB, 0:P].rearrange("p (t e) -> p t e", e=E),
                                 tot.unsqueeze(1).to_broadcast(bc), ALU.add))
            step(V.tensor_tensor(slot[:, 1:TILES, :], slot[:, 1:TILES, :], cnt[:, 0:TILES - 1, :], ALU.add))
            for k in range(2):
                step(V.tensor_tensor(tmp, oh[:, k, :, :], slot, ALU.mult))
                step(V.tensor_reduce(r1, tmp, AX.X, ALU.add))
                ins = V.tensor_copy(slot_u[:, k, :], r1)
                if k == 0:
                    step(ins)
            ins.then_inc(r_slot, 1)
            i = 0
            for q in range(5):
                if q < 4:
                    for f, (f0, fn) in enumerate(FTE):
                        dve.wait_ge(silu, i + 1)
                        dve.wait_ge(u_mm, i + 1)
                        if f == 0 and q >= 2:
                            dve.wait_ge(d_mm, q - 1)
                        V.tensor_tensor(hh[0:fn, q % 2, f, :], sg[0:fn, i % 2, :], ps[0:fn, 2 + i % 2, :],
                                        ALU.mult).then_inc(h_done, 1)
                        i += 1
                if q >= 1:
                    c = q - 1
                    dve.wait_ge(d_mm, c + 1)
                    V.tensor_tensor(x[:, 4 * c:4 * c + 4, :], ps[:, 4 + c % 2, :].rearrange("p (a d) -> p a d", a=4),
                                    x[:, 4 * c:4 * c + 4, :], ALU.add).then_inc(acc, 1)

            def lo(i):
                dve.wait_ge(a_hi, i + 1)
                if i >= 2:
                    dve.wait_ge(b_mm, i - 1)
                V.tensor_tensor(xl[:, i % 2, :], ps[:, 6 + i % 2, 0:P], xh[:, i % 2, :], ALU.subtract).then_inc(a_lo, 1)
                if i >= RING:
                    dve.wait_ge(back[i % RING], 16 * (i // RING))
                V.tensor_copy(dst_u[:, i % RING:i % RING + 1], rows[:, i % RING, 0:1]).then_inc(d2_idx, 1)

            lo(0)
            for i in range(SLOTS + 2):
                if i + 1 < SLOTS:
                    lo(i + 1)
                if i < SLOTS:
                    dve.wait_ge(b_silu, i + 1)
                    if i >= 2:
                        dve.wait_ge(c_t, i - 1)
                    V.tensor_tensor(ht[:, i % 2, :], sg[:, i % 2, 0:FE], ps[:, 2 * (i % 2) + 1, 0:FE], ALU.mult).then_inc(b_h, 1)
                if i >= 2:
                    p = i - 2
                    dve.wait_ge(d2_mm, p + 1)
                    if p >= RING:
                        dve.wait_ge(back[p % RING], 16 * (p // RING))
                    V.tensor_scalar(yb[:, p % RING, :], ps[:, 5, 0:D], rows[:, p % RING, 1:2], None, ALU.mult).then_inc(d2_ev, 1)
            for c in range(4):
                dve.wait_ge(y_in[c], 16)
                for k in range(2):
                    if k:
                        dve.wait_ge(y_sum, 2 * c + 1)
                    V.tensor_tensor(x[:, 4 * c:4 * c + 4, :], x[:, 4 * c:4 * c + 4, :], ytok[:, 4 * c:4 * c + 4, k, :],
                                    ALU.add).then_inc(y_sum, 1)


def kernel(**inputs):
    import concourse.bacc as _bacc
    from concourse import mybir as _mybir
    from concourse.bass_utils import run_bass_kernel_spmd as _run

    a = {k: np.asarray(v) for k, v in inputs.items()}
    f32 = np.float32

    order = np.array([(2 * g + j) * HD + d for j in range(2) for d in range(HD) for g in range(G)])
    swapped = np.array([(2 * g + j) * HD + (d + HD // 2) % HD for j in range(2) for d in range(HD) for g in range(G)])
    w0 = {k: a[f"L0_xattn_W{k}"].T for k in "qkvo"}
    w1 = {k: a[f"L1_xattn_w{k}"] for k in "qkvo"}
    w_at = np.stack([np.stack([w["q"][:, order], w["k"][:, order], w["v"], w["o"]], 1) for w in (w0, w1)], 1)
    w_sw = np.stack([w0["q"][:, swapped], w0["k"][:, swapped]], 1)
    b = [{k: a[f"L{n}_xattn_b{k}"] for k in "qkvo"} for n in range(2)]
    b_at = np.stack([np.stack([c["q"][order], c["k"][order]], 1) for c in b], 1)
    b_sw = np.stack([b[0]["q"][swapped], b[0]["k"][swapped]], 1)

    inv = (1.0 / 10000.0 ** (np.arange(0, HD, 2, dtype=f32) / f32(HD))).astype(f32)
    ang = np.outer(np.arange(S, dtype=f32), inv).astype(f32)
    dd = np.array([d for _ in range(2) for d in range(HD) for _ in range(G)])
    cos = np.cos(ang)[:, dd % (HD // 2)].T.astype(f32)
    sin = (np.sin(ang)[:, dd % (HD // 2)].T * np.where(dd < HD // 2, -1, 1)[:, None]).astype(f32)
    kp = np.zeros((2, G, 2, S), np.float16)
    kp[0, :, 0] = MAXROW
    kp[1, :, 1] = MAXROW

    gate = np.concatenate([a["L1_ffn_expert_gate"], a["L1_ffn_shared_gate"][None]])
    up = np.concatenate([a["L1_ffn_expert_up"], a["L1_ffn_shared_up"][None]])
    down = np.concatenate([a["L1_ffn_expert_down"], a["L1_ffn_shared_down"][None]])
    wgu = np.concatenate([gate, up], 1).transpose(0, 2, 1)
    wd = np.zeros((P, NE, 3, D), f32)
    for f, (f0, fn) in enumerate(FTE):
        wd[:fn, :, f] = down[:, :, f0:f0 + fn].transpose(2, 0, 1)
    arrays = {
        "x": a["x"],
        "ctxT": a["ctx_1024"].transpose(0, 2, 1),
        "w_at": w_at, "w_sw": w_sw, "b_at": b_at, "b_sw": b_sw,
        "bv": np.stack([c["v"] for c in b]), "bo": np.stack([c["o"] for c in b]),
        "w12": np.concatenate([a["L0_ffn_w1"].T, a["L0_ffn_w2"].T.reshape(FT, P, D).transpose(1, 0, 2).reshape(P, FF)], 1),
        "b1": a["L0_ffn_b1"].reshape(FT, P).T, "b2": a["L0_ffn_b2"],
        "wgu": wgu, "wd": wd, "gw": a["L1_ffn_gate_w"].T,
        "c_ident": np.eye(P, dtype=f32), "c_cos": cos, "c_sin": sin, "c_kp": kp,
        "c_tri": np.stack([np.triu(np.ones((P, P)), 1), np.ones((P, P))], 1).astype(np.float16),
        "c_tile0": np.tile((P * np.arange(SLOTS, dtype=f32))[:, None], (1, E)),
        "c_tokd": (2 * (P * np.arange(TILES)[None, None, :] + np.arange(P)[:, None, None])
                   + np.arange(2)[None, :, None]).astype(f32),
        "c_fill": np.concatenate([2 * NT + np.arange(SLOTS * P, dtype=f32)[:, None],
                                  np.zeros((SLOTS * P, ROW - 1), f32)], 1),
        "c_iota": np.tile(np.arange(E, dtype=f32), (TILES, 1)),
    }
    nc = _bacc.Bacc("TRN2", target_bir_lowering=False, num_devices=1)
    feeds, io = {}, {}
    for name, v in arrays.items():
        v = np.ascontiguousarray(v)
        feeds[f"in_{name}"] = v
        io[name] = nc.dram_tensor(f"in_{name}", v.shape, _mybir.dt.from_np(v.dtype), kind="ExternalInput").ap()
    out = nc.dram_tensor("out_0", (NB, S, D), F32, kind="ExternalOutput").ap()
    layers(nc, io, out)
    r = _run(nc, [feeds], core_ids=[0])
    return r.results[0]["out_0"]
```

```python
from contextlib import ExitStack

import numpy as np

import concourse.bass as bass
from concourse import mybir

F32 = mybir.dt.float32
F16 = mybir.dt.float16
BF16 = mybir.dt.bfloat16
U32 = mybir.dt.uint32
ALU = mybir.AluOpType
ACT = mybir.ActivationFunctionType
AX = mybir.AxisListType

P = 128
NB = 8
S = 256
D = 128
H = 16
HD = D // H
G = H // 2
NT = NB * S
TILES = NT // P
FF = 512
FT = FF // P
E = 8
NE = E + 1
FE = 352
FTE = [(0, 128), (128, 128), (256, 96)]
ROW = D + 2
SLOTS = 2 * NT // P + E - 1
CAP = NT + P
RING = 8
QP = 127.0
MIN_RANGE = 1e-6
LN_EPS = 1e-5
SM_SCALE = float(HD) ** -0.5
MAXROW = 64.0
ROUND = 12582912.0

T_K = -51
T_V = -43
T_X = -41
T_Q = -39
T_S = -22
T_MX = -5
T_AV = 6
T_O1 = 20
T_O2 = 24
T_OUT = 29
T_XT = 35
SP_K = -38
SP_KLO = -35
SP_Q = -25
SP_M = -9
G_PRE = -55
G_KROT = -43
G_KLO = -39
G_QROT = -38
G_QLO = -36
G_XB = 21
G_POST = 27
A_K = -47
A_X = -41
A_Q = -38
A_KHI = -42
A_QHI = -33
A_MX = -5
A_RAW = 17
A_O2 = 24
A_XT = 33
D_STAT = -55
D_V = -43
D_NORM = -45
D_O1 = 20
D_OUT = 29
D_POST = 33
T_R = 39
T_RK = 50
A_XHI = 35
G_XLO = 38
D_R0 = 39
D_R1 = 40
D_R2 = 41
A_R = 46
D_KEY = 41
D_KMAX = 41
D_OH = 42
D_KEY2 = 43
D_KMAX2 = 44
D_R3 = 48
G_SEL = 45
D_RK = 50
G_SLOT = 51
D_R4 = 54
G_SEND = 54
T_SH = 156
A_SH = 165
D_SH = 158
T_F2 = -54
A_F2 = -79
D_F2 = -58
F_SP_K = -45
F_SP_KLO = -29
F_SP_Q = -26
F_SP_M = -9
F_G_PRE = -52
F_G_KROT = -49
F_G_KLO = -47
F_G_QROT = -40
F_G_QLO = -27
F_G_XB = 25
F_A_K = -53
F_A_X = -50
F_A_Q = -42
F_A_KHI = -47
F_A_QHI = -35
F_A_MX = 0
F_D_STAT = -55
F_D_V = -54
F_D_NORM = -52
T_W = 16 * (NB - 1) + T_S + 17
T_FIRST = min(F_D_STAT, F_G_PRE, F_A_K, T_F2, A_F2, D_F2, T_K, SP_K, G_PRE, A_K, D_STAT)
T_LAST = 16 * (NB - 1) + max(T_XT, A_XT, D_POST, G_SEND) + 1


SHARED = [(c, f) for c in (0, 1) for f in range(3)] + [(0, None)] + [(2, f) for f in range(3)] + [(1, None)] \
    + [(3, f) for f in range(3)] + [(2, None), (3, None)]


SECOND = [(0, True), (1, True), (0, False), (2, True), (1, False), (3, True), (2, False), (3, False)]


EARLY = 3


def due_kv(offset, L, t, first=None):
    m, r = divmod(t - offset, 16)
    if L == 0 and first is not None:
        if t == first:
            assert r or m <= 0 or m >= NB + EARLY, "two sequences in one slot"
            return 0
        if m == 0:
            return None
    if r == 0 and (0 <= m < NB + EARLY if L == 0 else EARLY <= m < NB):
        return NB * L + m
    return None


def issued_kv(offset, L, t):
    c = max(0, -((offset - t) // 16))
    return min(NB + EARLY, c) if L == 0 else NB + max(EARLY, min(NB, c))


def shared_at(offset, t):
    j, r = divmod(t - offset, 2)
    return j if r == 0 and 0 <= j < len(SHARED) else None


def shared_left(offset):
    return max(0, -((offset - T_LAST - 1) // 2))


def issued(offset, t, per=1):
    return per * min(NB, max(0, -((offset - t) // 16)))


def due(offset, t, first=None):
    m, r = divmod(t - offset, 16)
    if first is not None:
        if t == first:
            assert r or m <= 0 or m >= NB, "two sequences in one slot"
            return 0
        if m == 0:
            return None
    return m if r == 0 and 0 <= m < NB else None


def head_of(k):
    half, j, c = k // 8, (k // 4) % 2, k % 4
    g = 4 * half + c
    return half, j, c, g, 2 * g + j


def layers(nc, io, out):
    ctx = ExitStack()
    with ctx:
        def sb(name, shape, dt=F32):
            return ctx.enter_context(nc.sbuf_tensor(name, shape, dt))

        def sem(name):
            return ctx.enter_context(nc.semaphore(name))

        ps = ctx.enter_context(nc.psum_tensor("ps", [P, 8, 512], F32))
        ps_st = [0, 1, 2]
        ps_s = [3, 4]
        AVB = 5
        BA = 6
        BB = 7
        MB = 3

        x = sb("x", [P, TILES, D])
        xb = sb("xb", [P, 2, 2, D])
        xn = sb("xn", [P, 2, 2, D])
        xp = sb("xp", [P, 2, 2, D])
        xT = sb("xT", [P, NT])
        pre_T = sb("pre_T", [P, 2, S])
        ctxT = sb("ctxT", [P, 2, S])
        first = sb("first", [P, 6 * D + 2 * S + P + 4])
        second = sb("second", [P, 4 * D + 2 + E + FT])
        w_at = [t[:, 0:4 * D].rearrange("p (i d) -> p i d", i=4) for t in (first, second)]
        w_sw = first[:, 4 * D:6 * D].rearrange("p (i d) -> p i d", i=2)
        c0 = 6 * D
        cos, sin = first[:, c0:c0 + S], first[:, c0 + S:c0 + 2 * S]
        ident = first[:, c0 + 2 * S:c0 + 2 * S + P]
        c0 += 2 * S + P
        b_at = [first[:, c0:c0 + 2], second[:, 4 * D:4 * D + 2]]
        b_sw = first[:, c0 + 2:c0 + 4]
        gw = second[:, 4 * D + 2:4 * D + 2 + E]
        b1 = second[:, 4 * D + 2 + E:]
        bv = sb("bv", [P, 2, D])
        bo = sb("bo", [P, 2, D])
        kf = sb("kf", [P, 2, S])
        rot = sb("rot", [P, 2, S])
        khi = sb("khi", [P, 2, S], F16)
        klo = sb("klo", [P, 2, S], F16)
        qf = sb("qf", [P, 2, S])
        rotq = sb("rotq", [P, 2, S])
        qhi = sb("qhi", [P, 2, S], F16)
        qlo = sb("qlo", [P, 2, S], F16)
        QS = sb("QS", [P, 4, G, S], F16)
        KP = sb("KP", [P, 4, G, 2, S], F16)
        VA = sb("VA", [P, 4, 2, G * 80])
        mx = sb("mx", [P, 2, 2, H])
        negm = sb("negm", [H, 2, S], F16)
        Pt = sb("Pt", [P, 2, 4, 512])
        raw = sb("raw", [P, 512])
        rsum = sb("rsum", [P, 4 * 4 * 2])
        on = sb("on", [P, 2, D])
        onT = sb("onT", [P, S])
        st6 = sb("st6", [P, 2, 2, 6])
        mv = sb("mv", [P, 2, 2, 2])
        sd = sb("sd", [P, 2, 2])
        rs = sb("rs", [P, 2, 2])
        st6p = sb("st6p", [P, 2, 2, 6])
        mvp = sb("mvp", [P, 2, 2, 2])
        sdp = sb("sdp", [P, 2, 2])
        rsp = sb("rsp", [P, 2, 2])
        neghalf = sb("neghalf", [P, 2])
        ones = sb("ones", [P, P])
        amax = sb("amax", [P, 16])
        g1 = sb("g1", [P, 8])
        scratch = sb("scratch", [P, 1])
        w1q = sb("w1q", [P, FF], BF16)
        w2q = sb("w2q", [P, FT, D], BF16)
        b1s = sb("b1s", [P, FT])
        b2 = sb("b2", [P, D])
        sc = sb("sc", [P, 16])
        xq = sb("xq", [P, NT], BF16)
        xhi = xq[:, :].bitcast(F16)
        hb = sb("hb", [P, FT, NT])
        hq = Pt[:, 0, :, :].rearrange("p a b -> p (a b)").bitcast(BF16).rearrange("p (f c t) -> p f c t", f=FT, c=2)
        w12 = hb[:, 0, 0:2 * FF]
        wst = sb("wst", [P, 2, 2 * FE])
        xlo = wst[:, :, :].rearrange("p b f -> p (b f)")[:, 0:NT // 2].bitcast(F16)
        whi = sb("whi", [P, NE, 2 * FE], F16)
        wlo = sb("wlo", [P, NE, 2 * FE], F16)
        kp32 = KP[:, :, :, :, :].rearrange("p b g j t -> p (b g j t)").bitcast(F32)
        qs32 = QS[:, :, :, :].rearrange("p b g t -> p (b g t)").bitcast(F32)
        hb32 = hb[:, :, :].rearrange("p f t -> p (f t)")
        wd = kp32[:, 0:NE * 3 * D].rearrange("p (e f d) -> p e f d", e=NE, f=3)
        ytok = kp32[:, 3456:3456 + TILES * 2 * D].rearrange("p (t k d) -> p t k d", t=TILES, k=2)
        xh = kp32[:, 7936:8064].bitcast(F16).rearrange("p (b t) -> p b t", b=2)
        xl = kp32[:, 8064:8192].bitcast(F16).rearrange("p (b t) -> p b t", b=2)
        ht = qs32[:, 2440:2440 + 2 * FE].rearrange("p (b f) -> p b f", b=2)
        hT = qs32[:, 3144:3144 + 6 * P].rearrange("p (b f t) -> p b f t", b=2, f=3)
        rows = hb32[:, 0:RING * ROW].rearrange("p (b c) -> p b c", b=RING)
        yb = hb32[:, RING * ROW:RING * (ROW + D)].rearrange("p (b d) -> p b d", b=RING)
        XR = hb32[:, 0:2 * TILES * ROW].rearrange("p (k t c) -> p k t c", k=2, t=TILES)
        TAB = E + 2 * TILES + 1 + E + SLOTS * E + E * ROW
        tab = hb32[:, 4160:4160 + TAB]
        c0 = 0
        desc = tab[:, 0:E]
        tokd = tab[:, E:E + 2 * TILES].rearrange("p (k t) -> p k t", k=2)
        c0 = E + 2 * TILES
        part = tab[:, c0:c0 + 1]
        base = tab[:, c0 + 1:c0 + 1 + E]
        tile_no = tab[:, c0 + 1 + E:c0 + 1 + E + SLOTS * E].rearrange("p (i e) -> p i e", e=E)
        tail = tab[:, TAB - E * ROW:TAB].rearrange("p (e c) -> p e c", e=E)
        tri = hb32[:, 5568:5696].bitcast(F16).rearrange("p (a c) -> p a c", a=2)
        at = [5696]

        def small(*shape, dt=F32):
            n = int(np.prod(shape))
            n32 = n if dt is not F16 else n // 2
            t = hb32[:, at[0]:at[0] + n32]
            at[0] += n32
            assert at[0] <= FT * NT
            if dt is not F32:
                t = t.bitcast(dt)
            names = "abcd"[:len(shape)]
            return t if len(shape) == 1 else t.rearrange(
                f"p ({' '.join(names)}) -> p {' '.join(names)}", **dict(zip(names, shape)))

        lg = small(NB, 2, 2 * E)
        ex = small(NB, 2, 2 * E)
        eq = small(NB, 4, E)
        key = small(NB, 4, E)
        kmax = small(NB, 4)
        oh = small(NB, 4, E)
        sel = small(NB, 2, E, dt=F16)
        rk = small(NB, 3, E)
        carry = small(NB + 1, E)
        rowe = small(NB, 2, E)
        pick = small(NB, 4, E)
        rowf = small(NB, 4)
        row_u = small(NB, 2, 2, dt=U32)
        zs = small(NB, 2)
        den = small(NB, 2)
        rcp = small(NB, 2)
        tail_u = small(E, dt=U32)
        nt_, ends_a, ends_b, ends_c, step_row = (small(E) for _ in range(5))
        cmp_ = qs32[:, 0:SLOTS * E].rearrange("p (i e) -> p i e", e=E)
        cmr = qs32[:, 512:512 + SLOTS * E].rearrange("p (i e) -> p i e", e=E)
        exf = small(SLOTS)
        exu = small(SLOTS, dt=U32)
        stf = small(SLOTS)
        stu = small(SLOTS, dt=U32)
        dst_u = sb("dst_u", [P, RING], U32)
        sg = Pt[:, :, :, :].rearrange("p a b c -> p (a b c)")[:, 3072:4096].rearrange("p (q t) -> p q t", q=2)
        hh = Pt[:, :, :, :].rearrange("p a b c -> p (a b c)")[:, 0:3072].rearrange("p (q f t) -> p q f t", q=2, f=3)

        in_x = [sem(f"in_x{i}") for i in range(2)]
        in_e = [sem(f"in_e{i}") for i in range(2)]
        in_ctx = [sem(f"in_ctx{i}") for i in range(2)]
        in_first, in_bv, in_second, in_w12, in_wd = (sem(n) for n in ("in_first", "in_bv", "in_second", "in_w12", "in_wd"))
        in_tab, in_kp = (sem(n) for n in ("in_tab", "in_kp"))
        memset_done, zero_done = (sem(n) for n in ("memset_done", "zero_done"))
        pre_st, pre_mv, pre_sd, pre_rs, pre_n = (sem(n) for n in ("pre_st", "pre_mv", "pre_sd", "pre_rs", "pre_n"))
        post_st, post_mv, post_sd, post_rs, post_n = (sem(n) for n in ("post_st", "post_mv", "post_sd", "post_rs", "post_n"))
        k_mm, v_mm, xt_mm, q_mm, k_ev = (sem(n) for n in ("k_mm", "v_mm", "xt_mm", "q_mm", "k_ev"))
        v_ev, xt_ev, q_ev = (sem(n) for n in ("v_ev", "xt_ev", "q_ev"))
        kp_in = [sem(f"kp_in{i}") for i in range(4)]
        qs_in = [sem(f"qs_in{i}") for i in range(4)]
        m_in = [sem(f"m_in{i}") for i in range(4)]
        k_rot, q_rot, k_hi, q_hi, k_lo = (sem(n) for n in ("k_rot", "q_rot", "k_hi", "q_hi", "k_lo"))
        q_lo = sem("q_lo")
        s_mm, s_max, mx_t, negm_ev = (sem(n) for n in ("s_mm", "s_max", "mx_t", "negm_ev"))
        st_mm, exp_done, av_mm, raw_ev = (sem(n) for n in ("st_mm", "exp_done", "av_mm", "raw_ev"))
        o1_t, rsum_done, on_done, o2_t, onT_ev = (sem(n) for n in ("o1_t", "rsum_done", "on_done", "o2_t", "onT_ev"))
        out_mm, xb_done, x_new = (sem(n) for n in ("out_mm", "xb_done", "x_new"))
        post_t, post_ev, amax_done = (sem(n) for n in ("post_t", "post_ev", "amax_done"))
        gm_a, gm_t, gm_b, gm_bc, gm_s = (sem(n) for n in ("gm_a", "gm_t", "gm_b", "gm_bc", "gm_s"))
        v_step, g_step = (sem(n) for n in ("v_step", "g_step"))
        w_q, f_sc, xq_a, xq_b, f1_mm = (sem(n) for n in ("w_q", "f_sc", "xq_a", "xq_b", "f1_mm"))
        gelu, habs = (sem(n) for n in ("gelu", "habs"))
        hq_a, hq_b, f2_mm, x_b2, ffn_out = (sem(n) for n in ("hq_a", "hq_b", "f2_mm", "x_b2", "ffn_out"))
        e_hi, e_lo, x2hi, x2lo = (sem(n) for n in ("e_hi", "e_lo", "x2hi", "x2lo"))
        r_mm, r_ev, r_top, r_eq, r_key = (sem(n) for n in ("r_mm", "r_ev", "r_top", "r_eq", "r_key"))
        r_kmax, r_key2, r_oh = (sem(n) for n in ("r_kmax", "r_key2", "r_oh"))
        r_sub, r_ex, r_zs, r_sel, rk_mm = (sem(n) for n in ("r_sub", "r_ex", "r_zs", "r_sel", "rk_mm"))
        rk_ev, r_carry, r_pick, r_row = (sem(n) for n in ("rk_ev", "r_carry", "r_pick", "r_row"))
        r_tail, r_exp = (sem(n) for n in ("r_tail", "r_exp"))
        xr_copy, filled, sent, tail_sent = (sem(n) for n in ("xr_copy", "filled", "sent", "tail_sent"))
        g_mm, u_mm, silu, h_done, d_mm = (sem(n) for n in ("g_mm", "u_mm", "silu", "h_done", "d_mm"))
        acc = sem("acc")
        row_in = [sem(f"row_in{i}") for i in range(RING)]
        a_t, a_hi, a_lo, b_mm, b_silu = (sem(n) for n in ("a_t", "a_hi", "a_lo", "b_mm", "b_silu"))
        b_h = sem("b_h")
        back = [sem(f"back{i}") for i in range(RING)]
        c_t, c_ev, d2_mm, d2_ev, d2_idx = (sem(n) for n in ("c_t", "c_ev", "d2_mm", "d2_ev", "d2_idx"))
        y_in = [sem(f"y_in{i}") for i in range(4)]
        y_sum, y_sum0, stored = (sem(n) for n in ("y_sum", "y_sum0", "stored"))

        def post_rows(n, a):
            return xp[:, n % 2, a, :] if n < NB else XR[:, 0, 2 * (n - NB) + a, 2:ROW]

        block = ctx.enter_context(nc.Block())

        x_dram = io["x"].rearrange("b (a p) d -> p (b a) d", p=P)
        out_dram = out.rearrange("b (a p) d -> p (b a) d", p=P)

        rows_dram = nc.dram_tensor("rows", [E * CAP + SLOTS * P, ROW], F32).ap()
        y_dram = nc.dram_tensor("y_rows", [2 * NT + (SLOTS + E) * P, D], F32).ap()
        tables = [(tab, io["c_tab"]), (tri, io["c_tri"])]

        @block.sync
        def _(sp):
            sp.dma_start(ctxT[:, 0, :], io["ctxT"][0]).then_inc(in_ctx[0], 16)
            sp.dma_start(first[:, :], io["first"]).then_inc(in_first, 16)
            sp.dma_start(x[:, 0:4, :], x_dram[:, 0:4, :]).then_inc(in_x[0], 16)
            sp.dma_start(bv[:, :, :], io["bv"].partition_broadcast(P)).then_inc(in_bv, 16)
            sp.dma_start(ctxT[:, 1, :], io["ctxT"][1]).then_inc(in_ctx[1], 16)
            sp.dma_start(x[:, 4:, :], x_dram[:, 4:, :]).then_inc(in_x[1], 16)
            sp.wait_ge(zero_done, 4)
            for i in range(4):
                sp.dma_start(KP[96:98, i], io["c_kp"]).then_inc(in_kp, 16)
            def rest():
                sp.dma_start(second[:, :], io["second"]).then_inc(in_second, 16)
                sp.dma_start(bo[:, :, :], io["bo"].partition_broadcast(P)).then_inc(in_second, 16)
                sp.dma_start(b2[:, :], io["b2"].partition_broadcast(P)).then_inc(in_second, 16)
                sp.dma_start(w12, io["w12"]).then_inc(in_w12, 16)
                for e in range(2):
                    sp.dma_start(wst[:, e, :], io["wgu"][e]).then_inc(in_e[e], 16)
                sp.dma_start(rows_dram[E * CAP:, :], io["c_fill"]).then_inc(filled, 16)

            for L in range(2):
                for t in range(T_FIRST, T_LAST + 1):
                    if L == 1 and t == SP_Q + 1:
                        sp.wait_ge(hq_b, 16)
                        for dst, src in tables:
                            sp.dma_start(dst, src).then_inc(in_tab, 16)
                    n = due_kv(SP_K, L, t, F_SP_K)
                    if n is not None:
                        if n + 2 < 2 * NB:
                            sp.wait_ge(k_mm, n + 1)
                            sp.wait_ge(v_mm, n + 1)
                            sp.dma_start(ctxT[:, n % 2, :], io["ctxT"][(n + 2) % NB]).then_inc(in_ctx[n % 2], 16)
                        if n >= 4:
                            sp.wait_ge(st_mm, H * (n - 3))
                        sp.wait_ge(k_hi, n + 1)
                        for r in range(2):
                            for j in range(2):
                                sp.dma_start(KP[16 * r + 8 * j:16 * r + 8 * j + 8, n % 4, :, j, :],
                                             khi[64 * j:64 * j + 64, n % 2, :]).then_inc(kp_in[n % 4], 16)
                    n = due_kv(SP_KLO, L, t, F_SP_KLO)
                    if n is not None:
                        sp.wait_ge(k_lo, n + 1)
                        for r in range(2, 4):
                            for j in range(2):
                                sp.dma_start(KP[16 * r + 8 * j:16 * r + 8 * j + 8, n % 4, :, j, :],
                                             klo[64 * j:64 * j + 64, n % 2, :]).then_inc(kp_in[n % 4], 16)
                    m = due(SP_Q, t, F_SP_Q)
                    if m is not None:
                        n = NB * L + m
                        if n >= 4:
                            sp.wait_ge(st_mm, H * (n - 3))
                        sp.wait_ge(q_hi, n + 1)
                        for r in (0, 2):
                            sp.dma_start(QS[16 * r:16 * r + 16, n % 4, :, :], qhi[:, n % 2, :]).then_inc(qs_in[n % 4], 16)
                        sp.wait_ge(q_lo, n + 1)
                        for r in (1, 3):
                            sp.dma_start(QS[16 * r:16 * r + 16, n % 4, :, :], qlo[:, n % 2, :]).then_inc(qs_in[n % 4], 16)
                        if n == 1:
                            rest()
                    m = due(SP_M, t, F_SP_M)
                    if m is not None:
                        n = NB * L + m
                        sp.wait_ge(negm_ev, n + 1)
                        sp.dma_start(QS[96:98, n % 4, :, :], negm[:, n % 2, :]).then_inc(m_in[n % 4], 16)
                    m = due(T_O1 + 4, t)
                    if m is not None and NB * L + m + 2 < NE:
                        n = NB * L + m
                        sp.wait_ge(e_lo, n + 1)
                        sp.dma_start(wst[:, n % 2, :], io["wgu"][n + 2]).then_inc(in_e[n % 2], 16)
            sp.wait_ge(st_mm, 2 * NB * H)
            sp.wait_ge(s_mm, 2 * NB * H)
            sp.dma_start(wd, io["wd"]).then_inc(in_wd, 16)
            sp.wait_ge(filled, 16)
            sp.wait_ge(r_exp, 1)
            sp.wait_ge(sent, 16 * 2 * TILES)
            sp.wait_ge(tail_sent, 16 * E)
            for i in range(SLOTS):
                if i >= RING:
                    sp.wait_ge(a_t, i - RING + 1)
                    sp.wait_ge(d2_ev, i - RING + 1)
                    sp.wait_ge(d2_idx, i - RING + 1)
                start = sp.value_load(stu[0:1, i:i + 1], min_val=0, max_val=E * CAP + (SLOTS - 1) * P)
                sp.dma_start(rows[:, i % RING, :], rows_dram[bass.ds(start, P), :]).then_inc(row_in[i % RING], 16)
            for b in range(RING):
                sp.wait_ge(back[b], 16 * len(range(b, SLOTS, RING)))
            for c in range(4):
                sp.dma_start(ytok[:, 4 * c:4 * c + 4, :, :], y_dram[0:2 * NT, :].rearrange(
                    "(t p k) d -> p t k d", p=P, k=2)[:, 4 * c:4 * c + 4]).then_inc(y_in[c], 16)
            for c in (1, 0, 2, 3):
                if c:
                    sp.wait_ge(y_sum, 2 * c)
                else:
                    sp.wait_ge(y_sum0, 2)
                sp.dma_start(out_dram[:, 4 * c:4 * c + 4, :], x[:, 4 * c:4 * c + 4, :]).then_inc(stored, 16)
            sp.wait_ge(stored, 64)

        @block.gpsimd
        def _(pool):
            nc.gpsimd.memset(neghalf[:, :], -0.5).then_inc(memset_done, 1)
            nc.gpsimd.memset(ones[:, :], 1.0).then_inc(memset_done, 1)
            nc.gpsimd.memset(VA[:, 0, :, :], 0.0).then_inc(memset_done, 1)
            nc.gpsimd.memset(VA[:, 1:4, :, :], 0.0).then_inc(memset_done, 1)
            va5 = VA[:, :, :, :].rearrange("p b k (g w) -> p (b k) g w", g=G)
            nc.gpsimd.memset(KP[:, 2:4, :, :, :].rearrange("p b g j t -> p (b g j t)").bitcast(U32), 0).then_inc(zero_done, 1)
            pool.wait_ge(memset_done, 4)
            nc.gpsimd.memset(va5[:, :, :, 16:17], 1.0).then_inc(memset_done, 1)
            nc.gpsimd.memset(va5[:, :, :, 49:50], 1.0).then_inc(memset_done, 1)

            def split_expert(e):
                pool.wait_ge(e_hi, e + 1)
                nc.gpsimd.tensor_tensor(wlo[:, e, :], wst[:, e % 2, :], whi[:, e, :], ALU.subtract).then_inc(e_lo, 1)

            def pre_norm(n):
                pool.wait_ge(pre_mv, 2 * (n + 1))
                if n >= 2:
                    pool.wait_ge(pre_n, 2 * (n - 1))
                nc.gpsimd.tensor_scalar(sd[:, n % 2, :], mv[:, n % 2, :, 1], LN_EPS, None, ALU.add).then_inc(pre_sd, 1)
                pool.wait_ge(pre_sd, n + 1)
                nc.gpsimd.tensor_tensor(rs[:, n % 2, :], sd[:, n % 2, :], neghalf[:, :], ALU.pow).then_inc(pre_rs, 1)

            def post_norm(n):
                pool.wait_ge(post_mv, 2 * (n + 1))
                if n >= 2:
                    pool.wait_ge(post_n, 2 * (n - 1))
                nc.gpsimd.tensor_scalar(sdp[:, n % 2, :], mvp[:, n % 2, :, 1], LN_EPS, None, ALU.add).then_inc(post_sd, 1)
                pool.wait_ge(post_sd, n + 1)
                nc.gpsimd.tensor_tensor(rsp[:, n % 2, :], sdp[:, n % 2, :], neghalf[:, :], ALU.pow).then_inc(post_rs, 1)

            GP = nc.gpsimd
            chain = [0]

            def gstep(ins):
                chain[0] += 1
                ins.then_inc(g_step, 1)
                pool.wait_ge(g_step, chain[0])

            pool.wait_ge(in_first, 16)
            for L in range(2):
                if L == 1:
                    pool.wait_ge(in_second, 48)
                    pool.wait_ge(f_sc, 2)
                    pool.wait_ge(post_st, 2 * NB)
                    gstep(GP.tensor_scalar(b2[:, :], b2[:, :], sc[:, 7:8], None, ALU.mult))
                    for c in range(4):
                        xs = x[:, 4 * c:4 * c + 4, :]
                        GP.tensor_tensor(xs, xs, b2[:, :].unsqueeze(1).to_broadcast([P, 4, D]), ALU.add).then_inc(x_b2, 1)
                for t in range(T_FIRST, T_LAST + 1):
                    m = due(G_PRE, t, F_G_PRE)
                    if m is not None:
                        n = NB * L + m
                        pre_norm(n)
                    n = due_kv(G_KROT, L, t, F_G_KROT)
                    if n is not None and n < NB:
                        pool.wait_ge(k_ev, n + 1)
                        nc.gpsimd.tensor_tensor(kf[:, n % 2, :], kf[:, n % 2, :], cos[:, :], ALU.mult).then_inc(k_rot, 1)
                        nc.gpsimd.tensor_tensor(rot[:, n % 2, :], rot[:, n % 2, :], sin[:, :], ALU.mult).then_inc(k_rot, 1)
                        pool.wait_ge(k_rot, 3 * n + 2)
                        nc.gpsimd.tensor_tensor(kf[:, n % 2, :], kf[:, n % 2, :], rot[:, n % 2, :], ALU.add).then_inc(k_rot, 1)
                    n = due_kv(G_KLO, L, t, F_G_KLO)
                    if n is not None:
                        pool.wait_ge(k_hi, n + 1)
                        nc.gpsimd.tensor_tensor(klo[:, n % 2, :], kf[:, n % 2, :], khi[:, n % 2, :], ALU.subtract).then_inc(k_lo, 1)
                    m = due(G_QROT, t, F_G_QROT)
                    if m is not None and L == 0:
                        n = NB * L + m
                        pool.wait_ge(q_ev, n + 1)
                        nc.gpsimd.tensor_tensor(qf[:, n % 2, :], qf[:, n % 2, :], cos[:, :], ALU.mult).then_inc(q_rot, 1)
                        nc.gpsimd.tensor_tensor(rotq[:, n % 2, :], rotq[:, n % 2, :], sin[:, :], ALU.mult).then_inc(q_rot, 1)
                        pool.wait_ge(q_rot, 3 * n + 2)
                        nc.gpsimd.tensor_tensor(qf[:, n % 2, :], qf[:, n % 2, :], rotq[:, n % 2, :], ALU.add).then_inc(q_rot, 1)
                    m = due(G_QLO, t, F_G_QLO)
                    if m is not None:
                        n = NB * L + m
                        pool.wait_ge(q_hi, n + 1)
                        nc.gpsimd.tensor_tensor(qlo[:, n % 2, :], qf[:, n % 2, :], qhi[:, n % 2, :], ALU.subtract).then_inc(q_lo, 1)
                    m = due(G_XB, t, F_G_XB)
                    if m is not None:
                        n = NB * L + m
                        if n == 0:
                            pool.wait_ge(in_second, 48)
                            pool.wait_ge(in_x[0], 16)
                            pool.wait_ge(in_x[1], 16)
                        if n == NB:
                            pool.wait_ge(ffn_out, 4)
                        if n >= 2:
                            pool.wait_ge(x_new, n - 1)
                        for a in range(2):
                            ins = nc.gpsimd.tensor_tensor(xb[:, n % 2, a, :], x[:, 2 * m + a, :], bo[:, L, :], ALU.add)
                        ins.then_inc(xb_done, 1)
                        if n < NE:
                            split_expert(n)
                    m = due(G_POST, t)
                    if m is not None:
                        post_norm(NB * L + m)
                    m = due(T_XT, t)
                    if m is not None and L == 1:
                        pool.wait_ge(post_n, 2 * (NB + m + 1))
                        nc.gpsimd.tensor_scalar(XR[:, 1, 2 * m:2 * m + 2, 2:ROW], XR[:, 0, 2 * m:2 * m + 2, 2:ROW],
                                                1.0, 0.0, ALU.mult, ALU.add).then_inc(xr_copy, 1)
                    m = due(G_XLO, t)
                    if m is not None and L == 1:
                        pool.wait_ge(x2hi, m + 1)
                        if m == 0:
                            pool.wait_ge(e_lo, NE)
                        GP.tensor_tensor(xlo[:, S * m:S * m + S], xT[:, S * m:S * m + S], xhi[:, S * m:S * m + S],
                                         ALU.subtract).then_inc(x2lo, 1)
                    m = due(G_SEL, t)
                    if m is not None and L == 1:
                        if m == 0:
                            pool.wait_ge(in_tab, 32)
                            GP.tensor_scalar(XR[:, :, :, 0], tokd, 1.0, 0.0, ALU.mult, ALU.add)
                            gstep(GP.tensor_scalar(carry[:, 0, :], base, 1.0, 0.0, ALU.mult, ALU.add))
                        pool.wait_ge(r_oh, 2 * m + 2)
                        GP.tensor_tensor(sel[:, m, :, :], oh[:, m, 0:2, :], oh[:, m, 2:4, :], ALU.add).then_inc(r_sel, 1)
                        pool.wait_ge(r_zs, m + 1)
                        gstep(GP.tensor_scalar(den[:, m, :], zs[:, m, :], 1e-20, None, ALU.mult))
                        for k in range(2):
                            gstep(GP.tensor_tensor(den[:, m, :], den[:, m, :], ex[:, m, :, E + k], ALU.add))
                    m = due(G_SLOT, t)
                    if m is not None and L == 1:
                        pool.wait_ge(rk_ev, m + 1)
                        GP.tensor_tensor(carry[:, m + 1, :], carry[:, m, :], rk[:, m, 2, :], ALU.add).then_inc(r_carry, 1)
                        gstep(GP.tensor_tensor(rowe[:, m, :, :], rk[:, m, 0:2, :],
                                               carry[:, m, :].unsqueeze(1).to_broadcast([P, 2, E]), ALU.add))
                        for k in range(2):
                            ins = GP.tensor_tensor(pick[:, m, 2 * k:2 * k + 2, :], oh[:, m, 2 * k:2 * k + 2, :],
                                                   rowe[:, m, :, :], ALU.mult)
                        ins.then_inc(r_pick, 1)
                        if m == NB - 1:
                            pool.wait_ge(r_carry, NB)
                            GP.tensor_scalar(tail_u, carry[:, NB, :], part, None, ALU.add).then_inc(r_tail, 1)
                    m = due(G_SEND, t)
                    if m is not None and L == 1:
                        pool.wait_ge(r_row, m + 1)
                        GP.tensor_scalar(row_u[:, m, :, :].rearrange("p k t -> p (k t)"), rowf[:, m, :], 1.0, 0.0,
                                         ALU.mult, ALU.add)
                        for k in range(2):
                            ins = GP.tensor_tensor(XR[:, k, 2 * m:2 * m + 2, 1], ex[:, m, :, E + k], rcp[:, m, :], ALU.mult)
                        gstep(ins)
                        pool.wait_ge(xr_copy, m + 1)
                        if m == 0:
                            pool.wait_ge(filled, 16)
                        for k in range(2):
                            for a in range(2):
                                pool.indirect_dma_start(
                                    rows_dram, bass.IndirectOffsetOnAxis(ap=row_u[:, m, k, a:a + 1], axis=0),
                                    XR[:, k, 2 * m + a, :], None).then_inc(sent, 16)
            pool.wait_ge(r_tail, 1)
            for e in range(E):
                pool.indirect_dma_start(rows_dram, bass.IndirectOffsetOnAxis(ap=tail_u[:, e:e + 1], axis=0),
                                        tail[:, e, :], None).then_inc(tail_sent, 16)
            for i in range(SLOTS):
                pool.wait_ge(d2_ev, i + 1)
                pool.wait_ge(d2_idx, i + 1)
                pool.indirect_dma_start(y_dram, bass.IndirectOffsetOnAxis(ap=dst_u[:, i % RING:i % RING + 1], axis=0),
                                        yb[:, i % RING, :], None).then_inc(back[i % RING], 16)
            pool.wait_ge(acc, 4)
            pool.wait_ge(y_in[0], 16)
            for k in range(2):
                if k:
                    pool.wait_ge(y_sum0, 1)
                GP.tensor_tensor(x[:, 0:4, :], x[:, 0:4, :], ytok[:, 0:4, k, :], ALU.add).then_inc(y_sum0, 1)
            pool.wait_ge(stored, 64)

        @block.tensor
        def _(pe):
            mm = nc.tensor.matmul

            def transpose_max(r, c0, n):
                pe.wait_ge(gm_a, r + 1)
                if r:
                    pe.wait_ge(gm_s, r)
                for i in range(n):
                    ins = pe.transpose(ps[0:1, MB, P * i:P * i + P], g1[:, c0 + i:c0 + i + 1], ident[:, :])
                ins.then_inc(gm_t, 1)

            def broadcast_max(r, c0, n):
                pe.wait_ge(gm_b, r + 1)
                mm(ps[:, MB, 2 * P:2 * P + n], ones[0:1, :], g1[0:1, 4 + c0:4 + c0 + n], start=True, stop=True).then_inc(gm_bc, 1)

            BANK_A = ((T_K, k_ev), (T_Q, q_ev), (T_O1, on_done), (T_R, r_ev), (T_RK, rk_ev))
            BANK_B = ((T_V, v_ev), (T_X, xt_ev), (T_MX, negm_ev), (T_O2, onT_ev), (T_OUT, x_new), (T_XT, post_ev))

            waited = {read: 0 for _, read in BANK_A + BANK_B}

            def bank_read(users, L, t):
                for offset, read in users:
                    if read in (k_ev, v_ev):
                        c = issued_kv(offset, L, t)
                    elif read in (r_ev, rk_ev):
                        c = issued(offset, t) if L == 1 else 0
                    else:
                        c = NB * L + issued(offset, t)
                    if c > waited[read]:
                        waited[read] = c
                        pe.wait_ge(read, c)

            def shared(c, f):
                e = E
                if f is not None:
                    i = 3 * c + f
                    f0, fn = FTE[f]
                    if i == 0:
                        pe.wait_ge(exp_done, 2 * NB * H)
                        pe.wait_ge(s_max, 2 * NB * H)
                        pe.wait_ge(e_lo, NE)
                    if f == 0:
                        pe.wait_ge(x2lo, 2 * (c + 1))
                    cols = slice(512 * c, 512 * c + 512)
                    for gu, s_in, s_free in ((0, g_mm, silu), (1, u_mm, h_done)):
                        if i >= 2:
                            pe.wait_ge(s_free, i - 1)
                        bank = 2 * gu + i % 2
                        w0 = FE * gu + f0
                        mm(ps[0:fn, bank, :], whi[:, e, w0:w0 + fn], xhi[:, cols], start=True, stop=False)
                        mm(ps[0:fn, bank, :], whi[:, e, w0:w0 + fn], xlo[:, cols], start=False, stop=False)
                        mm(ps[0:fn, bank, :], wlo[:, e, w0:w0 + fn], xhi[:, cols], start=False, stop=True).then_inc(s_in, 1)
                else:
                    pe.wait_ge(h_done, 3 * (c + 1))
                    if c == 0:
                        pe.wait_ge(in_wd, 16)
                    if c == 1:
                        pe.wait_ge(raw_ev, 2 * NB)
                    if c >= 2:
                        pe.wait_ge(acc, c - 1)
                    for a in range(4):
                        for f, (f0, fn) in enumerate(FTE):
                            ins = mm(ps[:, 4 + c % 2, P * a:P * a + P], hh[0:fn, c % 2, f, P * a:P * a + P],
                                     wd[0:fn, e, f, :], start=(f == 0), stop=(f == 2))
                    ins.then_inc(d_mm, 1)

            def second_product(c):
                if c >= 2:
                    pe.wait_ge(ffn_out, c - 1)
                pe.wait_ge(hq_b, FT * (c + 1))
                for a in range(4):
                    for f in range(FT):
                        ins = mm(ps[:, ps_s[c % 2], P * a:P * a + P], hq[:, f, c % 2, P * a:P * a + P],
                                 w2q[:, f, :], start=(f == 0), stop=(f == FT - 1))
                ins.then_inc(f2_mm, 1)

            pe.wait_ge(in_first, 16)

            for L in range(2):
                for t in range(T_FIRST, T_LAST + 1):
                    if L == 1 and 0 <= t - T_F2 < len(SECOND):
                        c, quantise = SECOND[t - T_F2]
                        if not quantise:
                            second_product(c)
                    n = due_kv(T_K, L, t)
                    if n is not None:
                        bank_read(BANK_A, L, t)
                        pe.wait_ge(in_ctx[n % 2], 16 * (n // 2 + 1))
                        if n == NB:
                            pe.wait_ge(in_second, 48)
                        ins = mm(ps[:, BA, 0:S], w_at[n // NB][:, 1, :], ctxT[:, n % 2, :], start=True, stop=True)
                        if n < NB:
                            ins = mm(ps[:, BA, S:2 * S], w_sw[:, 1, :], ctxT[:, n % 2, :], start=True, stop=True)
                        ins.then_inc(k_mm, 1)
                    n = due_kv(T_V, L, t)
                    if n is not None:
                        bank_read(BANK_B, L, t)
                        for a in range(2):
                            ins = mm(ps[:, BB, P * a:P * a + P], ctxT[:, n % 2, P * a:P * a + P], w_at[n // NB][:, 2, :],
                                     start=True, stop=True)
                        ins.then_inc(v_mm, 1)
                    m = due(T_X, t)
                    if m is not None:
                        n = NB * L + m
                        bank_read(BANK_B, L, t)
                        pe.wait_ge(pre_n, 2 * (n + 1))
                        for a in range(2):
                            ins = pe.transpose(ps[:, BB, P * a:P * a + P], xn[:, n % 2, a, :], ident[:, :])
                        ins.then_inc(xt_mm, 1)
                    m = due(T_Q, t)
                    if m is not None:
                        n = NB * L + m
                        bank_read(BANK_A, L, t)
                        pe.wait_ge(xt_ev, n + 1)
                        ins = mm(ps[:, BA, 0:S], w_at[L][:, 0, :], pre_T[:, n % 2, :], start=True, stop=True)
                        if L == 0:
                            ins = mm(ps[:, BA, S:2 * S], w_sw[:, 0, :], pre_T[:, n % 2, :], start=True, stop=True)
                        ins.then_inc(q_mm, 1)
                    m, k = divmod(t - T_S, 16)
                    if 0 <= m < NB:
                        n = NB * L + m
                        i = H * n + k
                        g, a = k // 2, k % 2
                        if k == 0:
                            if n == 0:
                                pe.wait_ge(in_kp, 64)
                            if n == NB:
                                pe.wait_ge(ffn_out, 4)
                            pe.wait_ge(kp_in[n % 4], 128 * (n // 4 + 1))
                            pe.wait_ge(qs_in[n % 4], 64 * (n // 4 + 1))
                        if i >= 2:
                            pe.wait_ge(s_max, i - 1)
                        mm(ps[:, ps_s[i % 2], :], QS[0:96, n % 4, g, P * a:P * a + P],
                           KP[0:96, n % 4, g, :, :].rearrange("p j k -> p (j k)"), start=True, stop=True).then_inc(s_mm, 1)
                    m = due(T_MX, t)
                    if m is not None:
                        n = NB * L + m
                        bank_read(BANK_B, L, t)
                        pe.wait_ge(s_max, H * (n + 1))
                        for a in range(2):
                            ins = pe.transpose(ps[0:H, BB, P * a:P * a + P], mx[:, n % 2, a, :], ident[:, :])
                        ins.then_inc(mx_t, 1)
                    if L == 0 and t == T_W + 1:
                        pe.wait_ge(s_max, H * NB)
                        transpose_max(0, 0, 2)
                    if L == 0 and t == T_W + 3:
                        pe.wait_ge(memset_done, 2)
                        broadcast_max(0, 0, 2)
                    m, k = divmod(t, 16)
                    if 0 <= m < NB:
                        n = NB * L + m
                        i = H * n + k
                        half, j, c4, g, h = head_of(k)
                        if k == 0:
                            pe.wait_ge(m_in[n % 4], 16 * (n // 4 + 1))
                        if i >= 3:
                            pe.wait_ge(exp_done, i - 2)
                        for a in range(2):
                            ins = mm(ps[:, ps_st[i % 3], S * a:S * a + S], KP[:, n % 4, g, j, P * a:P * a + P],
                                     QS[:, n % 4, g, :], start=True, stop=True)
                        ins.then_inc(st_mm, 1)
                    m, u = divmod(t - T_AV, 16)
                    if u % 4 == 0 and 0 <= m < NB:
                        n, u = NB * L + m, u // 4
                        pe.wait_ge(exp_done, H * n + 4 * u + 4)
                        if u == 0:
                            pe.wait_ge(v_ev, n + 1)
                            if n:
                                pe.wait_ge(raw_ev, n)
                        for a in range(2):
                            for c4 in range(4):
                                half, j, _, g, h = head_of(4 * u + c4)
                                ins = mm(ps[32 * c4:32 * c4 + 32, AVB, S * half:S * half + S],
                                         VA[:, n % 4, a, 80 * g + 32 * j:80 * g + 32 * j + 32],
                                         Pt[:, u % 2, c4, S * a:S * a + S],
                                         start=(j == 0 and a == 0), stop=(j == 1 and a == 1), skip_group_check=True)
                        ins.then_inc(av_mm, 1)
                    m = due(T_O1, t)
                    if m is not None:
                        n = NB * L + m
                        bank_read(BANK_A, L, t)
                        pe.wait_ge(raw_ev, n + 1)
                        for i in range(4):
                            ins = pe.transpose(ps[:, BA, P * i:P * i + P], raw[:, P * i:P * i + P], ident[:, :])
                        ins.then_inc(o1_t, 1)
                    m = due(T_O2, t)
                    if m is not None:
                        n = NB * L + m
                        bank_read(BANK_B, L, t)
                        pe.wait_ge(on_done, n + 1)
                        for a in range(2):
                            ins = pe.transpose(ps[:, BB, P * a:P * a + P], on[:, a, :], ident[:, :])
                        ins.then_inc(o2_t, 1)
                    m = due(T_OUT, t)
                    if m is not None:
                        n = NB * L + m
                        bank_read(BANK_B, L, t)
                        pe.wait_ge(onT_ev, n + 1)
                        for a in range(2):
                            ins = mm(ps[:, BB, P * a:P * a + P], onT[:, P * a:P * a + P], w_at[L][:, 3, :],
                                     start=True, stop=True)
                        ins.then_inc(out_mm, 1)
                    m = due(T_XT, t)
                    if m is not None:
                        n = NB * L + m
                        bank_read(BANK_B, L, t)
                        pe.wait_ge(post_n, 2 * (n + 1))
                        for a in range(2):
                            ins = pe.transpose(ps[:, BB, P * a:P * a + P], post_rows(n, a), ident[:, :])
                        ins.then_inc(post_t, 1)
                    m = due(T_R, t)
                    if m is not None and L == 1:
                        bank_read(BANK_A, L, t)
                        pe.wait_ge(post_ev, NB + m + 1)
                        for a in range(2):
                            i = 2 * m + a
                            ins = mm(ps[:, BA, E * a:E * a + E], xT[:, P * i:P * i + P], gw[:, :], start=True, stop=True)
                        ins.then_inc(r_mm, 1)
                    m = due(T_RK, t)
                    if m is not None and L == 1:
                        bank_read(BANK_A, L, t)
                        if m == 0:
                            pe.wait_ge(in_tab, 32)
                        pe.wait_ge(r_sel, m + 1)
                        before, every = tri[:, 0, :], tri[:, 1, :]
                        o = ps[:, BA, 0:3 * E].rearrange("p (a e) -> p a e", a=3)
                        mm(o[:, 0, :], before, sel[:, m, 0, :], start=True, stop=True)
                        mm(o[:, 1, :], before, sel[:, m, 1, :], start=True, stop=False)
                        mm(o[:, 1, :], every, sel[:, m, 0, :], start=False, stop=True)
                        mm(o[:, 2, :], every, sel[:, m, 0, :], start=True, stop=False)
                        mm(o[:, 2, :], every, sel[:, m, 1, :], start=False, stop=True).then_inc(rk_mm, 1)
                    if L == 1 and (j := shared_at(T_SH, t)) is not None:
                        shared(*SHARED[j])
                if L == 0:
                    pe.wait_ge(in_second, 48)
                    pe.wait_ge(w_q, 1)
                    transpose_max(1, 2, 1)
                    broadcast_max(1, 2, 1)
                    for c in range(4):
                        for f in range(FT):
                            i = 4 * c + f
                            if f == 0:
                                pe.wait_ge(xq_b, c + 1)
                            if i >= 3:
                                pe.wait_ge(gelu, i - 2)
                            mm(ps[:, ps_st[i % 3], :], w1q[:, P * f:P * f + P], xq[:, 512 * c:512 * c + 512],
                               start=True, stop=True).then_inc(f1_mm, 1)
                    transpose_max(2, 3, 1)
                    broadcast_max(2, 3, 1)

            for c, f in SHARED[shared_left(T_SH):]:
                shared(c, f)
            pe.wait_ge(acc, 4)
            pe.wait_ge(r_exp, 1)
            expert = {}
            wd_flat = wd.rearrange("p e f d -> p (e f d)")
            whi_flat = whi[:, :, :].rearrange("p e f -> p (e f)")
            wlo_flat = wlo[:, :, :].rearrange("p e f -> p (e f)")

            def a_step(i):
                pe.wait_ge(row_in[i % RING], 16 * (i // RING + 1))
                if i >= 2:
                    pe.wait_ge(a_lo, i - 1)
                pe.transpose(ps[:, 6 + i % 2, 0:P], rows[:, i % RING, 2:ROW], ident[:, :]).then_inc(a_t, 1)

            def b_step(i):
                expert[i] = e = pe.value_load(exu[0:1, i:i + 1], min_val=0, max_val=E - 1)
                pe.wait_ge(a_hi, i + 1)
                if i >= 2:
                    pe.wait_ge(b_h, i - 1)
                g, u = ps[:, 2 * (i % 2), 0:FE], ps[:, 2 * (i % 2) + 1, 0:FE]
                off = e * (2 * FE)
                mm(g, xh[:, i % 2, :], whi_flat[:, bass.ds(off, FE)], start=True, stop=False)
                mm(g, xh[:, i % 2, :], wlo_flat[:, bass.ds(off, FE)], start=False, stop=False)
                mm(u, xh[:, i % 2, :], whi_flat[:, bass.ds(off + FE, FE)], start=True, stop=False)
                mm(u, xh[:, i % 2, :], wlo_flat[:, bass.ds(off + FE, FE)], start=False, stop=False)
                pe.wait_ge(a_lo, i + 1)
                mm(g, xl[:, i % 2, :], whi_flat[:, bass.ds(off, FE)], start=False, stop=True)
                mm(u, xl[:, i % 2, :], whi_flat[:, bass.ds(off + FE, FE)], start=False, stop=True).then_inc(b_mm, 1)

            def c_step(i):
                pe.wait_ge(b_h, i + 1)
                if i >= 1:
                    pe.wait_ge(c_ev, i)
                for f, (f0, fn) in enumerate(FTE):
                    ins = pe.transpose(ps[0:fn, 4, P * f:P * f + P], ht[:, i % 2, f0:f0 + fn], ident[:, :])
                ins.then_inc(c_t, 1)

            def d_step(i):
                pe.wait_ge(c_ev, i + 1)
                if i >= 1:
                    pe.wait_ge(d2_ev, i)
                off = expert[i] * (3 * D)
                for f, (f0, fn) in enumerate(FTE):
                    ins = mm(ps[:, 5, 0:D], hT[0:fn, i % 2, f, :], wd_flat[0:fn, bass.ds(off + f * D, D)],
                             start=(f == 0), stop=(f == 2))
                ins.then_inc(d2_mm, 1)

            a_step(0)
            for i in range(SLOTS + 2):
                if i + 1 < SLOTS:
                    a_step(i + 1)
                if i < SLOTS:
                    b_step(i)
                if 1 <= i <= SLOTS:
                    c_step(i - 1)
                if i >= 2:
                    d_step(i - 2)

        @block.scalar
        def _(act):
            A = nc.scalar.activation

            def load_table(func):
                act.wait_ge(memset_done, 2)
                A(scratch[:, :], ones[:, 0:1], func)

            def split_expert(e):
                act.wait_ge(in_e[e % 2], 16 * (e // 2 + 1))
                A(whi[:, e, :], wst[:, e % 2, :], ACT.Identity).then_inc(e_hi, 1)

            def shared(c, f):
                if f is not None:
                    i, fn = 3 * c + f, FTE[f][1]
                    act.wait_ge(g_mm, i + 1)
                    if i == 0:
                        act.wait_ge(av_mm, 2 * NB * 4)
                    if i >= 2:
                        act.wait_ge(h_done, i - 1)
                    A(sg[0:fn, i % 2, :], ps[0:fn, i % 2, :], ACT.Silu).then_inc(silu, 1)

            load_table(ACT.Exp)
            act.wait_ge(in_first, 16)
            for L in range(2):
                for t in range(T_FIRST, T_LAST + 1):
                    if L == 1 and 0 <= t - A_F2 < len(SECOND):
                        c, quantise = SECOND[t - A_F2]
                        if quantise:
                            if c == 0:
                                load_table(ACT.Exp)
                                act.wait_ge(gm_s, 3)
                            for f in range(FT):
                                A(hb[:, f, 512 * c:512 * c + 512], hb[:, f, 512 * c:512 * c + 512], ACT.Copy,
                                  scale=sc[:, 6:7], bias=ROUND).then_inc(hq_a, 1)
                    n = due_kv(A_K, L, t, F_A_K)
                    if n is not None:
                        act.wait_ge(k_mm, n + 1)
                        if n >= 2:
                            act.wait_ge(k_lo, n - 1)
                        if n < NB:
                            A(kf[:, n % 2, :], ps[:, BA, 0:S], ACT.Identity, bias=b_at[n // NB][:, 1:2])
                            A(rot[:, n % 2, :], ps[:, BA, S:2 * S], ACT.Identity, bias=b_sw[:, 1:2]).then_inc(k_ev, 1)
                        else:
                            A(kf[:, n % 2, :], ps[:, BA, 0:S], ACT.Identity, bias=b_at[n // NB][:, 1:2]).then_inc(k_ev, 1)
                    m = due(A_X, t, F_A_X)
                    if m is not None:
                        n = NB * L + m
                        act.wait_ge(xt_mm, n + 1)
                        if n >= 2:
                            act.wait_ge(q_mm, n - 1)
                        A(pre_T[:, n % 2, :], ps[:, BB, 0:S], ACT.Copy).then_inc(xt_ev, 1)
                    m = due(A_Q, t, F_A_Q)
                    if m is not None:
                        n = NB * L + m
                        act.wait_ge(q_mm, n + 1)
                        if n >= 2:
                            act.wait_ge(q_lo, n - 1)
                        if L == 0:
                            A(qf[:, n % 2, :], ps[:, BA, 0:S], ACT.Identity, bias=b_at[L][:, 0:1])
                            A(rotq[:, n % 2, :], ps[:, BA, S:2 * S], ACT.Identity, bias=b_sw[:, 0:1]).then_inc(q_ev, 1)
                        else:
                            A(qf[:, n % 2, :], ps[:, BA, 0:S], ACT.Identity, bias=b_at[L][:, 0:1]).then_inc(q_ev, 1)
                    n = due_kv(A_KHI, L, t, F_A_KHI)
                    if n is not None:
                        if n < NB:
                            act.wait_ge(k_rot, 3 * n + 3)
                        else:
                            act.wait_ge(k_ev, n + 1)
                        if n >= 2:
                            act.wait_ge(kp_in[(n - 2) % 4], 128 * ((n - 2) // 4 + 1))
                        A(khi[:, n % 2, :], kf[:, n % 2, :], ACT.Copy).then_inc(k_hi, 1)
                    m = due(A_QHI, t, F_A_QHI)
                    if m is not None:
                        n = NB * L + m
                        if L == 0:
                            act.wait_ge(q_rot, 3 * n + 3)
                        else:
                            act.wait_ge(q_ev, n + 1)
                        if n >= 2:
                            act.wait_ge(qs_in[(n - 2) % 4], 64 * ((n - 2) // 4 + 1))
                        A(qhi[:, n % 2, :], qf[:, n % 2, :], ACT.Copy).then_inc(q_hi, 1)
                    m = due(A_MX, t, F_A_MX)
                    if m is not None:
                        n = NB * L + m
                        act.wait_ge(mx_t, n + 1)
                        if n >= 2:
                            act.wait_ge(m_in[(n - 2) % 4], 16 * ((n - 2) // 4 + 1))
                        A(negm[:, n % 2, :], ps[0:H, BB, 0:S], ACT.Copy, scale=-1.0 / MAXROW).then_inc(negm_ev, 1)
                    m, k = divmod(t, 16)
                    if 0 <= m < NB:
                        n = NB * L + m
                        i = H * n + k
                        act.wait_ge(st_mm, i + 1)
                        if i == H * NB:
                            act.wait_ge(f2_mm, 4)
                            act.wait_ge(ffn_out, 4)
                        if k % 4 == 0 and i >= 8:
                            act.wait_ge(av_mm, i // 4 - 1)
                        A(Pt[:, (i // 4) % 2, i % 4, :], ps[:, ps_st[i % 3], :], ACT.Exp, scale=SM_SCALE)\
                            .then_inc(exp_done, 1)
                    m = due(A_RAW, t)
                    if m is not None:
                        n = NB * L + m
                        act.wait_ge(av_mm, 4 * (n + 1))
                        if n:
                            act.wait_ge(o1_t, n)
                        A(raw[:, :], ps[:, AVB, :], ACT.Copy).then_inc(raw_ev, 1)
                    m = due(A_O2, t)
                    if m is not None:
                        n = NB * L + m
                        act.wait_ge(o2_t, n + 1)
                        if n:
                            act.wait_ge(out_mm, n)
                        A(onT[:, :], ps[:, BB, 0:S], ACT.Copy).then_inc(onT_ev, 1)
                        if n < NE:
                            split_expert(n)
                    m = due(A_XT, t)
                    if m is not None:
                        n = NB * L + m
                        act.wait_ge(post_t, n + 1)
                        if n == NB:
                            act.wait_ge(xq_a, 4)
                        A(xT[:, S * m:S * m + S], ps[:, BB, 0:S], ACT.Copy).then_inc(post_ev, 1)
                    m = due(A_XHI, t)
                    if m is not None and L == 1:
                        act.wait_ge(post_ev, NB + m + 1)
                        if m == 0:
                            act.wait_ge(f1_mm, 16)
                        A(xhi[:, S * m:S * m + S], xT[:, S * m:S * m + S], ACT.Copy).then_inc(x2hi, 1)
                    m = due(A_R, t)
                    if m is not None and L == 1:
                        act.wait_ge(r_sub, m + 1)
                        A(ex[:, m, :, :], ex[:, m, :, :], ACT.Exp).then_inc(r_ex, 1)
                    if L == 1 and (j := shared_at(A_SH, t)) is not None:
                        shared(*SHARED[j])
                if L == 0:
                    load_table(ACT.Gelu)
                    act.wait_ge(in_second, 48)
                    act.wait_ge(f_sc, 1)
                    for i in range(16):
                        c, f = divmod(i, 4)
                        act.wait_ge(f1_mm, i + 1)
                        A(hb[:, f, 512 * c:512 * c + 512], ps[:, ps_st[i % 3], :], ACT.Gelu,
                          bias=b1s[:, f:f + 1], scale=sc[:, 3:4]).then_inc(gelu, 1)

            for c, f in SHARED[shared_left(A_SH):]:
                shared(c, f)
            act.wait_ge(h_done, 12)

            def hi(i):
                act.wait_ge(a_t, i + 1)
                if i >= 2:
                    act.wait_ge(b_mm, i - 1)
                A(xh[:, i % 2, :], ps[:, 6 + i % 2, 0:P], ACT.Copy).then_inc(a_hi, 1)

            hi(0)
            for i in range(SLOTS + 2):
                if i + 1 < SLOTS:
                    hi(i + 1)
                if i < SLOTS:
                    act.wait_ge(b_mm, i + 1)
                    A(sg[:, i % 2, 0:FE], ps[:, 2 * (i % 2), 0:FE], ACT.Silu).then_inc(b_silu, 1)
                if 1 <= i <= SLOTS:
                    act.wait_ge(c_t, i)
                    if i >= 3:
                        act.wait_ge(d2_mm, i - 2)
                    A(hT[:, (i - 1) % 2, 0:2, :], ps[:, 4, 0:2 * P].rearrange("p (f t) -> p f t", f=2), ACT.Copy)
                    A(hT[0:96, (i - 1) % 2, 2, :], ps[0:96, 4, 2 * P:3 * P], ACT.Copy).then_inc(c_ev, 1)

        @block.vector
        def _(dve):
            V = nc.vector

            def norm_stats(n, src, st, mv_, s_st, s_mv, s_n):
                if n >= 2:
                    dve.wait_ge(s_n, 2 * (n - 1))
                for a in range(2):
                    V.bn_stats(st[:, n % 2, a, :], src(a)).then_inc(s_st, 1)
                for a in range(2):
                    dve.wait_ge(s_st, 2 * n + a + 1)
                    V.bn_aggr(mv_[:, n % 2, a, :], st[:, n % 2, a, :]).then_inc(s_mv, 1)

            def norm_rows(n, src, dst, mv_, r, s_rs, s_n):
                dve.wait_ge(s_rs, n + 1)
                for a in range(2):
                    V.tensor_scalar(dst(n, a), src(a), mv_[:, n % 2, a, 0:1], r[:, n % 2, a:a + 1],
                                    ALU.subtract, ALU.mult).then_inc(s_n, 1)

            def reduce_max(r, c0, n):
                dve.wait_ge(gm_t, r + 1)
                V.tensor_reduce(g1[0:1, 4 + c0:4 + c0 + n], ps[0:1, MB, 0:P * n].rearrange("p (n t) -> p n t", n=n),
                                AX.X, ALU.max).then_inc(gm_b, 1)

            def guard_max(r, c0, n):
                dve.wait_ge(gm_bc, r + 1)
                V.tensor_scalar(sc[:, 8 + c0:8 + c0 + n], ps[:, MB, 2 * P:2 * P + n], MIN_RANGE, None, ALU.max).then_inc(gm_s, 1)
                dve.wait_ge(gm_s, r + 1)

            chain = [0]

            def step(ins):
                chain[0] += 1
                ins.then_inc(v_step, 1)
                dve.wait_ge(v_step, chain[0])

            def shared(c, f):
                if f is not None:
                    i, fn = 3 * c + f, FTE[f][1]
                    dve.wait_ge(silu, i + 1)
                    dve.wait_ge(u_mm, i + 1)
                    if i == 0:
                        dve.wait_ge(av_mm, 2 * NB * 4)
                    if f == 0 and c >= 2:
                        dve.wait_ge(d_mm, c - 1)
                    V.tensor_tensor(hh[0:fn, c % 2, f, :], sg[0:fn, i % 2, :], ps[0:fn, 2 + i % 2, :], ALU.mult).then_inc(h_done, 1)
                else:
                    dve.wait_ge(d_mm, c + 1)
                    if c == 3:
                        dve.wait_ge(post_n, 4 * NB)
                    V.tensor_tensor(x[:, 4 * c:4 * c + 4, :], ps[:, 4 + c % 2, :].rearrange("p (a d) -> p a d", a=4),
                                    x[:, 4 * c:4 * c + 4, :], ALU.add).then_inc(acc, 1)

            def second(c, quantise):
                if quantise:
                    for f in range(FT):
                        dve.wait_ge(hq_a, FT * c + f + 1)
                        if f == 0 and c >= 2:
                            dve.wait_ge(f2_mm, c - 1)
                        V.tensor_scalar(hq[:, f, c % 2, :], hb[:, f, 512 * c:512 * c + 512], ROUND, None,
                                        ALU.subtract).then_inc(hq_b, 1)
                else:
                    dve.wait_ge(f2_mm, c + 1)
                    dve.wait_ge(x_b2, c + 1)
                    xs = x[:, 4 * c:4 * c + 4, :]
                    V.scalar_tensor_tensor(out=xs, in0=ps[:, ps_s[c % 2], :].rearrange("p (a d) -> p a d", a=4),
                                           scalar=sc[:, 7:8], in1=xs, op0=ALU.mult, op1=ALU.add).then_inc(ffn_out, 1)

            V.memset(KP[:, 0, :, :, :].rearrange("p g j t -> p (g j t)").bitcast(U32), 0).then_inc(zero_done, 1)
            V.memset(QS[:, :, :, :].rearrange("p b g t -> p (b g t)").bitcast(U32), 0).then_inc(zero_done, 1)
            V.memset(KP[:, 1, :, :, :].rearrange("p g j t -> p (g j t)").bitcast(U32), 0).then_inc(zero_done, 1)
            dve.wait_ge(in_first, 16)

            for L in range(2):
                for t in range(T_FIRST, T_LAST + 1):
                    if L == 1 and 0 <= t - D_F2 < len(SECOND):
                        second(*SECOND[t - D_F2])
                    if L == 0 and t == T_W:
                        dve.wait_ge(in_w12, 16)
                        V.tensor_reduce(g1[:, 0:2], w12.rearrange("p (i f) -> p i f", i=2), AX.X, ALU.max,
                                        apply_absolute_value=True).then_inc(gm_a, 1)
                    if L == 0 and t == T_W + 2:
                        reduce_max(0, 0, 2)
                    if L == 0 and t == T_W + 4:
                        guard_max(0, 0, 2)
                        step(V.reciprocal(sc[:, 12:14], sc[:, 8:10]))
                        step(V.tensor_scalar(sc[:, 12:14], sc[:, 12:14], QP, None, ALU.mult))
                        for i in range(2):
                            ins = V.tensor_scalar(w12[:, FF * i:FF * i + FF], w12[:, FF * i:FF * i + FF],
                                                  sc[:, 12 + i:13 + i], ROUND, ALU.mult, ALU.add)
                        step(ins)
                        V.tensor_scalar(w1q[:, :], w12[:, 0:FF], ROUND, None, ALU.subtract)
                        V.tensor_scalar(w2q[:, :, :].rearrange("p f d -> p (f d)"), w12[:, FF:2 * FF], ROUND, None,
                                        ALU.subtract).then_inc(w_q, 1)
                    m = due(D_STAT, t, F_D_STAT)
                    if m is not None:
                        n = NB * L + m
                        if n in (0, 2):
                            dve.wait_ge(in_x[n // 2], 16)
                        if L == 1:
                            dve.wait_ge(ffn_out, m // 2 + 1)
                        def src(a, m=m):
                            return x[:, 2 * m + a, :]
                        norm_stats(n, src, st6, mv, pre_st, pre_mv, pre_n)
                    n = due_kv(D_V, L, t, F_D_V)
                    if n is not None:
                        dve.wait_ge(v_mm, n + 1)
                        if n == 0:
                            dve.wait_ge(memset_done, 6)
                            dve.wait_ge(in_bv, 16)
                        if n >= 4:
                            dve.wait_ge(av_mm, 4 * (n - 3))
                        for a in range(2):
                            ins = V.tensor_tensor(
                                VA[:, n % 4, a, :].rearrange("p (g j w) -> p g j w", g=G, j=2)[:, :, :, 0:HD],
                                ps[:, BB, P * a:P * a + P].rearrange("p (g j d) -> p g j d", g=G, j=2),
                                bv[:, n // NB, :].rearrange("p (g j d) -> p g j d", g=G, j=2), ALU.add)
                        ins.then_inc(v_ev, 1)
                    m = due(D_NORM, t, F_D_NORM)
                    if m is not None:
                        n = NB * L + m
                        if n >= 2:
                            dve.wait_ge(xt_mm, n - 1)
                        def src(a, m=m):
                            return x[:, 2 * m + a, :]
                        norm_rows(n, src, lambda n, a: xn[:, n % 2, a, :], mv, rs, pre_rs, pre_n)
                    m, k = divmod(t - T_S, 16)
                    if 0 <= m < NB:
                        n = NB * L + m
                        i = H * n + k
                        g, a = k // 2, k % 2
                        dve.wait_ge(s_mm, i + 1)
                        if k == 0 and n >= 2:
                            dve.wait_ge(mx_t, n - 1)
                        V.tensor_reduce(mx[:, n % 2, a, g:H:G], ps[:, ps_s[i % 2], :].rearrange("p (j k) -> p j k", j=2),
                                        AX.X, ALU.max).then_inc(s_max, 1)
                    m = due(D_O1, t)
                    if m is not None:
                        n = NB * L + m
                        dve.wait_ge(o1_t, n + 1)
                        o = ps[:, BA, :].rearrange("p (u w) -> p u w", w=32)
                        V.reciprocal(rsum[:, :].rearrange("p (u j) -> p u j", j=2), o[:, :, 16:18]).then_inc(rsum_done, 1)
                        dve.wait_ge(rsum_done, n + 1)
                        if n:
                            dve.wait_ge(o2_t, n)
                        for half in range(2):
                            for a in range(2):
                                q0 = 2 * half + a
                                ins = V.tensor_tensor(
                                    on[:, a, 64 * half:64 * half + 64].rearrange("p (c j d) -> p c j d", c=4, j=2),
                                    ps[:, BA, P * q0:P * q0 + P].rearrange("p (c w) -> p c w", c=4)[:, :, 0:16]
                                        .rearrange("p c (j d) -> p c j d", j=2),
                                    rsum[:, 8 * q0:8 * q0 + 8].rearrange("p (c j) -> p c j", j=2).unsqueeze(3)
                                        .to_broadcast([P, 4, 2, HD]), ALU.mult)
                        ins.then_inc(on_done, 1)
                    m = due(D_OUT, t)
                    if m is not None:
                        n = NB * L + m
                        dve.wait_ge(out_mm, n + 1)
                        dve.wait_ge(xb_done, n + 1)
                        V.tensor_tensor(x[:, 2 * m:2 * m + 2, :], ps[:, BB, 0:S].rearrange("p (a d) -> p a d", a=2),
                                        xb[:, n % 2, :, :], ALU.add).then_inc(x_new, 1)
                        dve.wait_ge(x_new, n + 1)
                        def src(a, m=m):
                            return x[:, 2 * m + a, :]
                        norm_stats(n, src, st6p, mvp, post_st, post_mv, post_n)
                    m = due(D_POST, t)
                    if m is not None:
                        n = NB * L + m
                        if n >= 2:
                            dve.wait_ge(post_t, n - 1)
                            if n <= NB + 1:
                                dve.wait_ge(amax_done, min(n - 1, NB))
                        if n == NB:
                            dve.wait_ge(f2_mm, 4)
                        def src(a, m=m):
                            return x[:, 2 * m + a, :]
                        norm_rows(n, src, post_rows, mvp, rsp, post_rs, post_n)
                        if L == 0:
                            dve.wait_ge(post_n, 2 * (n + 1))
                            V.tensor_reduce(amax[:, m:m + 1], xp[:, n % 2, :, :].rearrange("p a d -> p (a d)"), AX.X, ALU.max,
                                            apply_absolute_value=True).then_inc(amax_done, 1)
                    if L == 1:
                        m = due(D_R0, t)
                        if m is not None:
                            dve.wait_ge(r_mm, m + 1)
                            if m == 0:
                                dve.wait_ge(in_tab, 32)
                            V.tensor_copy(lg[:, m, :, 0:E], ps[:, BA, 0:2 * E].rearrange("p (t e) -> p t e", e=E)).then_inc(r_ev, 1)
                        m = due(D_R1, t)
                        if m is not None:
                            dve.wait_ge(r_ev, m + 1)
                            for a in range(2):
                                V.max(lg[:, m, a, E:2 * E], lg[:, m, a, 0:E]).then_inc(r_top, 1)
                        m = due(D_R2, t)
                        if m is not None:
                            dve.wait_ge(r_top, 2 * m + 2)
                            V.tensor_tensor(eq[:, m, :, :].rearrange("p (k t) e -> p k t e", k=2),
                                            lg[:, m, :, 0:E].unsqueeze(1).to_broadcast([P, 2, 2, E]),
                                            lg[:, m, :, E:E + 2].rearrange("p t k -> p k t").unsqueeze(3)
                                            .to_broadcast([P, 2, 2, E]), ALU.is_equal).then_inc(r_eq, 1)
                            V.tensor_tensor(ex[:, m, :, :], lg[:, m, :, :],
                                            lg[:, m, :, E:E + 1].to_broadcast([P, 2, 2 * E]), ALU.subtract).then_inc(r_sub, 1)
                        m = due(D_KEY, t)
                        if m is not None:
                            dve.wait_ge(r_eq, m + 1)
                            V.tensor_tensor(key[:, m, :, :], eq[:, m, :, :], desc.unsqueeze(1).to_broadcast([P, 4, E]),
                                            ALU.mult).then_inc(r_key, 1)
                        m = due(D_KMAX, t)
                        if m is not None:
                            dve.wait_ge(r_key, m + 1)
                            V.tensor_reduce(kmax[:, m, 0:2], key[:, m, 0:2, :], AX.X, ALU.max).then_inc(r_kmax, 1)
                        m = due(D_OH, t)
                        if m is not None:
                            dve.wait_ge(r_kmax, 2 * m + 1)
                            V.tensor_tensor(oh[:, m, 0:2, :], key[:, m, 0:2, :],
                                            kmax[:, m, 0:2].unsqueeze(2).to_broadcast([P, 2, E]), ALU.is_equal).then_inc(r_oh, 1)
                        m = due(D_KEY2, t)
                        if m is not None:
                            dve.wait_ge(r_oh, 2 * m + 1)
                            V.scalar_tensor_tensor(out=key[:, m, 2:4, :], in0=oh[:, m, 0:2, :], scalar=-2.0 * E,
                                                   in1=key[:, m, 2:4, :], op0=ALU.mult, op1=ALU.add).then_inc(r_key2, 1)
                        m = due(D_KMAX2, t)
                        if m is not None:
                            dve.wait_ge(r_key2, m + 1)
                            V.tensor_reduce(kmax[:, m, 2:4], key[:, m, 2:4, :], AX.X, ALU.max).then_inc(r_kmax, 1)
                        m = due(D_R3, t)
                        if m is not None:
                            dve.wait_ge(r_kmax, 2 * m + 2)
                            V.tensor_tensor(oh[:, m, 2:4, :], key[:, m, 2:4, :],
                                            kmax[:, m, 2:4].unsqueeze(2).to_broadcast([P, 2, E]), ALU.is_equal).then_inc(r_oh, 1)
                            dve.wait_ge(r_ex, m + 1)
                            V.tensor_reduce(zs[:, m, :], ex[:, m, :, 0:E], AX.X, ALU.add).then_inc(r_zs, 1)
                        m = due(D_RK, t)
                        if m is not None:
                            dve.wait_ge(rk_mm, m + 1)
                            V.tensor_copy(rk[:, m, :, :], ps[:, BA, 0:3 * E].rearrange("p (a e) -> p a e", a=3)).then_inc(rk_ev, 1)
                        m = due(D_R4, t)
                        if m is not None:
                            dve.wait_ge(r_pick, m + 1)
                            V.tensor_reduce(rowf[:, m, :], pick[:, m, :, :], AX.X, ALU.add)
                            V.reciprocal(rcp[:, m, :], den[:, m, :]).then_inc(r_row, 1)
                    if L == 1 and (j := shared_at(D_SH, t)) is not None:
                        shared(*SHARED[j])
                if L == 0:
                    dve.wait_ge(amax_done, NB)
                    V.tensor_reduce(g1[:, 2:3], amax[:, 0:NB], AX.X, ALU.max).then_inc(gm_a, 1)
                    reduce_max(1, 2, 1)
                    guard_max(1, 2, 1)
                    step(V.reciprocal(sc[:, 2:3], sc[:, 10:11]))
                    step(V.tensor_scalar(sc[:, 2:3], sc[:, 2:3], QP, None, ALU.mult))
                    for c in range(4):
                        if c == 0:
                            dve.wait_ge(post_ev, NB)
                        V.tensor_scalar(xT[:, 512 * c:512 * c + 512], xT[:, 512 * c:512 * c + 512], sc[:, 2:3], ROUND,
                                        ALU.mult, ALU.add).then_inc(xq_a, 1)
                        dve.wait_ge(xq_a, c + 1)
                        V.tensor_scalar(xq[:, 512 * c:512 * c + 512], xT[:, 512 * c:512 * c + 512], ROUND, None,
                                        ALU.subtract).then_inc(xq_b, 1)
                        if c == 0:
                            step(V.tensor_scalar(sc[:, 0:1], sc[:, 8:9], 1.0 / QP, None, ALU.mult))
                            step(V.tensor_scalar(sc[:, 1:2], sc[:, 10:11], 1.0 / QP, sc[:, 0:1], ALU.mult, ALU.mult))
                            step(V.tensor_copy(sc[:, 3:4], sc[:, 1:2]))
                            dve.wait_ge(in_second, 48)
                            V.tensor_scalar(b1s[:, :], b1[:, :], sc[:, 3:4], None, ALU.mult).then_inc(f_sc, 1)
                    for i in range(16):
                        c, f = divmod(i, 4)
                        dve.wait_ge(gelu, i + 1)
                        V.tensor_reduce(amax[:, i:i + 1], hb[:, f, 512 * c:512 * c + 512], AX.X, ALU.max,
                                        apply_absolute_value=True).then_inc(habs, 1)
                    dve.wait_ge(habs, 16)
                    V.tensor_reduce(g1[:, 3:4], amax[:, 0:16], AX.X, ALU.max).then_inc(gm_a, 1)
                    reduce_max(2, 3, 1)
                    dve.wait_ge(gm_bc, 3)
                    step(V.tensor_scalar(sc[:, 11:12], ps[:, MB, 2 * P:2 * P + 1], MIN_RANGE, None, ALU.max))
                    step(V.reciprocal(sc[:, 5:6], sc[:, 11:12]))
                    V.tensor_scalar(sc[:, 6:7], sc[:, 5:6], QP, None, ALU.mult).then_inc(gm_s, 1)
                    step(V.tensor_scalar(sc[:, 4:5], sc[:, 9:10], 1.0 / QP, None, ALU.mult))
                    V.tensor_scalar(sc[:, 7:8], sc[:, 11:12], 1.0 / QP, sc[:, 4:5], ALU.mult, ALU.mult).then_inc(f_sc, 1)
                    dve.wait_ge(f_sc, 2)

            def tile_table():
                dve.wait_ge(r_carry, NB)
                step(V.tensor_tensor(nt_, carry[:, NB, :], base, ALU.subtract))
                step(V.tensor_scalar(nt_, nt_, 1.0 / P, (P - 1.0) / P - 0.5 + 0.5 / P, ALU.mult, ALU.add))
                step(V.tensor_scalar(nt_, nt_, ROUND, None, ALU.add))
                step(V.tensor_scalar(nt_, nt_, ROUND, None, ALU.subtract))
                V.tensor_scalar(step_row, nt_, -float(P), float(CAP), ALU.mult, ALU.add)
                src_, dst_ = nt_, ends_a
                for sh, spare in ((1, ends_b), (2, ends_c), (4, None)):
                    V.tensor_copy(dst_[:, 0:sh], src_[:, 0:sh])
                    step(V.tensor_tensor(dst_[:, sh:E], src_[:, sh:E], src_[:, 0:E - sh], ALU.add))
                    src_, dst_ = dst_, spare
                step(V.tensor_tensor(cmp_, tile_no, src_.unsqueeze(1).to_broadcast([P, SLOTS, E]), ALU.is_ge))
                step(V.tensor_reduce(exf, cmp_, AX.X, ALU.add))
                V.tensor_scalar(exu, exf, E - 1.0, None, ALU.min)
                step(V.tensor_tensor(cmr, cmp_, step_row.unsqueeze(1).to_broadcast([P, SLOTS, E]), ALU.mult))
                step(V.tensor_reduce(stf, cmr, AX.X, ALU.add))
                V.scalar_tensor_tensor(out=stu, in0=tile_no[:, :, 0], scalar=float(P), in1=stf, op0=ALU.mult,
                                       op1=ALU.add).then_inc(r_exp, 1)

            tile_table()
            for c, f in SHARED[shared_left(D_SH):]:
                shared(c, f)

            def lo(i):
                dve.wait_ge(a_hi, i + 1)
                if i >= 2:
                    dve.wait_ge(b_mm, i - 1)
                V.tensor_tensor(xl[:, i % 2, :], ps[:, 6 + i % 2, 0:P], xh[:, i % 2, :], ALU.subtract).then_inc(a_lo, 1)
                if i >= RING:
                    dve.wait_ge(back[i % RING], 16 * (i // RING))
                V.tensor_copy(dst_u[:, i % RING:i % RING + 1], rows[:, i % RING, 0:1]).then_inc(d2_idx, 1)

            lo(0)
            for i in range(SLOTS + 2):
                if i + 1 < SLOTS:
                    lo(i + 1)
                if i < SLOTS:
                    dve.wait_ge(b_silu, i + 1)
                    if i >= 2:
                        dve.wait_ge(c_t, i - 1)
                    V.tensor_tensor(ht[:, i % 2, :], sg[:, i % 2, 0:FE], ps[:, 2 * (i % 2) + 1, 0:FE], ALU.mult).then_inc(b_h, 1)
                if i >= 2:
                    p = i - 2
                    dve.wait_ge(d2_mm, p + 1)
                    if p >= RING:
                        dve.wait_ge(back[p % RING], 16 * (p // RING))
                    V.tensor_scalar(yb[:, p % RING, :], ps[:, 5, 0:D], rows[:, p % RING, 1:2], None, ALU.mult).then_inc(d2_ev, 1)
            for c in range(1, 4):
                dve.wait_ge(y_in[c], 16)
                for k in range(2):
                    if k:
                        dve.wait_ge(y_sum, 2 * c - 1)
                    V.tensor_tensor(x[:, 4 * c:4 * c + 4, :], x[:, 4 * c:4 * c + 4, :], ytok[:, 4 * c:4 * c + 4, k, :],
                                    ALU.add).then_inc(y_sum, 1)


def kernel(**inputs):
    import concourse.bacc as _bacc
    from concourse import mybir as _mybir
    from concourse.bass_utils import run_bass_kernel_spmd as _run

    a = {k: np.asarray(v) for k, v in inputs.items()}
    f32 = np.float32

    order = np.array([(2 * g + j) * HD + d for j in range(2) for d in range(HD) for g in range(G)])
    swapped = np.array([(2 * g + j) * HD + (d + HD // 2) % HD for j in range(2) for d in range(HD) for g in range(G)])
    w0 = {k: a[f"L0_xattn_W{k}"].T for k in "qkvo"}
    w1 = {k: a[f"L1_xattn_w{k}"] for k in "qkvo"}
    w_at = np.stack([np.stack([w["q"][:, order], w["k"][:, order], w["v"], w["o"]], 1) for w in (w0, w1)], 1)
    w_sw = np.stack([w0["q"][:, swapped], w0["k"][:, swapped]], 1)
    b = [{k: a[f"L{n}_xattn_b{k}"] for k in "qkvo"} for n in range(2)]
    b_at = np.stack([np.stack([c["q"][order], c["k"][order]], 1) for c in b], 1)
    b_sw = np.stack([b[0]["q"][swapped], b[0]["k"][swapped]], 1)

    inv = (1.0 / 10000.0 ** (np.arange(0, HD, 2, dtype=f32) / f32(HD))).astype(f32)
    ang = np.outer(np.arange(S, dtype=f32), inv).astype(f32)
    dd = np.array([d for _ in range(2) for d in range(HD) for _ in range(G)])
    cos = np.cos(ang)[:, dd % (HD // 2)].T.astype(f32)
    sin = (np.sin(ang)[:, dd % (HD // 2)].T * np.where(dd < HD // 2, -1, 1)[:, None]).astype(f32)
    kp = np.zeros((2, G, 2, S), np.float16)
    kp[0, :, 0] = MAXROW
    kp[1, :, 1] = MAXROW

    gate = np.concatenate([a["L1_ffn_expert_gate"], a["L1_ffn_shared_gate"][None]])
    up = np.concatenate([a["L1_ffn_expert_up"], a["L1_ffn_shared_up"][None]])
    down = np.concatenate([a["L1_ffn_expert_down"], a["L1_ffn_shared_down"][None]])
    wgu = np.concatenate([gate, up], 1).transpose(0, 2, 1)
    wd = np.zeros((P, NE, 3, D), f32)
    for f, (f0, fn) in enumerate(FTE):
        wd[:fn, :, f] = down[:, :, f0:f0 + fn].transpose(2, 0, 1)
    tail = np.zeros((P, E, ROW), f32)
    tail[:, :, 0] = 2 * NT + SLOTS * P + P * np.arange(E)[None, :] + np.arange(P)[:, None]
    arrays = {
        "x": a["x"],
        "ctxT": a["ctx_1024"].transpose(0, 2, 1),
        "first": np.concatenate([w_at[:, 0].reshape(D, 4 * D), w_sw.reshape(D, 2 * D), cos, sin, np.eye(P, dtype=f32),
                                 b_at[:, 0], b_sw], 1),
        "second": np.concatenate([w_at[:, 1].reshape(D, 4 * D), b_at[:, 1], a["L1_ffn_gate_w"].T,
                                  a["L0_ffn_b1"].reshape(FT, P).T], 1),
        "bv": np.stack([c["v"] for c in b]), "bo": np.stack([c["o"] for c in b]),
        "w12": np.concatenate([a["L0_ffn_w1"].T, a["L0_ffn_w2"].T.reshape(FT, P, D).transpose(1, 0, 2).reshape(P, FF)], 1),
        "b2": a["L0_ffn_b2"],
        "wgu": wgu, "wd": wd,
        "c_kp": kp,
        "c_tri": np.stack([np.triu(np.ones((P, P)), 1), np.ones((P, P))], 1).astype(np.float16),
        "c_tab": np.concatenate([
            np.tile(E - np.arange(E, dtype=f32), (P, 1)),
            (2 * (P * np.arange(TILES)[None, None, :] + np.arange(P)[:, None, None])
             + np.arange(2)[None, :, None]).astype(f32).reshape(P, -1),
            np.arange(P, dtype=f32)[:, None],
            np.tile(CAP * np.arange(E, dtype=f32), (P, 1)),
            np.tile(np.repeat(np.arange(SLOTS, dtype=f32), E), (P, 1)),
            tail.reshape(P, -1)], 1),
        "c_fill": np.concatenate([2 * NT + np.arange(SLOTS * P, dtype=f32)[:, None],
                                  np.zeros((SLOTS * P, ROW - 1), f32)], 1),
    }
    nc = _bacc.Bacc("TRN2", target_bir_lowering=False, num_devices=1)
    feeds, io = {}, {}
    for name, v in arrays.items():
        v = np.ascontiguousarray(v)
        feeds[f"in_{name}"] = v
        io[name] = nc.dram_tensor(f"in_{name}", v.shape, _mybir.dt.from_np(v.dtype), kind="ExternalInput").ap()
    out = nc.dram_tensor("out_0", (NB, S, D), F32, kind="ExternalOutput").ap()
    layers(nc, io, out)
    r = _run(nc, [feeds], core_ids=[0])
    return r.results[0]["out_0"]
```
